# Optimizing a Trainium2 kernel written in Bass

```python
import numpy as np
import jax
import jax.numpy as jnp

def _softmax(x, axis=-1):
    return jax.nn.softmax(x, axis=axis)

def _gelu(x):
    return jax.nn.gelu(x, approximate=True)

def _silu(x):
    return jax.nn.silu(x)

def _sigmoid(x):
    return jax.nn.sigmoid(x)

def _layernorm(x, axis=-1, eps=1e-05):
    m = jnp.mean(x, axis=axis, keepdims=True)
    v = jnp.var(x, axis=axis, keepdims=True)
    return (x - m) / jnp.sqrt(v + eps)

def _scatter_add(tgt, idx, src, axis=0):
    return tgt.at[idx].add(src)

def _segment_sum(src, seg, n):
    return jax.ops.segment_sum(src, seg, n)
kernel_name = 'mk_decoder_postln_d1_seqx_r8_b4dd00'

def setup_inputs(seed: int=0):
    np.random.seed(seed)
    _w = jnp.asarray

    def _rec_inputs():
        import jax
        import jax.numpy as jnp
        _rk = jax.random.key(seed)
        x = 4.136e-05 + 0.9999 * jax.random.normal(jax.random.fold_in(_rk, 1), (4, 256, 256), jnp.float32)
        _lenS = 256 - jax.random.randint(jax.random.fold_in(_rk, 7), (4,), 0, max(1, 256 // 4) + 1, jnp.int32)
        _lenS2 = 256 - jax.random.randint(jax.random.fold_in(_rk, 8), (4,), 0, max(1, 256 // 4) + 1, jnp.int32)
        _ctx_1024P = jax.random.normal(jax.random.fold_in(_rk, 11), (4, 16, 128), jnp.float32)
        _ctx_1024c = jax.random.dirichlet(jax.random.fold_in(_rk, 511), 0.3 * jnp.ones((16,), jnp.float32), (4, 256))
        _ctx_1024t = jnp.einsum('bsk,bkd->bsd', _ctx_1024c, _ctx_1024P)
        _ctx_1024t = _ctx_1024t * jax.lax.rsqrt(jnp.mean(jnp.square(_ctx_1024t)) + 1e-12) * 0.953939
        ctx_1024 = -0.000292821 + 1.00034 * (_ctx_1024t + 0.3 * jax.random.normal(jax.random.fold_in(_rk, 611), (4, 256, 128), jnp.float32))
        return (x, ctx_1024)
    x, ctx_1024 = _rec_inputs()

    def _L0_attn_setup():
        import jax, jax.numpy as jnp
        import numpy as np
        B, T, D_MODEL = (2, 256, 256)
        N_HEADS, D_HEAD = (16, 128)
        MAX_SEQ_LEN = 256
        LOGIT_SOFTCAP = 50.0
        EPS = 1e-06

        def precompute_rope(dim, max_seq_len, theta=10000.0):
            freqs = 1.0 / theta ** (np.arange(0, dim, 2, dtype=np.float32) / dim)
            t = np.arange(max_seq_len, dtype=np.float32)
            angles = np.outer(t, freqs)
            return (jnp.asarray(np.cos(angles)), jnp.asarray(np.sin(angles)))

        def rmsnorm(x, w):
            return x * jax.lax.rsqrt(jnp.mean(x * x, axis=-1, keepdims=True) + EPS) * w

        def apply_rope(x, cos, sin):
            n = x.shape[1]
            x1, x2 = (x[..., ::2], x[..., 1::2])
            c = cos[:n][None, :, None, :]
            s = sin[:n][None, :, None, :]
            out = jnp.stack([x1 * c - x2 * s, x1 * s + x2 * c], axis=-1)
            return out.reshape(x.shape)
        key = jax.random.key(seed)
        ks = jax.random.split(key, 6)
        x = jax.random.normal(ks[0], (B, T, D_MODEL), dtype=jnp.float32)
        wq = 0.02 * jax.random.normal(ks[1], (N_HEADS * D_HEAD, D_MODEL), dtype=jnp.float32)
        wk = 0.02 * jax.random.normal(ks[2], (N_HEADS * D_HEAD, D_MODEL), dtype=jnp.float32)
        wv = 0.02 * jax.random.normal(ks[3], (N_HEADS * D_HEAD, D_MODEL), dtype=jnp.float32)
        wo = 0.02 * jax.random.normal(ks[4], (D_MODEL, N_HEADS * D_HEAD), dtype=jnp.float32)
        q_norm_w = jnp.ones((D_HEAD,), dtype=jnp.float32)
        k_norm_w = jnp.ones((D_HEAD,), dtype=jnp.float32)
        rope_cos, rope_sin = precompute_rope(D_HEAD, MAX_SEQ_LEN)
        return {'x': x, 'wq': wq, 'wk': wk, 'wv': wv, 'wo': wo, 'q_norm_w': q_norm_w, 'k_norm_w': k_norm_w, 'rope_cos': rope_cos, 'rope_sin': rope_sin}
    _L0_attn_all = _L0_attn_setup()
    _L0_attn_in = {k: v for k, v in _L0_attn_all.items() if k in ('wq', 'wk', 'wv', 'wo', 'q_norm_w', 'k_norm_w', 'rope_cos', 'rope_sin')}
    del _L0_attn_all

    def _L0_xattn_setup():
        import jax, jax.numpy as jnp
        import numpy as np
        import math
        B, L, DM = (2, 256, 128)
        DS, DC, EXP = (16, 4, 2)
        DI = EXP * DM
        DR = math.ceil(DM / 16)
        DT_MIN, DT_MAX, DT_FLOOR = (0.001, 0.1, 0.0001)

        def _ssm_forward(hidden_states, z, in_proj_w, conv_w, conv_b, x_proj_w, dt_proj_w, dt_proj_b, A_log, D):
            b = hidden_states.shape[0]
            x = jnp.einsum('ed,bld->bel', in_proj_w, hidden_states)
            xp = jnp.pad(x, ((0, 0), (0, 0), (DC - 1, 0)))
            xc = jax.lax.conv_general_dilated(xp, conv_w[:, None, :], window_strides=(1,), padding='VALID', dimension_numbers=('NCH', 'OIH', 'NCH'), feature_group_count=DI)
            u = jax.nn.silu(xc + conv_b[None, :, None])
            x_dbl = jnp.einsum('ke,bel->bkl', x_proj_w, u)
            dt_lo = x_dbl[:, :DR]
            Bm = x_dbl[:, DR:DR + DS]
            Cm = x_dbl[:, DR + DS:]
            delta = jax.nn.softplus(jnp.einsum('er,brl->bel', dt_proj_w, dt_lo) + dt_proj_b[None, :, None])
            A = -jnp.exp(A_log)

            def step(state, xs):
                d_t, B_t, C_t, u_t = xs
                dA = jnp.exp(d_t[..., None] * A)
                state = state * dA + (d_t * u_t)[..., None] * B_t[:, None, :]
                y_t = jnp.einsum('ben,bn->be', state, C_t)
                return (state, y_t)
            xs = (jnp.moveaxis(delta, -1, 0), jnp.moveaxis(Bm, -1, 0), jnp.moveaxis(Cm, -1, 0), jnp.moveaxis(u, -1, 0))
            state0 = jnp.zeros((b, DI, DS), delta.dtype)
            _, ys = jax.lax.scan(step, state0, xs)
            y = jnp.moveaxis(ys, 0, -1)
            y = y + D[None, :, None] * u
            y = y * jax.nn.silu(z)
            return jnp.swapaxes(y, 1, 2)
        key = jax.random.key(seed)
        ks = jax.random.split(key, 8)
        hidden_states = jax.random.normal(ks[0], (B, L, DM), jnp.float32)
        z = jax.random.normal(ks[1], (B, DI, L), jnp.float32)
        in_proj_w = jax.random.normal(ks[2], (DI, DM), jnp.float32) * DM ** (-0.5)
        conv_w = jax.random.normal(ks[3], (DI, DC), jnp.float32) * DC ** (-0.5)
        conv_b = jnp.zeros((DI,), jnp.float32)
        x_proj_w = jax.random.normal(ks[4], (DR + 2 * DS, DI), jnp.float32) * DI ** (-0.5)
        dt_std = DR ** (-0.5)
        dt_proj_w = jax.random.uniform(ks[5], (DI, DR), jnp.float32, -dt_std, dt_std)
        dt = jnp.exp(jax.random.uniform(ks[6], (DI,), jnp.float32) * (math.log(DT_MAX) - math.log(DT_MIN)) + math.log(DT_MIN))
        dt = jnp.clip(dt, DT_FLOOR)
        dt_proj_b = dt + jnp.log(-jnp.expm1(-dt))
        A_log = jnp.log(jnp.broadcast_to(jnp.arange(1, DS + 1, dtype=jnp.float32), (DI, DS)))
        D = jnp.ones((DI,), jnp.float32)
        return dict(hidden_states=hidden_states, z=z, in_proj_w=in_proj_w, conv_w=conv_w, conv_b=conv_b, x_proj_w=x_proj_w, dt_proj_w=dt_proj_w, dt_proj_b=dt_proj_b, A_log=A_log, D=D)
    _L0_xattn_all = _L0_xattn_setup()
    _L0_xattn_in = {k: v for k, v in _L0_xattn_all.items() if k in ('in_proj_w', 'conv_w', 'conv_b', 'x_proj_w', 'dt_proj_w', 'dt_proj_b', 'A_log', 'D')}
    del _L0_xattn_all

    def _L0_ffn_setup():
        import jax, jax.numpy as jnp
        import numpy as np
        TOP_K = 2
        key = jax.random.key(seed)
        ks = jax.random.split(key, 5)
        B, S, D, M, E = (4, 256, 256, 256, 8)
        x = jax.random.normal(ks[0], (B, S, D), dtype=jnp.float32)
        gate_kernel = jax.random.normal(ks[1], (D, E), dtype=jnp.float32) / np.sqrt(D)
        wi_0 = jax.random.normal(ks[2], (E, D, M), dtype=jnp.float32) / np.sqrt(D)
        wi_1 = jax.random.normal(ks[3], (E, D, M), dtype=jnp.float32) / np.sqrt(D)
        wo = jax.random.normal(ks[4], (E, M, D), dtype=jnp.float32) / np.sqrt(M)
        return {'x': x, 'gate_kernel': gate_kernel, 'wi_0': wi_0, 'wi_1': wi_1, 'wo': wo}
    _L0_ffn_all = _L0_ffn_setup()
    _L0_ffn_in = {k: v for k, v in _L0_ffn_all.items() if k in ('gate_kernel', 'wi_0', 'wi_1', 'wo')}
    del _L0_ffn_all
    return {'x': x, 'ctx_1024': ctx_1024, 'L0_attn_wq': _L0_attn_in['wq'], 'L0_attn_wk': _L0_attn_in['wk'], 'L0_attn_wv': _L0_attn_in['wv'], 'L0_attn_wo': _L0_attn_in['wo'], 'L0_attn_q_norm_w': _L0_attn_in['q_norm_w'], 'L0_attn_k_norm_w': _L0_attn_in['k_norm_w'], 'L0_attn_rope_cos': _L0_attn_in['rope_cos'], 'L0_attn_rope_sin': _L0_attn_in['rope_sin'], 'L0_xattn_in_proj_w': _L0_xattn_in['in_proj_w'], 'L0_xattn_conv_w': _L0_xattn_in['conv_w'], 'L0_xattn_conv_b': _L0_xattn_in['conv_b'], 'L0_xattn_x_proj_w': _L0_xattn_in['x_proj_w'], 'L0_xattn_dt_proj_w': _L0_xattn_in['dt_proj_w'], 'L0_xattn_dt_proj_b': _L0_xattn_in['dt_proj_b'], 'L0_xattn_A_log': _L0_xattn_in['A_log'], 'L0_xattn_D': _L0_xattn_in['D'], 'L0_ffn_gate_kernel': _L0_ffn_in['gate_kernel'], 'L0_ffn_wi_0': _L0_ffn_in['wi_0'], 'L0_ffn_wi_1': _L0_ffn_in['wi_1'], 'L0_ffn_wo': _L0_ffn_in['wo']}

def reference(x, ctx_1024, L0_attn_wq, L0_attn_wk, L0_attn_wv, L0_attn_wo, L0_attn_q_norm_w, L0_attn_k_norm_w, L0_attn_rope_cos, L0_attn_rope_sin, L0_xattn_in_proj_w, L0_xattn_conv_w, L0_xattn_conv_b, L0_xattn_x_proj_w, L0_xattn_dt_proj_w, L0_xattn_dt_proj_b, L0_xattn_A_log, L0_xattn_D, L0_ffn_gate_kernel, L0_ffn_wi_0, L0_ffn_wi_1, L0_ffn_wo):
    import jax
    import jax.numpy as jnp

    def _L0_attn_ref(x, wq, wk, wv, wo, q_norm_w, k_norm_w, rope_cos, rope_sin):
        import jax, jax.numpy as jnp
        import numpy as np
        B, T, D_MODEL = (2, 256, 256)
        N_HEADS, D_HEAD = (16, 128)
        MAX_SEQ_LEN = 256
        LOGIT_SOFTCAP = 50.0
        EPS = 1e-06

        def precompute_rope(dim, max_seq_len, theta=10000.0):
            freqs = 1.0 / theta ** (np.arange(0, dim, 2, dtype=np.float32) / dim)
            t = np.arange(max_seq_len, dtype=np.float32)
            angles = np.outer(t, freqs)
            return (jnp.asarray(np.cos(angles)), jnp.asarray(np.sin(angles)))

        def rmsnorm(x, w):
            return x * jax.lax.rsqrt(jnp.mean(x * x, axis=-1, keepdims=True) + EPS) * w

        def apply_rope(x, cos, sin):
            n = x.shape[1]
            x1, x2 = (x[..., ::2], x[..., 1::2])
            c = cos[:n][None, :, None, :]
            s = sin[:n][None, :, None, :]
            out = jnp.stack([x1 * c - x2 * s, x1 * s + x2 * c], axis=-1)
            return out.reshape(x.shape)
        Bx, Tx, _ = x.shape
        scale = D_HEAD ** (-0.5)
        q = (x @ wq.T).reshape(Bx, Tx, N_HEADS, D_HEAD).transpose(0, 2, 1, 3)
        k = (x @ wk.T).reshape(Bx, Tx, N_HEADS, D_HEAD).transpose(0, 2, 1, 3)
        v = (x @ wv.T).reshape(Bx, Tx, N_HEADS, D_HEAD).transpose(0, 2, 1, 3)
        q = rmsnorm(q, q_norm_w)
        k = rmsnorm(k, k_norm_w)
        q = apply_rope(q, rope_cos, rope_sin)
        k = apply_rope(k, rope_cos, rope_sin)
        scores = jnp.einsum('bhtd,bhsd->bhts', q, k) * scale
        scores = LOGIT_SOFTCAP * jnp.tanh(scores / LOGIT_SOFTCAP)
        mask = jnp.triu(jnp.ones((Tx, Tx), dtype=bool), k=1)
        scores = jnp.where(mask[None, None], -jnp.inf, scores)
        attn = jax.nn.softmax(scores, axis=-1)
        out = jnp.einsum('bhts,bhsd->bhtd', attn, v)
        out = out.transpose(0, 2, 1, 3).reshape(Bx, Tx, N_HEADS * D_HEAD)
        return out @ wo.T

    def _L0_xattn_ref(hidden_states, z, in_proj_w, conv_w, conv_b, x_proj_w, dt_proj_w, dt_proj_b, A_log, D):
        import jax, jax.numpy as jnp
        import numpy as np
        import math
        B, L, DM = (2, 256, 128)
        DS, DC, EXP = (16, 4, 2)
        DI = EXP * DM
        DR = math.ceil(DM / 16)
        DT_MIN, DT_MAX, DT_FLOOR = (0.001, 0.1, 0.0001)

        def _ssm_forward(hidden_states, z, in_proj_w, conv_w, conv_b, x_proj_w, dt_proj_w, dt_proj_b, A_log, D):
            b = hidden_states.shape[0]
            x = jnp.einsum('ed,bld->bel', in_proj_w, hidden_states)
            xp = jnp.pad(x, ((0, 0), (0, 0), (DC - 1, 0)))
            xc = jax.lax.conv_general_dilated(xp, conv_w[:, None, :], window_strides=(1,), padding='VALID', dimension_numbers=('NCH', 'OIH', 'NCH'), feature_group_count=DI)
            u = jax.nn.silu(xc + conv_b[None, :, None])
            x_dbl = jnp.einsum('ke,bel->bkl', x_proj_w, u)
            dt_lo = x_dbl[:, :DR]
            Bm = x_dbl[:, DR:DR + DS]
            Cm = x_dbl[:, DR + DS:]
            delta = jax.nn.softplus(jnp.einsum('er,brl->bel', dt_proj_w, dt_lo) + dt_proj_b[None, :, None])
            A = -jnp.exp(A_log)

            def step(state, xs):
                d_t, B_t, C_t, u_t = xs
                dA = jnp.exp(d_t[..., None] * A)
                state = state * dA + (d_t * u_t)[..., None] * B_t[:, None, :]
                y_t = jnp.einsum('ben,bn->be', state, C_t)
                return (state, y_t)
            xs = (jnp.moveaxis(delta, -1, 0), jnp.moveaxis(Bm, -1, 0), jnp.moveaxis(Cm, -1, 0), jnp.moveaxis(u, -1, 0))
            state0 = jnp.zeros((b, DI, DS), delta.dtype)
            _, ys = jax.lax.scan(step, state0, xs)
            y = jnp.moveaxis(ys, 0, -1)
            y = y + D[None, :, None] * u
            y = y * jax.nn.silu(z)
            return jnp.swapaxes(y, 1, 2)
        return _ssm_forward(hidden_states, z, in_proj_w, conv_w, conv_b, x_proj_w, dt_proj_w, dt_proj_b, A_log, D)

    def _L0_ffn_ref(x, gate_kernel, wi_0, wi_1, wo):
        import jax, jax.numpy as jnp
        import numpy as np
        TOP_K = 2
        E = gate_kernel.shape[-1]
        gate_logits = jnp.einsum('bsd,de->bse', x, gate_kernel)
        top_k_weights, top_k_indices = jax.lax.top_k(gate_logits, TOP_K)
        top_k_weights = jax.nn.softmax(top_k_weights.astype(jnp.float32), axis=-1).astype(x.dtype)
        combine_w = jnp.sum(jax.nn.one_hot(top_k_indices, E, dtype=x.dtype) * top_k_weights[..., None], axis=-2)
        h0 = jnp.einsum('bsd,edm->bsem', x, wi_0)
        h1 = jnp.einsum('bsd,edm->bsem', x, wi_1)
        h = jax.nn.silu(h0) * h1 * combine_w[..., None]
        out = jnp.einsum('bsem,emd->bsd', h, wo)
        return out
    x = _layernorm(x + _L0_attn_ref(x, L0_attn_wq, L0_attn_wk, L0_attn_wv, L0_attn_wo, L0_attn_q_norm_w, L0_attn_k_norm_w, L0_attn_rope_cos, L0_attn_rope_sin), axis=-1)
    x = _layernorm(x + _L0_xattn_ref(ctx_1024, x, L0_xattn_in_proj_w, L0_xattn_conv_w, L0_xattn_conv_b, L0_xattn_x_proj_w, L0_xattn_dt_proj_w, L0_xattn_dt_proj_b, L0_xattn_A_log, L0_xattn_D), axis=-1)
    x = _layernorm(x + _L0_ffn_ref(x, L0_ffn_gate_kernel, L0_ffn_wi_0, L0_ffn_wi_1, L0_ffn_wo), axis=-1)
    return x

_drawn_inputs = setup_inputs


def setup_inputs(seed=0):
    import zlib

    import numpy as np

    out = dict(_drawn_inputs(seed))
    spreads = {'L0_attn_q_norm_w': (1.0, 0.2),
     'L0_attn_k_norm_w': (1.0, 0.55),
     'L0_xattn_conv_b': (0.0, 0.1),
     'L0_xattn_D': (1.0, 0.2)}
    factors = {'L0_xattn_dt_proj_w': 2.711}
    for name, (base, spread) in spreads.items():
        noise = np.random.default_rng([zlib.crc32(name.encode()), seed]).standard_normal(out[name].shape)
        drawn = base * np.exp(spread * noise) if base else spread * noise
        out[name] = jnp.asarray(drawn.astype(out[name].dtype))
    for name, factor in factors.items():
        out[name] = (out[name] * factor).astype(out[name].dtype)
    return out
```

```python
from contextlib import ExitStack

import numpy as np

import concourse.bass as bass
from concourse import mybir

ALU = mybir.AluOpType
ACT = mybir.ActivationFunctionType
F32 = mybir.dt.float32
F32R = mybir.dt.float32r
I32 = mybir.dt.int32
ds = bass.ds

P = 128
B, T, D = 4, 256, 256
N = B * T
NT = T // P
KD = D // P
HEADS, DH = 16, 128
G = 4
GROUPS = HEADS // G
GW = G * DH
DM, DI, DS, DC, DR = 128, 256, 16, 4, 8
NC = DI // P
E, M = 8, 256
KM = M // P
CAP = 50.0
RMS_EPS, LN_EPS = 1e-6, 1e-5
CAP_SCALE = DH ** -0.5 / CAP
MAGIC = float(0x5F3759DF)
HI, LO = 0, 1
Q, K, V = 0, 1, 2
FILLS = [(Q, 0), (K, 0), (Q, 1), (K, 1), (V, 0), (V, 1)]
NF = len(FILLS)
TURNS = 7
NEWTON = 3
CHAIN = 3 + 3 * NEWTON


def build(nc, xT, x, wqkv, woT, qw, kw, cosT, sinT, ctxT, in_projT, channels, x_projT,
          dt_projT, gate, experts, out):
    with ExitStack() as ctx:
        def sb(name, shape, dt=F32):
            return ctx.enter_context(nc.sbuf_tensor(name, shape, dt))

        def sem(name):
            return ctx.enter_context(nc.semaphore(name))

        bank = [ctx.enter_context(nc.psum_tensor(f"bank{i}", [P, 512], F32)) for i in range(8)]
        proj, turn, score = bank[0:2], bank[2:4], bank[4:6]
        pv_bank, bc_bank = bank[6], bank[7]

        ident = sb("ident", [P, P])
        causal = sb("causal", [P, P])
        cos_s = sb("cos_s", [P, HEADS])
        sin_s = sb("sin_s", [P, HEADS])
        norm_w = sb("norm_w", [P, 2])
        f_s = sb("f_s", [P, HEADS])
        f_cur = sb("f_cur", [P, G])
        xhl = sb("xhl", [P, 2, KD, N], F32R)
        wraw = sb("wraw", [P, 3 * KD * GW])
        whl = sb("whl", [P, 2, 3 * KD * GW], F32R)
        wo_s = sb("wo_s", [P, HEADS, D])
        qk = sb("qk", [P, 4, GW])
        squares = sb("squares", [P, GW])
        ss = sb("ss", [P, 4, G])
        nx = sb("nx", [P, 4, G])
        ny = sb("ny", [P, 4, G])
        nt = sb("nt", [P, 4, G])
        rs = sb("rs", [P, 2, 4, G])
        qT = sb("qT", [P, G, T])
        kT = sb("kT", [P, G, T])
        v_s = sb("v_s", [P, 2, NT, G, DH + 1])
        pT = sb("pT", [P, G, 3 * P])
        rz = sb("rz", [P, 2, NT])
        o_s = sb("o_s", [P, NT, GW])
        oT = sb("oT", [P, G, T])
        y_acc = sb("y_acc", [P, B, NT, D])
        xn = sb("xn", [P, B, NT, D])
        ctx_s = sb("ctx_s", [P, N])
        in_w = sb("in_w", [P, DI])
        xp_w = sb("xp_w", [P, NC, P])
        dt_w = sb("dt_w", [P, DI])
        chan = sb("chan", [P, NC, 3 + DC + DS])
        cb_s, db_s, dsk_s = chan[:, :, 0], chan[:, :, 1], chan[:, :, 2]
        cw_s, al_s = chan[:, :, 3:3 + DC], chan[:, :, 3 + DC:3 + DC + DS]
        a_s = sb("a_s", [P, NC, DS])
        u_s = sb("u_s", [P, NC, N])
        delta = sb("delta", [P, NC, N])
        du = sb("du", [P, NC, N])
        y_m = sb("y_m", [P, NC, N])
        xd_hl = sb("xd_hl", [P, 2, N], F32R)
        sel = sb("sel", [P, 2 * G], F32R)
        a_cur = sb("a_cur", [P, NC, G])
        dA = sb("dA", [P, 2, NC, T])
        hb = sb("hb", [P, 2, NC, T])
        gate_s = sb("gate_s", [P, KD, E])
        bn = sb("bn", [P, B * NT, 6])
        mv = sb("mv", [P, B * NT, 2])
        ln_r = sb("ln_r", [P, B * NT])
        lx = sb("lx", [P, B * NT])
        lt = sb("lt", [P, B * NT])
        gl = sb("gl", [P, B * NT, E])
        rank = sb("rank", [P, E])
        g1 = sb("g1", [P, B * NT, E])
        g2 = sb("g2", [P, B * NT, E])
        oh1 = sb("oh1", [P, B * NT, E])
        cwt = sb("cwt", [P, B * NT, E])
        m1 = sb("m1", [P, B * NT])
        m2 = sb("m2", [P, B * NT])
        mr = sb("mr", [P, B * NT])
        w1 = sb("w1", [P, B * NT])
        w2 = sb("w2", [P, B * NT])
        pool_mark = sb("pool_mark", [P, 1])
        h_odd = sb("h_odd", [P, 2, KM, 512], F32R)

        xT_raw = qk[:, :, :].rearrange("p a b -> p (a b)").rearrange("p (k n) -> p k n", k=KD)
        xd_s = pT[:, :, :].rearrange("p a b -> p (a b)")[:, 0:N]
        one_p = xn[:, :, :, :].rearrange("p b t d -> p (b t d)").rearrange("p (c n) -> p c n", c=NC)
        wq_raw = wraw[:, :].rearrange("p (x k n) -> p x k n", x=3, k=KD)
        wq_hl = whl[:, :, :].rearrange("p h (x k n) -> p h x k n", x=3, k=KD)
        wf_raw = wraw[:, :].rearrange("p (s m k n) -> p s m k n", s=2, m=3, k=KD)
        wf_hl = whl[:, :, :].rearrange("p h (s m k n) -> p h s m k n", s=2, m=3, k=KD)
        x2T = u_s
        tanh_s = delta[:, :, :].rearrange("p c n -> p (c n)").rearrange("p (b t d) -> p b t d", b=B, t=NT)
        gated = du[:, :, :].rearrange("p c n -> p (c n)").rearrange("p (b c l) -> p b c l", b=B, c=NC)
        sg = dA[:, :, :, :].rearrange("p s c t -> p s (c t)")
        h_hl = [xd_hl[:, :, :].rearrange("p h (m n) -> p h m n", m=KM), h_odd[:, :, :, :]]
        h32 = qk[:, :, :].rearrange("p (r m) n -> p r m n", r=2)

        s_zeroed, s_ctx, s_small, s_x, s_tab, s_wo = (sem(n) for n in (
            "zeroed", "ctx_loaded", "small_loaded", "x_loaded", "tables_loaded", "wo_loaded"))
        s_wraw = [sem(f"raw_loaded{x}") for x in range(3)]
        s_xn = sem("xn_loaded")
        s_eraw = [sem(f"expert_loaded{p}") for p in range(2)]
        s_const, s_ones = sem("constants_made"), sem("ones_made")
        s_inproj, s_conv, s_u, s_xdbl, s_xds, s_xdhl = (sem(n) for n in (
            "inproj_done", "conv_tap", "u_ready", "xdbl_done", "xdbl_copied", "xdbl_split"))
        s_dt, s_soft_a, s_soft_d, s_du, s_ready = (sem(n) for n in (
            "dt_done", "softplus_act", "softplus_dve", "du_ready", "a_ready"))
        s_xhi, s_xsplit, s_fac = sem("x_high"), sem("x_split"), sem("factors")
        s_whi, s_split = sem("w_high"), sem("w_split")
        s_proj, s_copied, s_squared, s_stat, s_scaled = (sem(n) for n in (
            "projected", "proj_copied", "squared", "norm_step", "q_scaled"))
        s_turned, s_evac, s_yadd, s_scores, s_tanh, s_exp, s_masked = (sem(n) for n in (
            "turned", "turn_copied", "y_added", "scored", "tanh_done", "exp_done", "masked"))
        s_pv, s_rz, s_onorm = sem("pv_done"), sem("z_inverted"), sem("o_normed")
        s_cur, s_bc, s_bcfree, s_dA, s_dbu, s_scan, s_ysum = (sem(n) for n in (
            "group_columns", "bc_spread", "bc_used", "dA_ready", "dbu_ready", "scanned", "y_summed"))
        s_mid, s_tg, s_gt, s_x2, s_x2T, s_x2c, s_logit, s_ge = (sem(n) for n in (
            "mid_step", "tanh_gate", "gated_turned", "x2_ready", "x2_turned", "x2_copied", "logits", "gate_exp"))
        s_x2hl, s_ehi, s_esplit = sem("x2_split"), sem("expert_high"), sem("expert_split")
        s_h0, s_h1, s_sg, s_h, s_hhi, s_hlo, s_out, s_outfree = (sem(n) for n in (
            "h0_done", "h1_done", "silu_done", "h_ready", "h_high", "h_low", "out_done", "out_added"))
        s_store, s_fin, s_own = sem("stored"), sem("normed"), sem("dve_step")

        block = ctx.enter_context(nc.Block())

        def bcast(ap, shape):
            return ap.broadcast_to(shape)

        @block.sync
        def _(sp):
            sp.dma_start(ctx_s[:, :], ctxT).then_inc(s_ctx, 16)
            sp.dma_start(in_w[:, :], in_projT).then_inc(s_small, 16)
            sp.dma_start(chan[:, :, :], channels.rearrange("(c p) n -> p c n", p=P)).then_inc(s_small, 16)
            sp.wait_ge(s_zeroed, 1)
            sp.dma_start(xp_w[:, :, 0:DR + 2 * DS], x_projT.rearrange("(c p) n -> p c n", p=P)).then_inc(s_small, 16)
            sp.dma_start(dt_w[0:DR, :], dt_projT).then_inc(s_small, 16)
            sp.dma_start(xT_raw, xT.rearrange("(k p) n -> p k n", p=P)).then_inc(s_x, 16)
            for x_ in range(3):
                sp.dma_start(wq_raw[:, x_], wqkv[0, x_].rearrange("(k p) n -> p k n", p=P)).then_inc(s_wraw[x_], 16)
            for half in range(2):
                sp.dma_start(cos_s[half * 64:half * 64 + 64, :], cosT).then_inc(s_tab, 16)
                sp.dma_start(sin_s[half * 64:half * 64 + 64, :], sinT).then_inc(s_tab, 16)
            sp.dma_start(norm_w[:, 0:1], qw.rearrange("(n o) -> n o", o=1)).then_inc(s_tab, 16)
            sp.dma_start(norm_w[:, 1:2], kw.rearrange("(n o) -> n o", o=1)).then_inc(s_tab, 16)
            sp.dma_start(wo_s[:, :, :], woT.rearrange("(h p) n -> p h n", p=P)).then_inc(s_wo, 16)
            sp.dma_start(gate_s[:, :, :], gate.rearrange("(k p) n -> p k n", p=P)).then_inc(s_wo, 16)
            with sp.Fori(0, GROUPS - 1) as i:
                for x_ in range(3):
                    sp.wait_ge(s_split, i * 3 + (x_ + 1))
                    src = wqkv[ds(i + 1, 1), x_].rearrange("o (k p) n -> p (o k) n", p=P)
                    sp.dma_start(wq_raw[:, x_], src).then_inc(s_wraw[x_], 16)
            sp.wait_ge(s_soft_d, 10)
            sp.dma_start(xn[:, :, :, :], x.rearrange("(b t p) d -> p b t d", p=P, t=NT)).then_inc(s_xn, 16)
            sp.wait_ge(s_split, 3 * GROUPS)
            for e in range(2):
                sp.dma_start(wf_raw[:, e].rearrange("p m k n -> p (m k) n"),
                             experts[e].rearrange("(a p) n -> p a n", p=P)).then_inc(s_eraw[e], 16)
            with sp.Fori(0, E // 2 - 1) as i:
                for p in range(2):
                    sp.wait_ge(s_esplit, i * 2 + (p + 1))
                    src = experts[ds(i * 2 + (2 + p), 1)].rearrange("o (a p) n -> p (o a) n", p=P)
                    sp.dma_start(wf_raw[:, p].rearrange("p m k n -> p (m k) n"), src).then_inc(s_eraw[p], 16)
            for half in range(2):
                sp.wait_ge(s_fin, half + 1)
                sp.dma_start(out.rearrange("(b t p) d -> p b t d", p=P, t=NT)[:, 2 * half:2 * half + 2],
                             xn[:, 2 * half:2 * half + 2]).then_inc(s_store, 16)
            sp.wait_ge(s_store, 32)

        @block.tensor
        def _(pe):
            def three_pass(dst, pairs):
                for n, (s, m) in enumerate(pairs):
                    pe.matmul(dst, s[HI], m[HI], start=n == 0, stop=False)
                    pe.matmul(dst, s[HI], m[LO], start=False, stop=False)
                    last = pe.matmul(dst, s[LO], m[HI], start=False, stop=n == len(pairs) - 1)
                return last

            def fill(U, b, f, first_of_group=None):
                part, t = FILLS[f]
                if isinstance(U, int) and U == 0:
                    if f >= 2:
                        pe.wait_ge(s_copied, f - 1)
                else:
                    pe.wait_ge(s_copied, U * NF + (f - 1))
                if first_of_group is not None:
                    pe.wait_ge(s_split, first_of_group * 3 + (part + 1))
                at = b * T + t * P
                pairs = [((xhl[:, HI, k, at:at + P], xhl[:, LO, k, at:at + P]),
                          (wq_hl[:, HI, part, k, :], wq_hl[:, LO, part, k, :])) for k in range(KD)]
                three_pass(proj[f % 2][:, :], pairs).then_inc(s_proj, 1)

            pe.wait_ge(s_ctx, 16)
            pe.wait_ge(s_small, 16 * 4)
            for half in range(2):
                for c in range(NC):
                    pe.matmul(bank[2 + 2 * half + c][:, :], in_w[:, c * P:(c + 1) * P],
                              ctx_s[:, half * 512:(half + 1) * 512], start=True, stop=True).then_inc(s_inproj, 1)
            pe.wait_ge(s_xsplit, 1)
            fill(0, 0, 0, 0)
            fill(0, 0, 1, 0)
            for half in range(2):
                pe.wait_ge(s_u, 2 * half + 2)
                for c in range(NC):
                    last = pe.matmul(bank[6 + half][:, :], xp_w[:, c, :], u_s[:, c, half * 512:(half + 1) * 512],
                                     start=c == 0, stop=c == NC - 1)
                last.then_inc(s_xdbl, 1)
            fill(0, 0, 2)
            fill(0, 0, 3)
            for c in range(NC):
                for half in range(2):
                    pe.wait_ge(s_xds, half + 1)
                    pe.matmul(bank[2 + 2 * c + half][:, :], dt_w[:, c * P:(c + 1) * P],
                              xd_s[:, half * 512:(half + 1) * 512], start=True, stop=True).then_inc(s_dt, 1)
            fill(0, 0, 4, 0)
            fill(0, 0, 5)
            pe.wait_ge(s_xdhl, 1)
            pe.wait_ge(s_wo, 32)

            def turn_bank(u, k):
                return turn[(TURNS * u + k) % 2]

            def turn_qk(U, u, x_):
                if x_ % 2 == 0:
                    pe.wait_ge(s_scaled, U * 2 + (x_ // 2 + 1))
                else:
                    pe.wait_ge(s_copied, U * NF + (x_ + 1))
                if x_ == 0 and isinstance(U, int) and U == 0:
                    pass
                elif x_ == 1:
                    pe.wait_ge(s_yadd, U + 1)
                elif x_ >= 2:
                    pe.wait_ge(s_evac, U * 6 + (x_ - 1))
                for h in range(G):
                    last = pe.transpose(turn_bank(u, x_)[:, h * P:(h + 1) * P], qk[:, x_, h * DH:(h + 1) * DH], ident[:, :])
                last.then_inc(s_turned, 1)

            def scores(U, h):
                if h == 0:
                    pe.wait_ge(s_evac, U * 6 + 4)
                if h >= 2:
                    pe.wait_ge(s_tanh, U * 4 + (h - 1))
                pe.matmul(score[h % 2][:, 0:T], kT[:, h, 0:P], qT[:, h, :], start=True, stop=True)
                pe.matmul(score[h % 2][:, T:T + P], kT[:, h, P:T], qT[:, h, P:T],
                          start=True, stop=True).then_inc(s_scores, 1)

            def values(U, u, h):
                pe.wait_ge(s_masked, U * 4 + (h + 1))
                if h == 0:
                    pe.wait_ge(s_copied, U * NF + NF)
                else:
                    pe.wait_ge(s_onorm, U * 4 + h)
                W = DH + 1
                pe.matmul(pv_bank[:, 0:W], pT[:, h, 0:P], v_s[:, u % 2, 0, h, :], start=True, stop=True)
                pe.matmul(pv_bank[:, T:T + W], pT[:, h, P:2 * P], v_s[:, u % 2, 0, h, :], start=True, stop=False)
                pe.matmul(pv_bank[:, T:T + W], pT[:, h, 2 * P:3 * P], v_s[:, u % 2, 1, h, :],
                          start=False, stop=True).then_inc(s_pv, 1)

            def spread(U, i, u, j):
                if u == 0 and j == 0:
                    pe.wait_ge(s_cur, i + 1)
                pe.wait_ge(s_bcfree, U * 4 + (j + 1))
                for s in range(2):
                    one_hot = bcast(sel[:, s * G + j:s * G + j + 1], [P, P])
                    for part in (HI, LO):
                        last = pe.matmul(bc_bank[:, s * T:(s + 1) * T], one_hot, xd_hl[:, part, u * T:(u + 1) * T],
                                         start=part == HI, stop=part == LO)
                last.then_inc(s_bc, 1)

            def turn_o(U, u, t):
                if t == 0:
                    pe.wait_ge(s_onorm, U * 4 + G)
                pe.wait_ge(s_evac, U * 6 + (3 + t))
                for h in range(G):
                    last = pe.transpose(turn_bank(u, 4 + t)[:, h * P:(h + 1) * P], o_s[:, t, h * DH:(h + 1) * DH], ident[:, :])
                last.then_inc(s_turned, 1)

            def project_out(U, i, u):
                pe.wait_ge(s_evac, U * 6 + 6)
                for t in range(NT):
                    for h in range(G):
                        w = wo_s[:, ds(i * G + h, 1), :].rearrange("p o n -> p (o n)")
                        last = pe.matmul(turn_bank(u, 6)[:, t * D:(t + 1) * D], oT[:, h, t * P:(t + 1) * P], w,
                                         start=h == 0, stop=h == G - 1)
                last.then_inc(s_turned, 1)

            def unit(i, u, more):
                U, nb = i * B + u, (u + 1) % B
                group = i + 1 if u == B - 1 else None

                def ahead(f):
                    if more:
                        fill(U + 1, nb, f, group if f in (0, 1, 4) else None)

                ahead(0)
                ahead(1)
                turn_qk(U, u, 0)
                turn_qk(U, u, 1)
                ahead(2)
                turn_qk(U, u, 2)
                turn_qk(U, u, 3)
                spread(U, i, u, 0)
                scores(U, 0)
                ahead(3)
                scores(U, 1)
                values(U, u, 0)
                spread(U, i, u, 1)
                scores(U, 2)
                values(U, u, 1)
                spread(U, i, u, 2)
                ahead(4)
                scores(U, 3)
                values(U, u, 2)
                spread(U, i, u, 3)
                values(U, u, 3)
                turn_o(U, u, 0)
                turn_o(U, u, 1)
                ahead(5)
                project_out(U, i, u)

            with pe.Fori(0, GROUPS - 1) as i:
                for u in range(B):
                    unit(i, u, True)
            for u in range(B):
                unit(GROUPS - 1, u, u < B - 1)

            for b in range(B):
                pe.wait_ge(s_gt, b + 1)
                for l in range(NT):
                    for c in range(NC):
                        last = pe.transpose(bank[b % 4][:, l * DI + c * P:l * DI + (c + 1) * P],
                                            gated[:, b, c, l * P:(l + 1) * P], ident[:, :])
                last.then_inc(s_tg, 1)
            for b in range(B):
                pe.wait_ge(s_x2, b + 1)
                for k in range(KD):
                    for t in range(NT):
                        last = pe.transpose(bank[b % 4][:, k * T + t * P:k * T + (t + 1) * P],
                                            xn[:, b, t, k * P:(k + 1) * P], ident[:, :])
                last.then_inc(s_x2T, 1)
            for b in range(B):
                pe.wait_ge(s_x2c, b + 1)
                for t in range(NT):
                    at = b * T + t * P
                    for k in range(KD):
                        last = pe.matmul(bank[7][:, (b * NT + t) * E:(b * NT + t + 1) * E], x2T[:, k, at:at + P],
                                         gate_s[:, k, :], start=k == 0, stop=k == KD - 1)
            last.then_inc(s_logit, 1)

            def hidden(S, e, slot, half):
                if half == 0:
                    pe.wait_ge(s_esplit, e + 1)
                for m in range(KM):
                    if not (isinstance(S, int) and S == 0):
                        pe.wait_ge(s_h, S * 2 + (m - 1))
                    for w, s_done in ((0, s_h0), (1, s_h1)):
                        pairs = [((wf_hl[:, HI, slot, w, k, m * P:(m + 1) * P], wf_hl[:, LO, slot, w, k, m * P:(m + 1) * P]),
                                  (xhl[:, HI, k, half * 512:(half + 1) * 512], xhl[:, LO, k, half * 512:(half + 1) * 512]))
                                 for k in range(KD)]
                        three_pass(bank[2 * m + w][:, :], pairs).then_inc(s_done, 1)

            def down(S, slot, par):
                pe.wait_ge(s_hlo, S * 2 + 2)
                for r in range(2):
                    pe.wait_ge(s_outfree, S * 2 + (r + 1))
                    for t in range(2):
                        at = (2 * r + t) * P
                        pairs = [((h_hl[par][:, HI, m, at:at + P], h_hl[par][:, LO, m, at:at + P]),
                                  (wf_hl[:, HI, slot, 2, m, :], wf_hl[:, LO, slot, 2, m, :])) for m in range(KM)]
                        last = three_pass(bank[4 + r][:, t * D:(t + 1) * D], pairs)
                    last.then_inc(s_out, 1)

            pe.wait_ge(s_x2hl, B)
            hidden(0, 0, 0, 0)

            def experts_pair(i, last_pair):
                for q in range(4):
                    S = i * 4 + q
                    if not (last_pair and q == 3):
                        nq = (q + 1) % 4
                        e = i * 2 + ((q + 1) // 2)
                        hidden(S + 1, e, nq // 2, nq % 2)
                    down(S, q // 2, q % 2)

            with pe.Fori(0, E // 2 - 1) as i:
                experts_pair(i, False)
            experts_pair(E // 2 - 1, True)

        @block.scalar
        def _(act):
            def copy_proj(U, par, f):
                part, t = FILLS[f]
                act.wait_ge(s_proj, U * NF + (f + 1))
                if part == V:
                    act.activation(v_s[:, par, t, :, 0:DH], proj[f % 2][:, :].rearrange("p (h d) -> p h d", h=G),
                                   ACT.Copy).then_inc(s_copied, 1)
                else:
                    if isinstance(U, int) and U == 0:
                        act.wait_ge(s_xsplit, 1)
                    else:
                        act.wait_ge(s_squared, U * 4 + (f - 3))
                        act.wait_ge(s_turned, U * TURNS + (f - 6))
                    act.activation(qk[:, f, :], proj[f % 2][:, :], ACT.Copy).then_inc(s_copied, 1)

            for half in range(2):
                for c in range(NC):
                    act.wait_ge(s_conv, (DC - 1) * 4 + 2 * half + c + 1)
                    act.activation(u_s[:, c, half * 512:(half + 1) * 512], y_m[:, c, half * 512:(half + 1) * 512],
                                   ACT.Silu, bias=cb_s[:, c:c + 1]).then_inc(s_u, 1)
            copy_proj(0, 0, 0)
            copy_proj(0, 0, 1)
            for half in range(2):
                act.wait_ge(s_xdbl, half + 1)
                act.activation(xd_s[:, half * 512:(half + 1) * 512], bank[6 + half][:, :], ACT.Copy).then_inc(s_xds, 1)
            act.activation(a_s[:, :, :], al_s[:, :, :], ACT.Exp).then_inc(s_ready, 1)
            copy_proj(0, 0, 2)
            copy_proj(0, 0, 3)
            for c in range(NC):
                for half in range(2):
                    z = bank[2 + 2 * c + half][:, :]
                    at = slice(half * 512, (half + 1) * 512)
                    act.wait_ge(s_dt, 2 * c + half + 1)
                    act.activation(du[:, c, at], z, ACT.Abs, bias=db_s[:, c:c + 1])
                    act.activation(y_m[:, c, at], z, ACT.Relu, bias=db_s[:, c:c + 1]).then_inc(s_soft_a, 1)
            for c in range(NC):
                act.wait_ge(s_soft_a, 2 * c + 2)
                act.activation(delta[:, c, :], du[:, c, :], ACT.Exp, scale=-1.0).then_inc(s_soft_a, 1)
            copy_proj(0, 0, 4)
            copy_proj(0, 0, 5)
            for c in range(NC):
                act.wait_ge(s_soft_d, c + 1)
                act.wait_ge(s_soft_a, 2 * NC + c + 1)
                act.activation(du[:, c, :], one_p[:, c, :], ACT.Ln).then_inc(s_soft_a, 1)

            def copy_turned(U, i, u, k):
                act.wait_ge(s_turned, U * TURNS + (k + 1))
                src = turn[(TURNS * u + k) % 2][:, :].rearrange("p (h t) -> p h t", h=G)
                t = (k // 2) if k < 4 else k - 4
                if k in (1, 3):
                    if u == 0 and k == 1:
                        act.wait_ge(s_cur, i + 1)
                    for h in range(G):
                        last = act.activation(kT[:, h, t * P:(t + 1) * P], src[:, h, :], ACT.Copy, scale=f_cur[:, h:h + 1])
                    last.then_inc(s_evac, 1)
                else:
                    dst = qT if k < 4 else oT
                    act.activation(dst[:, :, t * P:(t + 1) * P], src, ACT.Copy).then_inc(s_evac, 1)

            def softcap(U, u, h):
                act.wait_ge(s_scores, U * 4 + (h + 1))
                act.activation(pT[:, h, 0:T], score[h % 2][:, 0:T], ACT.Tanh, scale=rs[:, u % 2, 1, h:h + 1])
                act.activation(pT[:, h, T:T + P], score[h % 2][:, T:T + P], ACT.Tanh,
                               scale=rs[:, u % 2, 3, h:h + 1]).then_inc(s_tanh, 1)

            def exps(U, h):
                act.wait_ge(s_tanh, U * 4 + (h + 1))
                act.activation(pT[:, h, :], pT[:, h, :], ACT.Exp, scale=CAP).then_inc(s_exp, 1)

            def decay(U, i, u, j):
                if u == 0 and j == 0:
                    act.wait_ge(s_cur, i + 1)
                act.wait_ge(s_scan, U * 4 + (j + 1))
                for c in range(NC):
                    last = act.activation(dA[:, j % 2, c, :], delta[:, c, u * T:(u + 1) * T], ACT.Exp,
                                          scale=a_cur[:, c, j:j + 1])
                last.then_inc(s_dA, 1)

            def unit(i, u, more):
                U = i * B + u

                def ahead(f):
                    if more:
                        copy_proj(U + 1, (u + 1) % 2, f)

                ahead(0)
                ahead(1)
                copy_turned(U, i, u, 0)
                copy_turned(U, i, u, 1)
                ahead(2)
                copy_turned(U, i, u, 2)
                copy_turned(U, i, u, 3)
                decay(U, i, u, 0)
                softcap(U, u, 0)
                ahead(3)
                exps(U, 0)
                softcap(U, u, 1)
                decay(U, i, u, 1)
                exps(U, 1)
                softcap(U, u, 2)
                decay(U, i, u, 2)
                exps(U, 2)
                ahead(4)
                softcap(U, u, 3)
                decay(U, i, u, 3)
                exps(U, 3)
                copy_turned(U, i, u, 4)
                copy_turned(U, i, u, 5)
                ahead(5)

            act.wait_ge(s_du, 1)
            with act.Fori(0, GROUPS - 1) as i:
                for u in range(B):
                    unit(i, u, True)
            for u in range(B):
                unit(GROUPS - 1, u, u < B - 1)

            for b in range(B):
                act.wait_ge(s_mid, b + 1)
                act.activation(tanh_s[:, b], y_acc[:, b], ACT.Tanh, scale=0.5).then_inc(s_tanh, 1)
            for b in range(B):
                act.wait_ge(s_x2T, b + 1)
                act.activation(x2T[:, :, b * T:(b + 1) * T], bank[b % 4][:, :].rearrange("p (k t) -> p k t", k=KD),
                               ACT.Copy).then_inc(s_x2c, 1)
            act.wait_ge(s_ge, 1)
            act.activation(w1[:, :], m2[:, :], ACT.Exp).then_inc(s_ge, 1)

            def silu(S, m):
                act.wait_ge(s_h0, S * 2 + (m + 1))
                act.activation(sg[:, m, :], bank[2 * m][:, :], ACT.Silu).then_inc(s_sg, 1)

            def high(S, par, m):
                act.wait_ge(s_h, S * 2 + (m + 1))
                act.activation(h_hl[par][:, HI, m, :], h32[:, par, m, :], ACT.Copy).then_inc(s_hhi, 1)

            def step(S, par):
                silu(S, 0)
                silu(S, 1)
                high(S, par, 0)
                high(S, par, 1)

            with act.Fori(0, E // 2) as i:
                for q in range(4):
                    step(i * 4 + q, q % 2)

        @block.vector
        def _(dve):
            dve.memset(xp_w[:, :, :], 0.0)
            dve.memset(dt_w[:, :], 0.0).then_inc(s_zeroed, 1)
            dve.memset(y_acc[:, :, :, :], 0.0).then_inc(s_yadd, 1)
            dve.memset(rz[:, :, :], 0.0).then_inc(s_scan, 2)

            dve.wait_ge(s_small, 16 * 4)
            for tap in range(DC):
                back = tap
                for n in range(4):
                    half, c = n // 2, n % 2
                    src = bank[2 + n][:, :].rearrange("p (b t) -> p b t", b=2)[:, :, 0:T - back]
                    acc = y_m[:, c, half * 512:(half + 1) * 512].rearrange("p (b t) -> p b t", b=2)[:, :, back:T]
                    w = cw_s[:, c, DC - 1 - back:DC - back]
                    if tap == 0:
                        dve.wait_ge(s_inproj, n + 1)
                        dve.tensor_scalar(acc, src, w, None, ALU.mult).then_inc(s_conv, 1)
                    else:
                        dve.wait_ge(s_conv, (tap - 1) * 4 + n + 1)
                        dve.scalar_tensor_tensor(out=acc, in0=src, scalar=w, in1=acc, op0=ALU.mult,
                                                 op1=ALU.add).then_inc(s_conv, 1)

            dve.wait_ge(s_x, 16)
            dve.tensor_copy(xhl[:, HI], xT_raw).then_inc(s_xhi, 1)
            dve.wait_ge(s_xhi, 1)
            dve.tensor_tensor(xhl[:, LO], xT_raw, xhl[:, HI].bitcast(F32), ALU.subtract).then_inc(s_xsplit, 1)

            def split(i, part):
                dve.wait_ge(s_wraw[part], i * 16 + 16)
                dve.tensor_copy(wq_hl[:, HI, part], wq_raw[:, part]).then_inc(s_whi, 1)
                dve.wait_ge(s_whi, i * 3 + (part + 1))
                dve.tensor_tensor(wq_hl[:, LO, part], wq_raw[:, part], wq_hl[:, HI, part].bitcast(F32),
                                  ALU.subtract).then_inc(s_split, 1)

            for part in (Q, K, V):
                split(0, part)

            dve.wait_ge(s_tab, 96)
            dve.tensor_tensor(cos_s[:, :], cos_s[:, :], cos_s[:, :], ALU.mult)
            dve.tensor_tensor(sin_s[:, :], sin_s[:, :], sin_s[:, :], ALU.mult).then_inc(s_fac, 1)
            dve.wait_ge(s_fac, 1)
            dve.tensor_tensor(f_s[:, :], cos_s[:, :], sin_s[:, :], ALU.add).then_inc(s_fac, 1)
            dve.wait_ge(s_fac, 2)
            dve.tensor_scalar(f_s[:, :], f_s[:, :], norm_w[:, 0:1], norm_w[:, 1:2], ALU.mult, ALU.mult).then_inc(s_fac, 1)

            def squares_of(U, x_):
                dve.wait_ge(s_copied, U * NF + (x_ + 1))
                if not (isinstance(U, int) and U == 0 and x_ == 0):
                    dve.wait_ge(s_squared, U * 4 + x_)
                for h in range(G):
                    col = qk[:, x_, h * DH:(h + 1) * DH]
                    last = dve.tensor_tensor_reduce(squares[:, h * DH:(h + 1) * DH], col, col, 1.0, 0.0, ALU.mult, ALU.add, ss[:, x_, h:h + 1])
                last.then_inc(s_squared, 1)

            def chain_steps(x, y, t, first, final, s, at):
                steps = [first]
                steps.append(lambda: dve.tensor_scalar(t.bitcast(I32), x.bitcast(I32), 1, None, ALU.logical_shift_right))
                steps.append(lambda: dve.tensor_scalar(y.bitcast(I32), t.bitcast(I32), -1.0, MAGIC, ALU.mult, ALU.add))
                for k in range(NEWTON):
                    dst = final if k == NEWTON - 1 else y
                    steps.append(lambda: dve.tensor_tensor(t, y, y, ALU.mult))
                    steps.append(lambda: dve.scalar_tensor_tensor(out=t, in0=t, scalar=-0.5, in1=x, op0=ALU.mult, op1=ALU.mult))
                    steps.append(lambda dst=dst: dve.scalar_tensor_tensor(out=dst, in0=t, scalar=1.5, in1=y, op0=ALU.add, op1=ALU.mult))
                for n, make in enumerate(steps):
                    if n:
                        dve.wait_ge(s, at + n)
                    make().then_inc(s, 1)
                    yield

            def norm_factors(U, par):
                c2 = CAP_SCALE ** 2

                def first():
                    dve.wait_ge(s_squared, U * 4 + 4)
                    dve.tensor_scalar(nx[:, 0::2, :], ss[:, 0::2, :], 1.0 / DH, RMS_EPS, ALU.mult, ALU.add)
                    return dve.tensor_scalar(nx[:, 1::2, :], ss[:, 1::2, :], 1.0 / (DH * c2), RMS_EPS / c2, ALU.mult, ALU.add)
                return chain_steps(nx[:, :, :], ny[:, :, :], nt[:, :, :], first, rs[:, par], s_stat, U * CHAIN)

            def run(steps, n=CHAIN):
                for _ in range(n):
                    next(steps, None)

            def soft_one(c):
                dve.wait_ge(s_soft_a, 2 * NC + c + 1)
                dve.tensor_scalar(one_p[:, c, :], delta[:, c, :], 1.0, None, ALU.add).then_inc(s_soft_d, 1)

            dve.wait_ge(s_xds, 2)
            dve.tensor_copy(xd_hl[:, HI, :], xd_s).then_inc(s_xhi, 1)
            dve.wait_ge(s_xhi, 2)
            dve.tensor_tensor(xd_hl[:, LO, :], xd_s, xd_hl[:, HI, :].bitcast(F32), ALU.subtract).then_inc(s_xdhl, 1)
            squares_of(0, 0)
            squares_of(0, 1)
            for c in range(NC):
                soft_one(c)
            dve.wait_ge(s_ready, 1)
            dve.tensor_scalar(a_s[:, :, :], a_s[:, :, :], -1.0, None, ALU.mult).then_inc(s_ready, 1)
            squares_of(0, 2)
            squares_of(0, 3)
            run(norm_factors(0, 0))
            s2 = 2 * NC
            for c in range(NC):
                dve.wait_ge(s_soft_a, 3 * NC + c + 1)
                dve.tensor_scalar(one_p[:, c, :], one_p[:, c, :], -1.0, None, ALU.add).then_inc(s_soft_d, 1)
            for c in range(NC):
                dve.wait_ge(s_soft_d, NC + c + 1)
                dve.tensor_tensor(one_p[:, c, :], delta[:, c, :], one_p[:, c, :], ALU.subtract).then_inc(s_soft_d, 1)
            for c in range(NC):
                dve.wait_ge(s_soft_d, 2 * NC + c + 1)
                dve.tensor_tensor(du[:, c, :], du[:, c, :], one_p[:, c, :], ALU.add).then_inc(s_soft_d, 1)
            for c in range(NC):
                dve.wait_ge(s_soft_d, 3 * NC + c + 1)
                dve.tensor_tensor(delta[:, c, :], du[:, c, :], y_m[:, c, :], ALU.add).then_inc(s_soft_d, 1)
            dve.wait_ge(s_soft_d, 5 * NC)
            dve.tensor_tensor(du[:, :, :], delta[:, :, :], u_s[:, :, :], ALU.mult).then_inc(s_du, 1)
            for c in range(NC):
                last = dve.tensor_scalar(y_m[:, c, :], u_s[:, c, :], dsk_s[:, c:c + 1], None, ALU.mult)
            last.then_inc(s_bcfree, 1)
            dve.wait_ge(s_bcfree, 1)
            dve.wait_ge(s_ready, 2)
            dve.wait_ge(s_fac, 3)
            dve.wait_ge(s_const, 1)

            def group_columns(i):
                for s in range(2):
                    dve.tensor_scalar(sel[:, s * G:(s + 1) * G], ident[:, ds(i * G + (DR + s * DS), G)], 1.0, None, ALU.mult)
                dve.tensor_scalar(f_cur[:, :], f_s[:, ds(i * G, G)], 1.0, None, ALU.mult)
                dve.tensor_scalar(a_cur[:, :, :], a_s[:, :, ds(i * G, G)], 1.0, None, ALU.mult).then_inc(s_cur, 1)

            def bx(ap):
                return bcast(ap.rearrange("p (o t) -> p o t", o=1), [P, NC, T])

            def scan_in(U, u, j):
                dve.wait_ge(s_bc, U * 4 + (j + 1))
                dve.wait_ge(s_ysum, U * 4 + (j + 1))
                dve.tensor_tensor(hb[:, j % 2], du[:, :, u * T:(u + 1) * T], bx(bc_bank[:, 0:T]), ALU.mult).then_inc(s_dbu, 1)

            def scan(U, j):
                dve.wait_ge(s_dbu, U * 4 + (j + 1))
                dve.wait_ge(s_dA, U * 4 + (j + 1))
                for c in range(NC):
                    last = dve.tensor_tensor_scan(hb[:, j % 2, c, :], dA[:, j % 2, c, :], hb[:, j % 2, c, :], 0.0,
                                                  ALU.mult, ALU.add)
                last.then_inc(s_scan, 1)

            def scan_out(U, j):
                dve.wait_ge(s_scan, U * 4 + (j + 3))
                dve.tensor_tensor(hb[:, j % 2], hb[:, j % 2], bx(bc_bank[:, T:2 * T]), ALU.mult).then_inc(s_bcfree, 1)

            def invert_z(U, h):
                dve.wait_ge(s_pv, U * 4 + (h + 1))
                z = pv_bank[:, :].rearrange("p (t c) -> p t c", t=NT)[:, :, DH:DH + 1]
                dve.reciprocal(rz[:, h % 2, :].rearrange("p (t o) -> p t o", o=1), z).then_inc(s_rz, 1)

            def norm_o(U, h):
                dve.wait_ge(s_rz, U * 4 + (h + 1))
                o = pv_bank[:, :].rearrange("p (t c) -> p t c", t=NT)[:, :, 0:DH]
                dve.tensor_tensor(o_s[:, :, h * DH:(h + 1) * DH], o,
                                  bcast(rz[:, h % 2, :].rearrange("p (t o) -> p t o", o=1), [P, NT, DH]), ALU.mult).then_inc(s_onorm, 1)

            def unit(i, u, more, splits):
                U = i * B + u
                if u == 0:
                    group_columns(i)
                nf = norm_factors(U + 1, (u + 1) % 2) if more else iter(())

                def ahead(x_):
                    if more:
                        squares_of(U + 1, x_)

                ahead(0)
                scan_in(U, u, 0)
                ahead(1)
                scan(U, 0)
                if splits and u == 3:
                    dve.wait_ge(s_copied, U * NF + NF)
                    split(i + 1, V)
                scan_out(U, 0)
                ahead(2)
                if splits and u == 2:
                    split(i + 1, Q)
                invert_z(U, 0)
                scan_in(U, u, 1)
                norm_o(U, 0)
                scan(U, 1)
                ahead(3)
                run(nf, 1)
                scan_out(U, 1)
                run(nf, 1)
                invert_z(U, 1)
                if splits and u == 2:
                    split(i + 1, K)
                run(nf, 1)
                norm_o(U, 1)
                run(nf, 1)
                scan_in(U, u, 2)
                run(nf, 1)
                scan(U, 2)
                run(nf, 1)
                invert_z(U, 2)
                run(nf, 1)
                scan_out(U, 2)
                run(nf, 1)
                norm_o(U, 2)
                run(nf, 1)
                scan_in(U, u, 3)
                run(nf, 1)
                scan(U, 3)
                run(nf)
                invert_z(U, 3)
                scan_out(U, 3)
                norm_o(U, 3)
                dve.wait_ge(s_turned, U * TURNS + TURNS)
                dve.tensor_tensor(y_acc[:, u].rearrange("p t d -> p (t d)"), y_acc[:, u].rearrange("p t d -> p (t d)"),
                                  turn[(TURNS * u + 6) % 2][:, :], ALU.add).then_inc(s_yadd, 1)

            with dve.Fori(0, GROUPS - 1) as i:
                for u in range(B):
                    unit(i, u, True, True)
            for u in range(B):
                unit(GROUPS - 1, u, u < B - 1, False)

            own = [0]

            def mark(ins):
                own[0] += 1
                ins.then_inc(s_own, 1)

            def seen():
                dve.wait_ge(s_own, own[0])

            def inverse_std(lo, hi):
                n = slice(lo, hi)
                at = own[0]
                steps = chain_steps(lx[:, n], ln_r[:, n], lt[:, n],
                                    lambda: dve.tensor_scalar(lx[:, n], mv[:, n, 1], LN_EPS, None, ALU.add),
                                    ln_r[:, n], s_own, at)
                run(steps)
                own[0] += CHAIN

            def layer_norm(buf, tiles):
                for n in tiles:
                    last = dve.bn_stats(bn[:, n, :], buf[:, n // NT, n % NT, :])
                mark(last)
                seen()
                for n in tiles:
                    last = dve.bn_aggr(mv[:, n, :], bn[:, n, :])
                mark(last)
                seen()
                inverse_std(tiles[0], tiles[-1] + 1)
                seen()

            def normalise(buf, n):
                t = buf[:, n // NT, n % NT, :]
                return dve.tensor_scalar(t, t, mv[:, n, 0:1], ln_r[:, n:n + 1], ALU.subtract, ALU.mult)

            tiles = list(range(B * NT))
            dve.wait_ge(s_xn, 16)
            dve.wait_ge(s_yadd, GROUPS * B + 1)
            for b in range(B):
                last = dve.tensor_tensor(y_acc[:, b], y_acc[:, b], xn[:, b], ALU.add)
            mark(last)
            seen()
            layer_norm(y_acc, tiles)
            for b in range(B):
                normalise(y_acc, 2 * b)
                normalise(y_acc, 2 * b + 1).then_inc(s_mid, 1)
            dve.wait_ge(s_ysum, GROUPS * B * 4 + 2)
            for b in range(B):
                dve.wait_ge(s_tanh, GROUPS * B * 4 + b + 1)
                mark(dve.scalar_tensor_tensor(out=tanh_s[:, b], in0=tanh_s[:, b], scalar=1.0, in1=y_acc[:, b],
                                              op0=ALU.add, op1=ALU.mult))
                seen()
                dve.scalar_tensor_tensor(out=gated[:, b], in0=y_m[:, :, b * T:(b + 1) * T], scalar=0.5, in1=tanh_s[:, b],
                                         op0=ALU.mult, op1=ALU.mult).then_inc(s_gt, 1)
            for b in range(B):
                dve.wait_ge(s_tg, b + 1)
                last = dve.tensor_tensor(xn[:, b], y_acc[:, b], bank[b % 4][:, :].rearrange("p (t d) -> p t d", t=NT), ALU.add)
            mark(last)
            seen()
            layer_norm(xn, tiles)
            for b in range(B):
                normalise(xn, 2 * b)
                normalise(xn, 2 * b + 1).then_inc(s_x2, 1)
            for b in range(B):
                at = slice(b * T, (b + 1) * T)
                dve.wait_ge(s_x2c, b + 1)
                dve.tensor_copy(xhl[:, HI, :, at], x2T[:, :, at]).then_inc(s_xhi, 1)
                dve.wait_ge(s_xhi, 3 + b)
                dve.tensor_tensor(xhl[:, LO, :, at], x2T[:, :, at], xhl[:, HI, :, at].bitcast(F32), ALU.subtract).then_inc(s_x2hl, 1)

            def split_expert(e_plus, p, times):
                dve.wait_ge(s_eraw[p], times * 16)
                dve.tensor_copy(wf_hl[:, HI, p], wf_raw[:, p]).then_inc(s_ehi, 1)
                dve.wait_ge(s_ehi, e_plus)
                dve.tensor_tensor(wf_hl[:, LO, p], wf_raw[:, p], wf_hl[:, HI, p].bitcast(F32), ALU.subtract).then_inc(s_esplit, 1)

            split_expert(1, 0, 1)
            split_expert(2, 1, 1)

            for e in range(E):
                last = dve.memset(rank[:, e:e + 1], float(E - e))
            mark(last)
            dve.wait_ge(s_logit, 1)
            NTL = B * NT

            def wide(col):
                return bcast(col[:, :].rearrange("p (n o) -> p n o", o=1), [P, NTL, E])

            rank_w = bcast(rank[:, :].rearrange("p (o e) -> p o e", o=1), [P, NTL, E])
            AX = mybir.AxisListType.X

            def do(ins):
                mark(ins)
                seen()

            do(dve.tensor_copy(gl[:, :, :], bank[7][:, 0:NTL * E].rearrange("p (n e) -> p n e", e=E)))
            do(dve.tensor_reduce(m1[:, :], gl[:, :, :], AX, ALU.max))
            do(dve.tensor_tensor(g1[:, :, :], gl[:, :, :], wide(m1), ALU.is_equal))
            do(dve.tensor_tensor(g1[:, :, :], g1[:, :, :], rank_w, ALU.mult))
            do(dve.tensor_reduce(mr[:, :], g1[:, :, :], AX, ALU.max))
            do(dve.tensor_tensor(oh1[:, :, :], g1[:, :, :], wide(mr), ALU.is_equal))
            do(dve.scalar_tensor_tensor(out=gl[:, :, :], in0=oh1[:, :, :], scalar=-3.0e38, in1=gl[:, :, :], op0=ALU.mult, op1=ALU.add))
            do(dve.tensor_reduce(m2[:, :], gl[:, :, :], AX, ALU.max))
            do(dve.tensor_tensor(g2[:, :, :], gl[:, :, :], wide(m2), ALU.is_equal))
            dve.tensor_tensor(m2[:, :], m2[:, :], m1[:, :], ALU.subtract).then_inc(s_ge, 1)
            do(dve.tensor_tensor(g2[:, :, :], g2[:, :, :], rank_w, ALU.mult))
            do(dve.tensor_reduce(mr[:, :], g2[:, :, :], AX, ALU.max))
            do(dve.tensor_tensor(g2[:, :, :], g2[:, :, :], wide(mr), ALU.is_equal))
            dve.wait_ge(s_ge, 2)
            do(dve.tensor_scalar(w2[:, :], w1[:, :], 1.0, None, ALU.add))
            do(dve.reciprocal(w2[:, :], w2[:, :]))
            do(dve.tensor_tensor(w1[:, :], w1[:, :], w2[:, :], ALU.mult))
            do(dve.tensor_tensor(g2[:, :, :], g2[:, :, :], wide(w1), ALU.mult))
            do(dve.tensor_tensor(oh1[:, :, :], oh1[:, :, :], wide(w2), ALU.mult))
            mark(dve.tensor_tensor(cwt[:, :, :], oh1[:, :, :], g2[:, :, :], ALU.add))
            seen()
            dve.memset(lt[:, 0:1], 0.0).then_inc(s_outfree, 2)

            def make_h(S, par, m):
                dve.wait_ge(s_sg, S * 2 + (m + 1))
                dve.wait_ge(s_h1, S * 2 + (m + 1))
                dve.tensor_tensor(h32[:, par, m, :], sg[:, m, :], bank[2 * m + 1][:, :], ALU.mult).then_inc(s_h, 1)

            def low(S, par, m):
                dve.wait_ge(s_hhi, S * 2 + (m + 1))
                dve.tensor_tensor(h_hl[par][:, LO, m, :], h32[:, par, m, :], h_hl[par][:, HI, m, :].bitcast(F32),
                                  ALU.subtract).then_inc(s_hlo, 1)

            def add_out(S, half, e):
                for r in range(2):
                    dve.wait_ge(s_out, S * 2 + (r + 1))
                    for t in range(2):
                        n = half * 4 + 2 * r + t
                        acc = xn[:, n // NT, n % NT, :]
                        w = cwt[:, n, ds(e, 1)]
                        last = dve.scalar_tensor_tensor(out=acc, in0=bank[4 + r][:, t * D:(t + 1) * D], scalar=w, in1=acc,
                                                        op0=ALU.mult, op1=ALU.add)
                    last.then_inc(s_outfree, 1)

            def make(S, par):
                make_h(S, par, 0)
                make_h(S, par, 1)
                low(S, par, 0)
                low(S, par, 1)

            make(0, 0)

            def experts_pair(i, last_pair):
                for q in range(4):
                    S = i * 4 + q
                    if not (last_pair and q == 3):
                        make(S + 1, (q + 1) % 2)
                    add_out(S, q % 2, i * 2 + q // 2)
                    if q % 2 == 1 and not last_pair:
                        p = q // 2
                        split_expert(i * 2 + (3 + p), p, i + 2)

            with dve.Fori(0, E // 2 - 1) as i:
                experts_pair(i, False)
            experts_pair(E // 2 - 1, True)

            for half in range(2):
                t4 = tiles[4 * half:4 * half + 4]
                if half == 0:
                    dve.wait_ge(s_outfree, 2 * 2 * E + 2)
                layer_norm(xn, t4)
                for n in t4:
                    last = normalise(xn, n)
                last.then_inc(s_fin, 1)

        @block.gpsimd
        def _(pool):
            pool.memset(ident[:, :], 0.0)
            pool.memset(causal[:, :], 1.0)
            pool.memset(v_s[:, :, :, :, DH:DH + 1], 1.0).then_inc(s_ones, 1)
            pool.wait_ge(s_ones, 1)
            pool.affine_select(out=causal[:, :], in_=causal[:, :], compare_op=ALU.is_ge, fill=0.0, base=0,
                               pattern=[[1, P]], channel_multiplier=-1)
            pool.affine_select(out=ident[:, :], in_=ident[:, :], compare_op=ALU.not_equal, fill=1.0, base=0,
                               pattern=[[-1, P]], channel_multiplier=1).then_inc(s_const, 1)
            pool.wait_ge(s_const, 1)

            def scale_q(U, par, t):
                pool.wait_ge(s_stat, U * CHAIN + CHAIN)
                q = qk[:, 2 * t, :].rearrange("p (h d) -> p h d", h=G)
                f = rs[:, par, 2 * t, :].rearrange("p (h o) -> p h o", o=1)
                pool.tensor_tensor(q, q, bcast(f, [P, G, DH]), ALU.mult).then_inc(s_scaled, 1)

            def mask(U, h):
                pool.wait_ge(s_exp, U * 4 + (h + 1))
                d = pT[:, h, :].rearrange("p (k t) -> p k t", k=3)[:, 0:3:2, :]
                pool.tensor_tensor(d, d, bcast(causal[:, :].rearrange("p (o t) -> p o t", o=1), [P, 2, P]),
                                   ALU.mult).then_inc(s_masked, 1)

            def sum_y(U, u, j):
                pool.wait_ge(s_bcfree, U * 4 + (j + 2))
                pool.wait_ge(s_ysum, U * 4 + (j + 2))
                y = y_m[:, :, u * T:(u + 1) * T]
                pool.tensor_tensor(y, y, hb[:, j % 2], ALU.add).then_inc(s_ysum, 1)

            scale_q(0, 0, 0)
            scale_q(0, 0, 1)
            pool.wait_ge(s_ones, 1)
            pool.memset(pool_mark[:, :], 0.0).then_inc(s_ysum, 2)

            def unit(i, u, more):
                U = i * B + u

                mask(U, 0)
                sum_y(U, u, 0)
                mask(U, 1)
                sum_y(U, u, 1)
                mask(U, 2)
                sum_y(U, u, 2)
                mask(U, 3)
                if more:
                    scale_q(U + 1, (u + 1) % 2, 0)
                    scale_q(U + 1, (u + 1) % 2, 1)
                sum_y(U, u, 3)

            with pool.Fori(0, GROUPS - 1) as i:
                for u in range(B):
                    unit(i, u, True)
            for u in range(B):
                unit(GROUPS - 1, u, u < B - 1)


def kernel(**inputs):
    import concourse.bacc as _bacc
    from concourse.bass_utils import run_bass_kernel_spmd as _run

    a = {k.replace("L0_", ""): np.asarray(v) for k, v in inputs.items()}
    halves = np.concatenate([np.arange(0, DH, 2), np.arange(1, DH, 2)])

    def grouped(w, permute):
        w = w.reshape(GROUPS, G, DH, D)
        if permute:
            w = w[:, :, halves, :]
        return w.transpose(0, 3, 1, 2).reshape(GROUPS, D, GW)

    x2d = a["x"].reshape(N, D)
    arrays = {
        "xT": x2d.T,
        "x": x2d,
        "wqkv": np.stack([grouped(a["attn_wq"], True), grouped(a["attn_wk"], True), grouped(a["attn_wv"], False)], axis=1),
        "woT": a["attn_wo"].T,
        "qw": a["attn_q_norm_w"][halves],
        "kw": a["attn_k_norm_w"][halves],
        "cosT": a["attn_rope_cos"][:HEADS].T,
        "sinT": a["attn_rope_sin"][:HEADS].T,
        "ctxT": a["ctx_1024"].reshape(N, DM).T,
        "in_projT": a["xattn_in_proj_w"].T,
        "channels": np.concatenate([a["xattn_conv_b"][:, None], a["xattn_dt_proj_b"][:, None], a["xattn_D"][:, None],
                                    a["xattn_conv_w"], a["xattn_A_log"]], axis=1),
        "x_projT": a["xattn_x_proj_w"].T,
        "dt_projT": a["xattn_dt_proj_w"].T,
        "gate": a["ffn_gate_kernel"],
        "experts": np.stack([a["ffn_wi_0"], a["ffn_wi_1"], a["ffn_wo"]], axis=1).reshape(E, 3 * D, M),
    }
    nc = _bacc.Bacc("TRN2", target_bir_lowering=False, num_devices=1)
    feeds, args = {}, []
    for name, v in arrays.items():
        v = np.ascontiguousarray(v)
        feeds[f"in_{name}"] = v
        args.append(nc.dram_tensor(f"in_{name}", v.shape, mybir.dt.from_np(v.dtype), kind="ExternalInput").ap())
    out = nc.dram_tensor("out", (N, D), F32, kind="ExternalOutput").ap()
    build(nc, *args, out)
    r = _run(nc, [feeds], core_ids=[0])
    return np.asarray(r.results[0]["out"]).reshape(B, T, D)
```

```python
from contextlib import ExitStack

import numpy as np

import concourse.bass as bass
from concourse import mybir

ALU = mybir.AluOpType
ACT = mybir.ActivationFunctionType
F32 = mybir.dt.float32
F32R = mybir.dt.float32r
I32 = mybir.dt.int32
ds = bass.ds

P = 128
B, T, D = 4, 256, 256
N = B * T
NT = T // P
KD = D // P
HEADS, DH = 16, 128
G = 4
GROUPS = HEADS // G
GW = G * DH
DM, DI, DS, DC, DR = 128, 256, 16, 4, 8
NC = DI // P
E, M = 8, 256
KM = M // P
CAP = 50.0
RMS_EPS, LN_EPS = 1e-6, 1e-5
CAP_SCALE = DH ** -0.5 / CAP
MAGIC = float(0x5F3759DF)
HI, LO = 0, 1
K, Q, V = 0, 1, 2
FILLS = [(K, 0), (Q, 0), (K, 1), (Q, 1), (V, 0), (V, 1)]
NF = len(FILLS)
K_TURN, O_TURN, Q_TURN, Y_TURN, TURNS, EVACS, FIRST = 0, 2, 4, 6, 7, 6, 4
NEWTON = 3
CHAIN = 3 + 3 * NEWTON


def build(nc, xT, x, wkqv, woT, qw, kw, cosT, sinT, ctxT, in_projT, channels, x_projT,
          dt_projT, gate, experts, out):
    with ExitStack() as ctx:
        def sb(name, shape, dt=F32):
            return ctx.enter_context(nc.sbuf_tensor(name, shape, dt))

        def sem(name):
            return ctx.enter_context(nc.semaphore(name))

        bank = [ctx.enter_context(nc.psum_tensor(f"bank{i}", [P, 512], F32)) for i in range(8)]
        proj, turn, score = bank[0:2], bank[2:4], bank[4:6]
        pv_bank, bc_bank = bank[6], bank[7]

        ident = sb("ident", [P, P])
        causal = sb("causal", [P, P])
        cos_s = sb("cos_s", [P, HEADS])
        sin_s = sb("sin_s", [P, HEADS])
        norm_w = sb("norm_w", [P, 2])
        f_s = sb("f_s", [P, HEADS])
        f_cur = sb("f_cur", [P, G])
        xhl = sb("xhl", [P, 2, KD, N], F32R)
        wraw = sb("wraw", [P, 3 * KD * GW])
        whl = sb("whl", [P, 2, 3 * KD * GW], F32R)
        wo_s = sb("wo_s", [P, HEADS, D])
        qk = sb("qk", [P, 4, GW])
        squares = sb("squares", [P, GW])
        ss = sb("ss", [P, 4, G])
        nx = sb("nx", [P, 4, G])
        ny = sb("ny", [P, 4, G])
        nt = sb("nt", [P, 4, G])
        rs = sb("rs", [P, 2, 4, G])
        qT = sb("qT", [P, G, T])
        kT = sb("kT", [P, G, T])
        v_s = sb("v_s", [P, 2, NT, G, DH + 1])
        pT = sb("pT", [P, G, 3 * P])
        rz = sb("rz", [P, 2, NT])
        o_s = sb("o_s", [P, NT, GW])
        oT = sb("oT", [P, G, T])
        y_acc = sb("y_acc", [P, B, NT, D])
        xn = sb("xn", [P, B, NT, D])
        ctx_s = sb("ctx_s", [P, N])
        in_w = sb("in_w", [P, DI])
        xp_w = sb("xp_w", [P, NC, P])
        dt_w = sb("dt_w", [P, DI])
        chan = sb("chan", [P, NC, 3 + DC + DS])
        cb_s, db_s, dsk_s = chan[:, :, 0], chan[:, :, 1], chan[:, :, 2]
        cw_s, al_s = chan[:, :, 3:3 + DC], chan[:, :, 3 + DC:3 + DC + DS]
        a_s = sb("a_s", [P, NC, DS])
        u_s = sb("u_s", [P, NC, N])
        delta = sb("delta", [P, NC, N])
        du = sb("du", [P, NC, N])
        y_m = sb("y_m", [P, NC, N])
        xd_hl = sb("xd_hl", [P, 2, N], F32R)
        sel = sb("sel", [P, 2 * G], F32R)
        a_cur = sb("a_cur", [P, NC, G])
        dA = sb("dA", [P, 2, NC, T])
        hb = sb("hb", [P, 2, NC, T])
        gate_s = sb("gate_s", [P, KD, E])
        bn = sb("bn", [P, B * NT, 6])
        mv = sb("mv", [P, B * NT, 2])
        ln_r = sb("ln_r", [P, B * NT])
        lx = sb("lx", [P, B * NT])
        lt = sb("lt", [P, B * NT])
        gl = sb("gl", [P, B * NT, E])
        rank = sb("rank", [P, E])
        g1 = sb("g1", [P, B * NT, E])
        g2 = sb("g2", [P, B * NT, E])
        oh1 = sb("oh1", [P, B * NT, E])
        cwt = sb("cwt", [P, B * NT, E])
        m1 = sb("m1", [P, B * NT])
        m2 = sb("m2", [P, B * NT])
        mr = sb("mr", [P, B * NT])
        w1 = sb("w1", [P, B * NT])
        w2 = sb("w2", [P, B * NT])
        pool_mark = sb("pool_mark", [P, 1])
        h_odd = sb("h_odd", [P, 2, KM, 512], F32R)

        xT_raw = qk[:, :, :].rearrange("p a b -> p (a b)").rearrange("p (k n) -> p k n", k=KD)
        xd_s = pT[:, :, :].rearrange("p a b -> p (a b)")[:, 0:N]
        one_p = xn[:, :, :, :].rearrange("p b t d -> p (b t d)").rearrange("p (c n) -> p c n", c=NC)
        wq_raw = wraw[:, :].rearrange("p (x k n) -> p x k n", x=3, k=KD)
        wq_hl = whl[:, :, :].rearrange("p h (x k n) -> p h x k n", x=3, k=KD)
        wf_raw = wraw[:, :].rearrange("p (s m k n) -> p s m k n", s=2, m=3, k=KD)
        wf_hl = whl[:, :, :].rearrange("p h (s m k n) -> p h s m k n", s=2, m=3, k=KD)
        x2T = u_s
        tanh_s = delta[:, :, :].rearrange("p c n -> p (c n)").rearrange("p (b t d) -> p b t d", b=B, t=NT)
        gated = du[:, :, :].rearrange("p c n -> p (c n)").rearrange("p (b c l) -> p b c l", b=B, c=NC)
        sg = dA[:, :, :, :].rearrange("p s c t -> p s (c t)")
        h_hl = [xd_hl[:, :, :].rearrange("p h (m n) -> p h m n", m=KM), h_odd[:, :, :, :]]
        h32 = qk[:, :, :].rearrange("p (r m) n -> p r m n", r=2)

        s_zeroed, s_ctx, s_small, s_x, s_tab, s_wo = (sem(n) for n in (
            "zeroed", "ctx_loaded", "small_loaded", "x_loaded", "tables_loaded", "wo_loaded"))
        s_wraw = [sem(f"raw_loaded{x}") for x in range(3)]
        s_xn = sem("xn_loaded")
        s_eraw = [sem(f"expert_loaded{p}") for p in range(2)]
        s_const, s_ones = sem("constants_made"), sem("ones_made")
        s_inproj, s_conv, s_u, s_xdbl, s_xds, s_xdhl = (sem(n) for n in (
            "inproj_done", "conv_tap", "u_ready", "xdbl_done", "xdbl_copied", "xdbl_split"))
        s_dt, s_soft_a, s_soft_d, s_du, s_ready = (sem(n) for n in (
            "dt_done", "softplus_act", "softplus_dve", "du_ready", "a_ready"))
        s_xhi, s_xsplit, s_fac = sem("x_high"), sem("x_split"), sem("factors")
        s_whi, s_split = sem("w_high"), [sem(f"w_split{x}") for x in range(3)]
        s_proj, s_copied, s_squared, s_stat, s_scaled = (sem(n) for n in (
            "projected", "proj_copied", "squared", "norm_step", "q_scaled"))
        s_turned, s_evac, s_yadd, s_scores, s_tanh, s_exp, s_masked = (sem(n) for n in (
            "turned", "turn_copied", "y_added", "scored", "tanh_done", "exp_done", "masked"))
        s_pv, s_rz, s_onorm = sem("pv_done"), sem("z_inverted"), sem("o_normed")
        s_fcur = sem("score_factors")
        s_cur, s_bc, s_bcfree, s_dA, s_dbu, s_scan, s_ysum = (sem(n) for n in (
            "group_columns", "bc_spread", "bc_used", "dA_ready", "dbu_ready", "scanned", "y_summed"))
        s_mid, s_tg, s_gt, s_x2, s_x2T, s_x2c, s_logit, s_ge = (sem(n) for n in (
            "mid_step", "tanh_gate", "gated_turned", "x2_ready", "x2_turned", "x2_copied", "logits", "gate_exp"))
        s_x2hl, s_ehi, s_esplit = sem("x2_split"), sem("expert_high"), sem("expert_split")
        s_h0, s_h1, s_sg, s_h, s_hhi, s_hlo, s_out, s_outfree = (sem(n) for n in (
            "h0_done", "h1_done", "silu_done", "h_ready", "h_high", "h_low", "out_done", "out_added"))
        s_store, s_fin, s_own = sem("stored"), sem("normed"), sem("dve_step")

        block = ctx.enter_context(nc.Block())

        def bcast(ap, shape):
            return ap.broadcast_to(shape)

        @block.sync
        def _(sp):
            sp.dma_start(ctx_s[:, :], ctxT).then_inc(s_ctx, 16)
            sp.dma_start(in_w[:, :], in_projT).then_inc(s_small, 16)
            sp.dma_start(chan[:, :, :], channels.rearrange("(c p) n -> p c n", p=P)).then_inc(s_small, 16)
            sp.wait_ge(s_zeroed, 1)
            sp.dma_start(xp_w[:, :, 0:DR + 2 * DS], x_projT.rearrange("(c p) n -> p c n", p=P)).then_inc(s_small, 16)
            sp.dma_start(dt_w[0:DR, :], dt_projT).then_inc(s_small, 16)
            sp.dma_start(xT_raw, xT.rearrange("(k p) n -> p k n", p=P)).then_inc(s_x, 16)
            for x_ in range(3):
                sp.dma_start(wq_raw[:, x_], wkqv[0, x_].rearrange("(k p) n -> p k n", p=P)).then_inc(s_wraw[x_], 16)
            for half in range(2):
                sp.dma_start(cos_s[half * 64:half * 64 + 64, :], cosT).then_inc(s_tab, 16)
                sp.dma_start(sin_s[half * 64:half * 64 + 64, :], sinT).then_inc(s_tab, 16)
            sp.dma_start(norm_w[:, 0:1], qw.rearrange("(n o) -> n o", o=1)).then_inc(s_tab, 16)
            sp.dma_start(norm_w[:, 1:2], kw.rearrange("(n o) -> n o", o=1)).then_inc(s_tab, 16)
            sp.dma_start(wo_s[:, :, :], woT.rearrange("(h p) n -> p h n", p=P)).then_inc(s_wo, 16)
            sp.dma_start(gate_s[:, :, :], gate.rearrange("(k p) n -> p k n", p=P)).then_inc(s_wo, 16)
            with sp.Fori(0, GROUPS - 1) as i:
                for x_ in range(3):
                    sp.wait_ge(s_split[x_], i + 1)
                    src = wkqv[ds(i + 1, 1), x_].rearrange("o (k p) n -> p (o k) n", p=P)
                    sp.dma_start(wq_raw[:, x_], src).then_inc(s_wraw[x_], 16)
            sp.wait_ge(s_soft_d, 10)
            sp.dma_start(xn[:, :, :, :], x.rearrange("(b t p) d -> p b t d", p=P, t=NT)).then_inc(s_xn, 16)
            for x_ in range(3):
                sp.wait_ge(s_split[x_], GROUPS)
            for e in range(2):
                sp.dma_start(wf_raw[:, e].rearrange("p m k n -> p (m k) n"),
                             experts[e].rearrange("(a p) n -> p a n", p=P)).then_inc(s_eraw[e], 16)
            with sp.Fori(0, E // 2 - 1) as i:
                for p in range(2):
                    sp.wait_ge(s_esplit, i * 2 + (p + 1))
                    src = experts[ds(i * 2 + (2 + p), 1)].rearrange("o (a p) n -> p (o a) n", p=P)
                    sp.dma_start(wf_raw[:, p].rearrange("p m k n -> p (m k) n"), src).then_inc(s_eraw[p], 16)
            for half in range(2):
                sp.wait_ge(s_fin, half + 1)
                sp.dma_start(out.rearrange("(b t p) d -> p b t d", p=P, t=NT)[:, 2 * half:2 * half + 2],
                             xn[:, 2 * half:2 * half + 2]).then_inc(s_store, 16)
            sp.wait_ge(s_store, 32)

        @block.tensor
        def _(pe):
            def three_pass(dst, pairs):
                for n, (s, m) in enumerate(pairs):
                    pe.matmul(dst, s[HI], m[HI], start=n == 0, stop=False)
                    pe.matmul(dst, s[HI], m[LO], start=False, stop=False)
                    last = pe.matmul(dst, s[LO], m[HI], start=False, stop=n == len(pairs) - 1)
                return last

            def fill(U, b, f, first_of_group=None):
                part, t = FILLS[f]
                if isinstance(U, int) and U == 0:
                    if f >= 2:
                        pe.wait_ge(s_copied, f - 1)
                else:
                    pe.wait_ge(s_copied, U * NF + (f - 1))
                if first_of_group is not None:
                    pe.wait_ge(s_split[part], first_of_group + 1)
                at = b * T + t * P
                pairs = [((xhl[:, HI, k, at:at + P], xhl[:, LO, k, at:at + P]),
                          (wq_hl[:, HI, part, k, :], wq_hl[:, LO, part, k, :])) for k in range(KD)]
                three_pass(proj[f % 2][:, :], pairs).then_inc(s_proj, 1)

            pe.wait_ge(s_ctx, 16)
            pe.wait_ge(s_small, 16 * 4)
            for half in range(2):
                for c in range(NC):
                    pe.matmul(bank[2 + 2 * half + c][:, :], in_w[:, c * P:(c + 1) * P],
                              ctx_s[:, half * 512:(half + 1) * 512], start=True, stop=True).then_inc(s_inproj, 1)
            pe.wait_ge(s_xsplit, 1)
            fill(0, 0, 0, 0)
            fill(0, 0, 1, 0)
            for half in range(2):
                pe.wait_ge(s_u, 2 * half + 2)
                for c in range(NC):
                    last = pe.matmul(bank[6 + half][:, :], xp_w[:, c, :], u_s[:, c, half * 512:(half + 1) * 512],
                                     start=c == 0, stop=c == NC - 1)
                last.then_inc(s_xdbl, 1)
            fill(0, 0, 2)
            fill(0, 0, 3)
            for c in range(NC):
                for half in range(2):
                    pe.wait_ge(s_xds, half + 1)
                    pe.matmul(bank[2 + 2 * c + half][:, :], dt_w[:, c * P:(c + 1) * P],
                              xd_s[:, half * 512:(half + 1) * 512], start=True, stop=True).then_inc(s_dt, 1)
            fill(0, 0, 4, 0)
            fill(0, 0, 5)

            def turns(n, src):
                for h in range(G):
                    last = pe.transpose(turn[n % 2][:, h * P:(h + 1) * P], src[:, h * DH:(h + 1) * DH], ident[:, :])
                last.then_inc(s_turned, 1)

            def turn_k(V_, t, n):
                pe.wait_ge(s_copied, V_ * NF + (2 * t + 1))
                turns(n, qk[:, 2 * t])

            def turn_q(V_, t, n):
                pe.wait_ge(s_scaled, V_ * 2 + (t + 1))
                turns(n, qk[:, 2 * t + 1])

            def scores(U, h):
                if h == 0:
                    pe.wait_ge(s_evac, U * EVACS + FIRST)
                if h >= 2:
                    pe.wait_ge(s_tanh, U * 4 + (h - 1))
                pe.matmul(score[h % 2][:, 0:T], kT[:, h, 0:P], qT[:, h, :], start=True, stop=True)
                pe.matmul(score[h % 2][:, T:T + P], kT[:, h, P:T], qT[:, h, P:T],
                          start=True, stop=True).then_inc(s_scores, 1)

            def values(U, u, h):
                pe.wait_ge(s_masked, U * 4 + (h + 1))
                if h == 0:
                    pe.wait_ge(s_copied, U * NF + NF)
                else:
                    pe.wait_ge(s_onorm, U * 4 + h)
                W = DH + 1
                pe.matmul(pv_bank[:, 0:W], pT[:, h, 0:P], v_s[:, u % 2, 0, h, :], start=True, stop=True)
                pe.matmul(pv_bank[:, T:T + W], pT[:, h, P:2 * P], v_s[:, u % 2, 0, h, :], start=True, stop=False)
                pe.matmul(pv_bank[:, T:T + W], pT[:, h, 2 * P:3 * P], v_s[:, u % 2, 1, h, :],
                          start=False, stop=True).then_inc(s_pv, 1)

            def spread(U, i, u, j):
                if u == 0 and j == 0:
                    pe.wait_ge(s_cur, i + 1)
                pe.wait_ge(s_bcfree, U * 4 + (j + 1))
                for s in range(2):
                    one_hot = bcast(sel[:, s * G + j:s * G + j + 1], [P, P])
                    for part in (HI, LO):
                        last = pe.matmul(bc_bank[:, s * T:(s + 1) * T], one_hot, xd_hl[:, part, u * T:(u + 1) * T],
                                         start=part == HI, stop=part == LO)
                last.then_inc(s_bc, 1)

            def turn_o(U, t, n):
                if t == 0:
                    pe.wait_ge(s_onorm, U * 4 + G)
                turns(n, o_s[:, t])

            def project_out(i, n):
                for t in range(NT):
                    for h in range(G):
                        w = wo_s[:, ds(i * G + h, 1), :].rearrange("p o n -> p (o n)")
                        last = pe.matmul(turn[n % 2][:, t * D:(t + 1) * D], oT[:, h, t * P:(t + 1) * P], w,
                                         start=h == 0, stop=h == G - 1)
                last.then_inc(s_turned, 1)

            def unit(i, u, after, after2):
                U = i * B + u
                first, second = (i + 1 if u == B - 1 else None), (i + 1 if u == B - 2 else None)
                n0 = TURNS * u
                evacs = U * EVACS + FIRST

                def ahead(f):
                    if f >= 2 and after:
                        fill(U + 1, (u + 1) % B, f, first if f == 4 else None)
                    if f < 2 and after2:
                        fill(U + 2, (u + 2) % B, f, second)

                spread(U, i, u, 0)
                scores(U, 0)
                scores(U, 1)
                ahead(2)
                scores(U, 2)
                values(U, u, 0)
                ahead(3)
                spread(U, i, u, 1)
                scores(U, 3)
                values(U, u, 1)
                ahead(4)
                values(U, u, 2)
                if after:
                    pe.wait_ge(s_evac, evacs)
                    turn_k(U + 1, 0, n0 + K_TURN)
                    pe.wait_ge(s_yadd, U + 1)
                    turn_k(U + 1, 1, n0 + K_TURN + 1)
                ahead(5)
                values(U, u, 3)
                spread(U, i, u, 2)
                ahead(0)
                if after:
                    pe.wait_ge(s_evac, evacs + (K_TURN + 1))
                    turn_o(U, 0, n0 + O_TURN)
                    pe.wait_ge(s_evac, evacs + (K_TURN + 2))
                    turn_o(U, 1, n0 + O_TURN + 1)
                else:
                    turn_o(U, 0, n0)
                    pe.wait_ge(s_yadd, U + 1)
                    turn_o(U, 1, n0 + 1)
                ahead(1)
                if after:
                    for t in range(NT):
                        pe.wait_ge(s_evac, evacs + (O_TURN + t + 1))
                        turn_q(U + 1, t, n0 + Q_TURN + t)
                spread(U, i, u, 3)
                if after:
                    pe.wait_ge(s_evac, evacs + (Q_TURN + 1))
                    project_out(i, n0 + Y_TURN)
                else:
                    pe.wait_ge(s_evac, evacs + 2)
                    project_out(i, n0 + 2)

            pe.wait_ge(s_copied, NF)
            pe.wait_ge(s_const, 1)
            turn_k(0, 0, 0)
            turn_k(0, 1, 1)
            fill(1, 1, 0)
            for t in range(NT):
                pe.wait_ge(s_evac, t + 1)
                turn_q(0, t, t)
            fill(1, 1, 1)
            pe.wait_ge(s_xdhl, 1)
            pe.wait_ge(s_wo, 32)
            with pe.Fori(0, GROUPS - 1) as i:
                for u in range(B):
                    unit(i, u, True, True)
            for u in range(B):
                unit(GROUPS - 1, u, u < B - 1, u < B - 2)

            for b in range(B):
                pe.wait_ge(s_gt, b + 1)
                for l in range(NT):
                    for c in range(NC):
                        last = pe.transpose(bank[b % 4][:, l * DI + c * P:l * DI + (c + 1) * P],
                                            gated[:, b, c, l * P:(l + 1) * P], ident[:, :])
                last.then_inc(s_tg, 1)
            for b in range(B):
                pe.wait_ge(s_x2, b + 1)
                for k in range(KD):
                    for t in range(NT):
                        last = pe.transpose(bank[b % 4][:, k * T + t * P:k * T + (t + 1) * P],
                                            xn[:, b, t, k * P:(k + 1) * P], ident[:, :])
                last.then_inc(s_x2T, 1)
            for b in range(B):
                pe.wait_ge(s_x2c, b + 1)
                for t in range(NT):
                    at = b * T + t * P
                    for k in range(KD):
                        last = pe.matmul(bank[7][:, (b * NT + t) * E:(b * NT + t + 1) * E], x2T[:, k, at:at + P],
                                         gate_s[:, k, :], start=k == 0, stop=k == KD - 1)
            last.then_inc(s_logit, 1)

            def hidden(S, e, slot, half):
                if half == 0:
                    pe.wait_ge(s_esplit, e + 1)
                for m in range(KM):
                    if not (isinstance(S, int) and S == 0):
                        pe.wait_ge(s_h, S * 2 + (m - 1))
                    for w, s_done in ((0, s_h0), (1, s_h1)):
                        pairs = [((wf_hl[:, HI, slot, w, k, m * P:(m + 1) * P], wf_hl[:, LO, slot, w, k, m * P:(m + 1) * P]),
                                  (xhl[:, HI, k, half * 512:(half + 1) * 512], xhl[:, LO, k, half * 512:(half + 1) * 512]))
                                 for k in range(KD)]
                        three_pass(bank[2 * m + w][:, :], pairs).then_inc(s_done, 1)

            def down(S, slot, par):
                pe.wait_ge(s_hlo, S * 2 + 2)
                for r in range(2):
                    pe.wait_ge(s_outfree, S * 2 + (r + 1))
                    for t in range(2):
                        at = (2 * r + t) * P
                        pairs = [((h_hl[par][:, HI, m, at:at + P], h_hl[par][:, LO, m, at:at + P]),
                                  (wf_hl[:, HI, slot, 2, m, :], wf_hl[:, LO, slot, 2, m, :])) for m in range(KM)]
                        last = three_pass(bank[4 + r][:, t * D:(t + 1) * D], pairs)
                    last.then_inc(s_out, 1)

            pe.wait_ge(s_x2hl, B)
            hidden(0, 0, 0, 0)

            def experts_pair(i, last_pair):
                for q in range(4):
                    S = i * 4 + q
                    if not (last_pair and q == 3):
                        nq = (q + 1) % 4
                        e = i * 2 + ((q + 1) // 2)
                        hidden(S + 1, e, nq // 2, nq % 2)
                    down(S, q // 2, q % 2)

            with pe.Fori(0, E // 2 - 1) as i:
                experts_pair(i, False)
            experts_pair(E // 2 - 1, True)

        @block.scalar
        def _(act):
            def copy_proj(U, par, f):
                part, t = FILLS[f]
                act.wait_ge(s_proj, U * NF + (f + 1))
                if part == V:
                    act.activation(v_s[:, par, t, :, 0:DH], proj[f % 2][:, :].rearrange("p (h d) -> p h d", h=G),
                                   ACT.Copy).then_inc(s_copied, 1)
                else:
                    if isinstance(U, int) and U == 0:
                        act.wait_ge(s_xsplit, 1)
                    else:
                        act.wait_ge(s_squared, U * 4 + (f - 3))
                    act.activation(qk[:, f, :], proj[f % 2][:, :], ACT.Copy).then_inc(s_copied, 1)

            for half in range(2):
                for c in range(NC):
                    act.wait_ge(s_conv, (DC - 1) * 4 + 2 * half + c + 1)
                    act.activation(u_s[:, c, half * 512:(half + 1) * 512], y_m[:, c, half * 512:(half + 1) * 512],
                                   ACT.Silu, bias=cb_s[:, c:c + 1]).then_inc(s_u, 1)
            copy_proj(0, 0, 0)
            copy_proj(0, 0, 1)
            for half in range(2):
                act.wait_ge(s_xdbl, half + 1)
                act.activation(xd_s[:, half * 512:(half + 1) * 512], bank[6 + half][:, :], ACT.Copy).then_inc(s_xds, 1)
            act.activation(a_s[:, :, :], al_s[:, :, :], ACT.Exp).then_inc(s_ready, 1)
            copy_proj(0, 0, 2)
            copy_proj(0, 0, 3)
            for c in range(NC):
                for half in range(2):
                    z = bank[2 + 2 * c + half][:, :]
                    at = slice(half * 512, (half + 1) * 512)
                    act.wait_ge(s_dt, 2 * c + half + 1)
                    act.activation(du[:, c, at], z, ACT.Abs, bias=db_s[:, c:c + 1])
                    act.activation(y_m[:, c, at], z, ACT.Relu, bias=db_s[:, c:c + 1]).then_inc(s_soft_a, 1)
            for c in range(NC):
                act.wait_ge(s_soft_a, 2 * c + 2)
                act.activation(delta[:, c, :], du[:, c, :], ACT.Exp, scale=-1.0).then_inc(s_soft_a, 1)
            copy_proj(0, 0, 4)
            copy_proj(0, 0, 5)
            for c in range(NC):
                act.wait_ge(s_soft_d, c + 1)
                act.wait_ge(s_soft_a, 2 * NC + c + 1)
                act.activation(du[:, c, :], one_p[:, c, :], ACT.Ln).then_inc(s_soft_a, 1)

            def turned(n, count):
                act.wait_ge(s_turned, count + 1)
                return turn[n % 2][:, :].rearrange("p (h t) -> p h t", h=G)

            def copy_turned(dst, t, n, count):
                act.activation(dst[:, :, t * P:(t + 1) * P], turned(n, count), ACT.Copy).then_inc(s_evac, 1)

            def copy_k(t, n, count):
                src = turned(n, count)
                for h in range(G):
                    last = act.activation(kT[:, h, t * P:(t + 1) * P], src[:, h, :], ACT.Copy, scale=f_cur[:, h:h + 1])
                last.then_inc(s_evac, 1)

            def softcap(U, u, h):
                act.wait_ge(s_scores, U * 4 + (h + 1))
                act.activation(pT[:, h, 0:T], score[h % 2][:, 0:T], ACT.Tanh, scale=rs[:, u % 2, 0, h:h + 1])
                act.activation(pT[:, h, T:T + P], score[h % 2][:, T:T + P], ACT.Tanh,
                               scale=rs[:, u % 2, 2, h:h + 1]).then_inc(s_tanh, 1)

            def exps(U, h):
                act.wait_ge(s_tanh, U * 4 + (h + 1))
                act.activation(pT[:, h, :], pT[:, h, :], ACT.Exp, scale=CAP).then_inc(s_exp, 1)

            def decay(U, u, j):
                act.wait_ge(s_scan, U * 4 + (j + 1))
                for c in range(NC):
                    last = act.activation(dA[:, j % 2, c, :], delta[:, c, u * T:(u + 1) * T], ACT.Exp,
                                          scale=a_cur[:, c, j:j + 1])
                last.then_inc(s_dA, 1)

            def unit(i, u, after, after2):
                U = i * B + u
                n0, count = TURNS * u, U * TURNS + FIRST

                def ahead(f):
                    if f >= 2 and after:
                        copy_proj(U + 1, (u + 1) % 2, f)
                    if f < 2 and after2:
                        copy_proj(U + 2, u % 2, f)

                softcap(U, u, 0)
                exps(U, 0)
                softcap(U, u, 1)
                exps(U, 1)
                ahead(2)
                softcap(U, u, 2)
                exps(U, 2)
                ahead(3)
                decay(U, u, 1)
                softcap(U, u, 3)
                exps(U, 3)
                ahead(4)
                if after:
                    if u == B - 1:
                        act.wait_ge(s_fcur, i + 2)
                    copy_k(0, n0 + K_TURN, count + K_TURN)
                    copy_k(1, n0 + K_TURN + 1, count + (K_TURN + 1))
                decay(U, u, 2)
                ahead(5)
                decay(U, u, 3)
                ahead(0)
                for t in range(NT):
                    k = (O_TURN if after else 0) + t
                    copy_turned(oT, t, n0 + k, count + k)
                if after:
                    for t in range(NT):
                        copy_turned(qT, t, n0 + Q_TURN + t, count + (Q_TURN + t))
                ahead(1)
                if after:
                    if u == B - 1:
                        act.wait_ge(s_cur, i + 2)
                    decay(U + 1, (u + 1) % B, 0)

            act.wait_ge(s_fcur, 1)
            for t in range(NT):
                copy_k(t, t, t)
            copy_proj(1, 1, 0)
            for t in range(NT):
                copy_turned(qT, t, t, NT + t)
            copy_proj(1, 1, 1)
            act.wait_ge(s_du, 1)
            act.wait_ge(s_cur, 1)
            decay(0, 0, 0)
            with act.Fori(0, GROUPS - 1) as i:
                for u in range(B):
                    unit(i, u, True, True)
            for u in range(B):
                unit(GROUPS - 1, u, u < B - 1, u < B - 2)

            for b in range(B):
                act.wait_ge(s_mid, b + 1)
                act.activation(tanh_s[:, b], y_acc[:, b], ACT.Tanh, scale=0.5).then_inc(s_tanh, 1)
            for b in range(B):
                act.wait_ge(s_x2T, b + 1)
                act.activation(x2T[:, :, b * T:(b + 1) * T], bank[b % 4][:, :].rearrange("p (k t) -> p k t", k=KD),
                               ACT.Copy).then_inc(s_x2c, 1)
            act.wait_ge(s_ge, 1)
            act.activation(w1[:, :], m2[:, :], ACT.Exp).then_inc(s_ge, 1)

            def silu(S, m):
                act.wait_ge(s_h0, S * 2 + (m + 1))
                act.activation(sg[:, m, :], bank[2 * m][:, :], ACT.Silu).then_inc(s_sg, 1)

            def high(S, par, m):
                act.wait_ge(s_h, S * 2 + (m + 1))
                act.activation(h_hl[par][:, HI, m, :], h32[:, par, m, :], ACT.Copy).then_inc(s_hhi, 1)

            def step(S, par):
                silu(S, 0)
                silu(S, 1)
                high(S, par, 0)
                high(S, par, 1)

            with act.Fori(0, E // 2) as i:
                for q in range(4):
                    step(i * 4 + q, q % 2)

        @block.vector
        def _(dve):
            dve.memset(xp_w[:, :, :], 0.0)
            dve.memset(dt_w[:, :], 0.0).then_inc(s_zeroed, 1)
            dve.memset(y_acc[:, :, :, :], 0.0).then_inc(s_yadd, 1)
            dve.memset(rz[:, :, :], 0.0).then_inc(s_scan, 2)

            dve.wait_ge(s_small, 16 * 4)
            for tap in range(DC):
                back = tap
                for n in range(4):
                    half, c = n // 2, n % 2
                    src = bank[2 + n][:, :].rearrange("p (b t) -> p b t", b=2)[:, :, 0:T - back]
                    acc = y_m[:, c, half * 512:(half + 1) * 512].rearrange("p (b t) -> p b t", b=2)[:, :, back:T]
                    w = cw_s[:, c, DC - 1 - back:DC - back]
                    if tap == 0:
                        dve.wait_ge(s_inproj, n + 1)
                        dve.tensor_scalar(acc, src, w, None, ALU.mult).then_inc(s_conv, 1)
                    else:
                        dve.wait_ge(s_conv, (tap - 1) * 4 + n + 1)
                        dve.scalar_tensor_tensor(out=acc, in0=src, scalar=w, in1=acc, op0=ALU.mult,
                                                 op1=ALU.add).then_inc(s_conv, 1)

            dve.wait_ge(s_x, 16)
            dve.tensor_copy(xhl[:, HI], xT_raw).then_inc(s_xhi, 1)
            dve.wait_ge(s_xhi, 1)
            dve.tensor_tensor(xhl[:, LO], xT_raw, xhl[:, HI].bitcast(F32), ALU.subtract).then_inc(s_xsplit, 1)

            def split_high(i, part):
                dve.wait_ge(s_wraw[part], i * 16 + 16)
                dve.tensor_copy(wq_hl[:, HI, part], wq_raw[:, part]).then_inc(s_whi, 1)

            def split(i, part):
                split_high(i, part)
                dve.wait_ge(s_whi, i * 3 + (part + 1))
                dve.tensor_tensor(wq_hl[:, LO, part], wq_raw[:, part], wq_hl[:, HI, part].bitcast(F32),
                                  ALU.subtract).then_inc(s_split[part], 1)

            for part in (K, Q, V):
                split(0, part)

            dve.wait_ge(s_tab, 96)
            dve.tensor_tensor(cos_s[:, :], cos_s[:, :], cos_s[:, :], ALU.mult)
            dve.tensor_tensor(sin_s[:, :], sin_s[:, :], sin_s[:, :], ALU.mult).then_inc(s_fac, 1)
            dve.wait_ge(s_fac, 1)
            dve.tensor_tensor(f_s[:, :], cos_s[:, :], sin_s[:, :], ALU.add).then_inc(s_fac, 1)
            dve.wait_ge(s_fac, 2)
            dve.tensor_scalar(f_s[:, :], f_s[:, :], norm_w[:, 0:1], norm_w[:, 1:2], ALU.mult, ALU.mult).then_inc(s_fac, 1)

            def squares_of(U, x_):
                dve.wait_ge(s_copied, U * NF + (x_ + 1))
                if not (isinstance(U, int) and U == 0 and x_ == 0):
                    dve.wait_ge(s_squared, U * 4 + x_)
                for h in range(G):
                    col = qk[:, x_, h * DH:(h + 1) * DH]
                    last = dve.tensor_tensor_reduce(squares[:, h * DH:(h + 1) * DH], col, col, 1.0, 0.0, ALU.mult, ALU.add, ss[:, x_, h:h + 1])
                last.then_inc(s_squared, 1)

            def chain_steps(x, y, t, first, final, s, at):
                steps = [first]
                steps.append(lambda: dve.tensor_scalar(t.bitcast(I32), x.bitcast(I32), 1, None, ALU.logical_shift_right))
                steps.append(lambda: dve.tensor_scalar(y.bitcast(I32), t.bitcast(I32), -1.0, MAGIC, ALU.mult, ALU.add))
                for k in range(NEWTON):
                    dst = final if k == NEWTON - 1 else y
                    steps.append(lambda: dve.tensor_tensor(t, y, y, ALU.mult))
                    steps.append(lambda: dve.scalar_tensor_tensor(out=t, in0=t, scalar=-0.5, in1=x, op0=ALU.mult, op1=ALU.mult))
                    steps.append(lambda dst=dst: dve.scalar_tensor_tensor(out=dst, in0=t, scalar=1.5, in1=y, op0=ALU.add, op1=ALU.mult))
                for n, make in enumerate(steps):
                    if n:
                        dve.wait_ge(s, at + n)
                    make().then_inc(s, 1)
                    yield

            def norm_factors(U, par):
                c2 = CAP_SCALE ** 2

                def first():
                    dve.wait_ge(s_squared, U * 4 + 4)
                    dve.tensor_scalar(nx[:, 1::2, :], ss[:, 1::2, :], 1.0 / DH, RMS_EPS, ALU.mult, ALU.add)
                    return dve.tensor_scalar(nx[:, 0::2, :], ss[:, 0::2, :], 1.0 / (DH * c2), RMS_EPS / c2, ALU.mult, ALU.add)
                return chain_steps(nx[:, :, :], ny[:, :, :], nt[:, :, :], first, rs[:, par], s_stat, U * CHAIN)

            def run(steps, n=CHAIN):
                for _ in range(n):
                    next(steps, None)

            def soft_one(c):
                dve.wait_ge(s_soft_a, 2 * NC + c + 1)
                dve.tensor_scalar(one_p[:, c, :], delta[:, c, :], 1.0, None, ALU.add).then_inc(s_soft_d, 1)

            dve.wait_ge(s_xds, 2)
            dve.tensor_copy(xd_hl[:, HI, :], xd_s).then_inc(s_xhi, 1)
            dve.wait_ge(s_xhi, 2)
            dve.tensor_tensor(xd_hl[:, LO, :], xd_s, xd_hl[:, HI, :].bitcast(F32), ALU.subtract).then_inc(s_xdhl, 1)
            squares_of(0, 0)
            squares_of(0, 1)
            for c in range(NC):
                soft_one(c)
            dve.wait_ge(s_ready, 1)
            dve.tensor_scalar(a_s[:, :, :], a_s[:, :, :], -1.0, None, ALU.mult).then_inc(s_ready, 1)
            squares_of(0, 2)
            squares_of(0, 3)
            run(norm_factors(0, 0))
            s2 = 2 * NC
            for c in range(NC):
                dve.wait_ge(s_soft_a, 3 * NC + c + 1)
                dve.tensor_scalar(one_p[:, c, :], one_p[:, c, :], -1.0, None, ALU.add).then_inc(s_soft_d, 1)
            for c in range(NC):
                dve.wait_ge(s_soft_d, NC + c + 1)
                dve.tensor_tensor(one_p[:, c, :], delta[:, c, :], one_p[:, c, :], ALU.subtract).then_inc(s_soft_d, 1)
            for c in range(NC):
                dve.wait_ge(s_soft_d, 2 * NC + c + 1)
                dve.tensor_tensor(du[:, c, :], du[:, c, :], one_p[:, c, :], ALU.add).then_inc(s_soft_d, 1)
            for c in range(NC):
                dve.wait_ge(s_soft_d, 3 * NC + c + 1)
                dve.tensor_tensor(delta[:, c, :], du[:, c, :], y_m[:, c, :], ALU.add).then_inc(s_soft_d, 1)
            dve.wait_ge(s_soft_d, 5 * NC)
            dve.tensor_tensor(du[:, :, :], delta[:, :, :], u_s[:, :, :], ALU.mult).then_inc(s_du, 1)
            for c in range(NC):
                last = dve.tensor_scalar(y_m[:, c, :], u_s[:, c, :], dsk_s[:, c:c + 1], None, ALU.mult)
            last.then_inc(s_bcfree, 1)
            dve.wait_ge(s_bcfree, 1)
            dve.wait_ge(s_ready, 2)
            dve.wait_ge(s_const, 1)

            def group_columns(i):
                for s in range(2):
                    dve.tensor_scalar(sel[:, s * G:(s + 1) * G], ident[:, ds(i * G + (DR + s * DS), G)], 1.0, None, ALU.mult)
                dve.tensor_scalar(a_cur[:, :, :], a_s[:, :, ds(i * G, G)], 1.0, None, ALU.mult).then_inc(s_cur, 1)

            def bx(ap):
                return bcast(ap.rearrange("p (o t) -> p o t", o=1), [P, NC, T])

            def scan_in(U, u, j):
                dve.wait_ge(s_bc, U * 4 + (j + 1))
                dve.wait_ge(s_ysum, U * 4 + (j + 1))
                dve.tensor_tensor(hb[:, j % 2], du[:, :, u * T:(u + 1) * T], bx(bc_bank[:, 0:T]), ALU.mult).then_inc(s_dbu, 1)

            def scan(U, j):
                dve.wait_ge(s_dbu, U * 4 + (j + 1))
                dve.wait_ge(s_dA, U * 4 + (j + 1))
                for c in range(NC):
                    last = dve.tensor_tensor_scan(hb[:, j % 2, c, :], dA[:, j % 2, c, :], hb[:, j % 2, c, :], 0.0,
                                                  ALU.mult, ALU.add)
                last.then_inc(s_scan, 1)

            def scan_out(U, j):
                dve.wait_ge(s_scan, U * 4 + (j + 3))
                dve.tensor_tensor(hb[:, j % 2], hb[:, j % 2], bx(bc_bank[:, T:2 * T]), ALU.mult).then_inc(s_bcfree, 1)

            def invert_z(U, h):
                dve.wait_ge(s_pv, U * 4 + (h + 1))
                z = pv_bank[:, :].rearrange("p (t c) -> p t c", t=NT)[:, :, DH:DH + 1]
                dve.reciprocal(rz[:, h % 2, :].rearrange("p (t o) -> p t o", o=1), z).then_inc(s_rz, 1)

            def norm_o(U, h):
                dve.wait_ge(s_rz, U * 4 + (h + 1))
                o = pv_bank[:, :].rearrange("p (t c) -> p t c", t=NT)[:, :, 0:DH]
                dve.tensor_tensor(o_s[:, :, h * DH:(h + 1) * DH], o,
                                  bcast(rz[:, h % 2, :].rearrange("p (t o) -> p t o", o=1), [P, NT, DH]), ALU.mult).then_inc(s_onorm, 1)

            def unit(i, u, after, after2, splits):
                U = i * B + u
                nf = norm_factors(U + 1, (u + 1) % 2) if after else iter(())

                def ahead(f):
                    if f >= 2 and after:
                        squares_of(U + 1, f)
                    if f < 2 and after2:
                        squares_of(U + 2, f)

                def weights(part, at):
                    if splits and u == B - 2:
                        dve.wait_ge(s_copied, (U + 1) * NF + at)
                        if part == Q:
                            split(i + 1, part)
                        else:
                            split_high(i + 1, part)

                scan_in(U, u, 0)
                scan(U, 0)
                if splits and u == B - 1:
                    dve.wait_ge(s_evac, U * EVACS + FIRST)
                    dve.tensor_scalar(f_cur[:, :], f_s[:, ds(i * G + G, G)], 1.0, None, ALU.mult).then_inc(s_fcur, 1)
                scan_out(U, 0)
                invert_z(U, 0)
                ahead(2)
                norm_o(U, 0)
                weights(K, 3)
                ahead(3)
                invert_z(U, 1)
                run(nf, 1)
                norm_o(U, 1)
                run(nf, 1)
                scan_in(U, u, 1)
                run(nf, 1)
                scan(U, 1)
                run(nf, 1)
                invert_z(U, 2)
                run(nf, 1)
                norm_o(U, 2)
                scan_out(U, 1)
                run(nf, 5)
                invert_z(U, 3)
                run(nf, 1)
                norm_o(U, 3)
                weights(Q, 4)
                run(nf, 1)
                scan_in(U, u, 2)
                run(nf)
                scan(U, 2)
                scan_out(U, 2)
                ahead(0)
                scan_in(U, u, 3)
                scan(U, 3)
                if splits and u == B - 1:
                    group_columns(i + 1)
                scan_out(U, 3)
                weights(V, 6)
                ahead(1)
                n_y = TURNS * u + (Y_TURN if after else 2)
                dve.wait_ge(s_turned, U * TURNS + (FIRST + (Y_TURN if after else 2) + 1))
                dve.tensor_tensor(y_acc[:, u].rearrange("p t d -> p (t d)"), y_acc[:, u].rearrange("p t d -> p (t d)"),
                                  turn[n_y % 2][:, :], ALU.add).then_inc(s_yadd, 1)

            group_columns(0)
            dve.wait_ge(s_fac, 3)
            dve.tensor_scalar(f_cur[:, :], f_s[:, 0:G], 1.0, None, ALU.mult).then_inc(s_fcur, 1)
            squares_of(1, 0)
            squares_of(1, 1)
            with dve.Fori(0, GROUPS - 1) as i:
                for u in range(B):
                    unit(i, u, True, True, True)
            for u in range(B):
                unit(GROUPS - 1, u, u < B - 1, u < B - 2, False)

            own = [0]

            def mark(ins):
                own[0] += 1
                ins.then_inc(s_own, 1)

            def seen():
                dve.wait_ge(s_own, own[0])

            def inverse_std(lo, hi):
                n = slice(lo, hi)
                at = own[0]
                steps = chain_steps(lx[:, n], ln_r[:, n], lt[:, n],
                                    lambda: dve.tensor_scalar(lx[:, n], mv[:, n, 1], LN_EPS, None, ALU.add),
                                    ln_r[:, n], s_own, at)
                run(steps)
                own[0] += CHAIN

            def layer_norm(buf, tiles):
                for n in tiles:
                    last = dve.bn_stats(bn[:, n, :], buf[:, n // NT, n % NT, :])
                mark(last)
                seen()
                for n in tiles:
                    last = dve.bn_aggr(mv[:, n, :], bn[:, n, :])
                mark(last)
                seen()
                inverse_std(tiles[0], tiles[-1] + 1)
                seen()

            def normalise(buf, n):
                t = buf[:, n // NT, n % NT, :]
                return dve.tensor_scalar(t, t, mv[:, n, 0:1], ln_r[:, n:n + 1], ALU.subtract, ALU.mult)

            tiles = list(range(B * NT))
            dve.wait_ge(s_xn, 16)
            dve.wait_ge(s_yadd, GROUPS * B + 1)
            for b in range(B):
                last = dve.tensor_tensor(y_acc[:, b], y_acc[:, b], xn[:, b], ALU.add)
            mark(last)
            seen()
            layer_norm(y_acc, tiles)
            for b in range(B):
                normalise(y_acc, 2 * b)
                normalise(y_acc, 2 * b + 1).then_inc(s_mid, 1)
            dve.wait_ge(s_ysum, GROUPS * B * 4 + 2)
            for b in range(B):
                dve.wait_ge(s_tanh, GROUPS * B * 4 + b + 1)
                mark(dve.scalar_tensor_tensor(out=tanh_s[:, b], in0=tanh_s[:, b], scalar=1.0, in1=y_acc[:, b],
                                              op0=ALU.add, op1=ALU.mult))
                seen()
                dve.scalar_tensor_tensor(out=gated[:, b], in0=y_m[:, :, b * T:(b + 1) * T], scalar=0.5, in1=tanh_s[:, b],
                                         op0=ALU.mult, op1=ALU.mult).then_inc(s_gt, 1)
            for b in range(B):
                dve.wait_ge(s_tg, b + 1)
                last = dve.tensor_tensor(xn[:, b], y_acc[:, b], bank[b % 4][:, :].rearrange("p (t d) -> p t d", t=NT), ALU.add)
            mark(last)
            seen()
            layer_norm(xn, tiles)
            for b in range(B):
                normalise(xn, 2 * b)
                normalise(xn, 2 * b + 1).then_inc(s_x2, 1)
            for b in range(B):
                at = slice(b * T, (b + 1) * T)
                dve.wait_ge(s_x2c, b + 1)
                dve.tensor_copy(xhl[:, HI, :, at], x2T[:, :, at]).then_inc(s_xhi, 1)
                dve.wait_ge(s_xhi, 3 + b)
                dve.tensor_tensor(xhl[:, LO, :, at], x2T[:, :, at], xhl[:, HI, :, at].bitcast(F32), ALU.subtract).then_inc(s_x2hl, 1)

            def split_expert(e_plus, p, times):
                dve.wait_ge(s_eraw[p], times * 16)
                dve.tensor_copy(wf_hl[:, HI, p], wf_raw[:, p]).then_inc(s_ehi, 1)
                dve.wait_ge(s_ehi, e_plus)
                dve.tensor_tensor(wf_hl[:, LO, p], wf_raw[:, p], wf_hl[:, HI, p].bitcast(F32), ALU.subtract).then_inc(s_esplit, 1)

            split_expert(1, 0, 1)
            split_expert(2, 1, 1)

            for e in range(E):
                last = dve.memset(rank[:, e:e + 1], float(E - e))
            mark(last)
            dve.wait_ge(s_logit, 1)
            NTL = B * NT

            def wide(col):
                return bcast(col[:, :].rearrange("p (n o) -> p n o", o=1), [P, NTL, E])

            rank_w = bcast(rank[:, :].rearrange("p (o e) -> p o e", o=1), [P, NTL, E])
            AX = mybir.AxisListType.X

            def do(ins):
                mark(ins)
                seen()

            do(dve.tensor_copy(gl[:, :, :], bank[7][:, 0:NTL * E].rearrange("p (n e) -> p n e", e=E)))
            do(dve.tensor_reduce(m1[:, :], gl[:, :, :], AX, ALU.max))
            do(dve.tensor_tensor(g1[:, :, :], gl[:, :, :], wide(m1), ALU.is_equal))
            do(dve.tensor_tensor(g1[:, :, :], g1[:, :, :], rank_w, ALU.mult))
            do(dve.tensor_reduce(mr[:, :], g1[:, :, :], AX, ALU.max))
            do(dve.tensor_tensor(oh1[:, :, :], g1[:, :, :], wide(mr), ALU.is_equal))
            do(dve.scalar_tensor_tensor(out=gl[:, :, :], in0=oh1[:, :, :], scalar=-3.0e38, in1=gl[:, :, :], op0=ALU.mult, op1=ALU.add))
            do(dve.tensor_reduce(m2[:, :], gl[:, :, :], AX, ALU.max))
            do(dve.tensor_tensor(g2[:, :, :], gl[:, :, :], wide(m2), ALU.is_equal))
            dve.tensor_tensor(m2[:, :], m2[:, :], m1[:, :], ALU.subtract).then_inc(s_ge, 1)
            do(dve.tensor_tensor(g2[:, :, :], g2[:, :, :], rank_w, ALU.mult))
            do(dve.tensor_reduce(mr[:, :], g2[:, :, :], AX, ALU.max))
            do(dve.tensor_tensor(g2[:, :, :], g2[:, :, :], wide(mr), ALU.is_equal))
            dve.wait_ge(s_ge, 2)
            do(dve.tensor_scalar(w2[:, :], w1[:, :], 1.0, None, ALU.add))
            do(dve.reciprocal(w2[:, :], w2[:, :]))
            do(dve.tensor_tensor(w1[:, :], w1[:, :], w2[:, :], ALU.mult))
            do(dve.tensor_tensor(g2[:, :, :], g2[:, :, :], wide(w1), ALU.mult))
            do(dve.tensor_tensor(oh1[:, :, :], oh1[:, :, :], wide(w2), ALU.mult))
            mark(dve.tensor_tensor(cwt[:, :, :], oh1[:, :, :], g2[:, :, :], ALU.add))
            seen()
            dve.memset(lt[:, 0:1], 0.0).then_inc(s_outfree, 2)

            def make_h(S, par, m):
                dve.wait_ge(s_sg, S * 2 + (m + 1))
                dve.wait_ge(s_h1, S * 2 + (m + 1))
                dve.tensor_tensor(h32[:, par, m, :], sg[:, m, :], bank[2 * m + 1][:, :], ALU.mult).then_inc(s_h, 1)

            def low(S, par, m):
                dve.wait_ge(s_hhi, S * 2 + (m + 1))
                dve.tensor_tensor(h_hl[par][:, LO, m, :], h32[:, par, m, :], h_hl[par][:, HI, m, :].bitcast(F32),
                                  ALU.subtract).then_inc(s_hlo, 1)

            def add_out(S, half, e):
                for r in range(2):
                    dve.wait_ge(s_out, S * 2 + (r + 1))
                    for t in range(2):
                        n = half * 4 + 2 * r + t
                        acc = xn[:, n // NT, n % NT, :]
                        w = cwt[:, n, ds(e, 1)]
                        last = dve.scalar_tensor_tensor(out=acc, in0=bank[4 + r][:, t * D:(t + 1) * D], scalar=w, in1=acc,
                                                        op0=ALU.mult, op1=ALU.add)
                    last.then_inc(s_outfree, 1)

            def make(S, par):
                make_h(S, par, 0)
                make_h(S, par, 1)
                low(S, par, 0)
                low(S, par, 1)

            make(0, 0)

            def experts_pair(i, last_pair):
                for q in range(4):
                    S = i * 4 + q
                    if not (last_pair and q == 3):
                        make(S + 1, (q + 1) % 2)
                    add_out(S, q % 2, i * 2 + q // 2)
                    if q % 2 == 1 and not last_pair:
                        p = q // 2
                        split_expert(i * 2 + (3 + p), p, i + 2)

            with dve.Fori(0, E // 2 - 1) as i:
                experts_pair(i, False)
            experts_pair(E // 2 - 1, True)

            for half in range(2):
                t4 = tiles[4 * half:4 * half + 4]
                if half == 0:
                    dve.wait_ge(s_outfree, 2 * 2 * E + 2)
                layer_norm(xn, t4)
                for n in t4:
                    last = normalise(xn, n)
                last.then_inc(s_fin, 1)

        @block.gpsimd
        def _(pool):
            pool.memset(ident[:, :], 0.0)
            pool.memset(causal[:, :], 1.0)
            pool.memset(v_s[:, :, :, :, DH:DH + 1], 1.0).then_inc(s_ones, 1)
            pool.wait_ge(s_ones, 1)
            pool.affine_select(out=causal[:, :], in_=causal[:, :], compare_op=ALU.is_ge, fill=0.0, base=0,
                               pattern=[[1, P]], channel_multiplier=-1)
            pool.affine_select(out=ident[:, :], in_=ident[:, :], compare_op=ALU.not_equal, fill=1.0, base=0,
                               pattern=[[-1, P]], channel_multiplier=1).then_inc(s_const, 1)
            pool.wait_ge(s_const, 1)

            def scale_q(U, par, t):
                pool.wait_ge(s_stat, U * CHAIN + CHAIN)
                q = qk[:, 2 * t + 1, :].rearrange("p (h d) -> p h d", h=G)
                f = rs[:, par, 2 * t + 1, :].rearrange("p (h o) -> p h o", o=1)
                pool.tensor_tensor(q, q, bcast(f, [P, G, DH]), ALU.mult).then_inc(s_scaled, 1)

            def mask(U, h):
                pool.wait_ge(s_exp, U * 4 + (h + 1))
                d = pT[:, h, :].rearrange("p (k t) -> p k t", k=3)[:, 0:3:2, :]
                pool.tensor_tensor(d, d, bcast(causal[:, :].rearrange("p (o t) -> p o t", o=1), [P, 2, P]),
                                   ALU.mult).then_inc(s_masked, 1)

            def sum_y(U, u, j):
                pool.wait_ge(s_bcfree, U * 4 + (j + 2))
                pool.wait_ge(s_ysum, U * 4 + (j + 2))
                y = y_m[:, :, u * T:(u + 1) * T]
                pool.tensor_tensor(y, y, hb[:, j % 2], ALU.add).then_inc(s_ysum, 1)

            scale_q(0, 0, 0)
            scale_q(0, 0, 1)
            pool.wait_ge(s_ones, 1)
            pool.memset(pool_mark[:, :], 0.0).then_inc(s_ysum, 2)

            def split_low(i, part):
                pool.wait_ge(s_whi, i * 3 + (part + 1))
                pool.tensor_tensor(wq_hl[:, LO, part], wq_raw[:, part], wq_hl[:, HI, part].bitcast(F32),
                                   ALU.subtract).then_inc(s_split[part], 1)

            def unit(i, u, more, splits):
                U = i * B + u

                mask(U, 0)
                mask(U, 1)
                sum_y(U, u, 0)
                mask(U, 2)
                mask(U, 3)
                if splits and u == B - 2:
                    split_low(i + 1, K)
                sum_y(U, u, 1)
                if more:
                    scale_q(U + 1, (u + 1) % 2, 0)
                    scale_q(U + 1, (u + 1) % 2, 1)
                sum_y(U, u, 2)
                sum_y(U, u, 3)
                if splits and u == B - 2:
                    split_low(i + 1, V)

            with pool.Fori(0, GROUPS - 1) as i:
                for u in range(B):
                    unit(i, u, True, True)
            for u in range(B):
                unit(GROUPS - 1, u, u < B - 1, False)


def kernel(**inputs):
    import concourse.bacc as _bacc
    from concourse.bass_utils import run_bass_kernel_spmd as _run

    a = {k.replace("L0_", ""): np.asarray(v) for k, v in inputs.items()}
    halves = np.concatenate([np.arange(0, DH, 2), np.arange(1, DH, 2)])

    def grouped(w, permute):
        w = w.reshape(GROUPS, G, DH, D)
        if permute:
            w = w[:, :, halves, :]
        return w.transpose(0, 3, 1, 2).reshape(GROUPS, D, GW)

    x2d = a["x"].reshape(N, D)
    arrays = {
        "xT": x2d.T,
        "x": x2d,
        "wkqv": np.stack([grouped(a["attn_wk"], True), grouped(a["attn_wq"], True), grouped(a["attn_wv"], False)], axis=1),
        "woT": a["attn_wo"].T,
        "qw": a["attn_q_norm_w"][halves],
        "kw": a["attn_k_norm_w"][halves],
        "cosT": a["attn_rope_cos"][:HEADS].T,
        "sinT": a["attn_rope_sin"][:HEADS].T,
        "ctxT": a["ctx_1024"].reshape(N, DM).T,
        "in_projT": a["xattn_in_proj_w"].T,
        "channels": np.concatenate([a["xattn_conv_b"][:, None], a["xattn_dt_proj_b"][:, None], a["xattn_D"][:, None],
                                    a["xattn_conv_w"], a["xattn_A_log"]], axis=1),
        "x_projT": a["xattn_x_proj_w"].T,
        "dt_projT": a["xattn_dt_proj_w"].T,
        "gate": a["ffn_gate_kernel"],
        "experts": np.stack([a["ffn_wi_0"], a["ffn_wi_1"], a["ffn_wo"]], axis=1).reshape(E, 3 * D, M),
    }
    nc = _bacc.Bacc("TRN2", target_bir_lowering=False, num_devices=1)
    feeds, args = {}, []
    for name, v in arrays.items():
        v = np.ascontiguousarray(v)
        feeds[f"in_{name}"] = v
        args.append(nc.dram_tensor(f"in_{name}", v.shape, mybir.dt.from_np(v.dtype), kind="ExternalInput").ap())
    out = nc.dram_tensor("out", (N, D), F32, kind="ExternalOutput").ap()
    build(nc, *args, out)
    r = _run(nc, [feeds], core_ids=[0])
    return np.asarray(r.results[0]["out"]).reshape(B, T, D)
```

```python
from contextlib import ExitStack

import numpy as np

import concourse.bass as bass
from concourse import mybir

ALU = mybir.AluOpType
ACT = mybir.ActivationFunctionType
F32 = mybir.dt.float32
F32R = mybir.dt.float32r
I32 = mybir.dt.int32
ds = bass.ds

P = 128
B, T, D = 4, 256, 256
N = B * T
NT = T // P
KD = D // P
HEADS, DH = 16, 128
G = 4
GROUPS = HEADS // G
GW = G * DH
DM, DI, DS, DC, DR = 128, 256, 16, 4, 8
NC = DI // P
E, M = 8, 256
KM = M // P
CAP = 50.0
RMS_EPS, LN_EPS = 1e-6, 1e-5
CAP_SCALE = DH ** -0.5 / CAP
MAGIC = float(0x5F3759DF)
HI, LO = 0, 1
K, Q, V = 0, 1, 2
FILLS = [(K, 0), (Q, 0), (K, 1), (Q, 1), (V, 0), (V, 1)]
NF = len(FILLS)
K_TURN, O_TURN, Q_TURN, Y_TURN, TURNS, EVACS, FIRST = 0, 2, 4, 6, 7, 6, 4
NEWTON = 3
CHAIN = 3 + 3 * NEWTON


def build(nc, xT, x, wkqv, woT, qw, kw, cosT, sinT, ctxT, in_projT, channels, x_projT,
          dt_projT, gate, experts, out):
    with ExitStack() as ctx:
        def sb(name, shape, dt=F32):
            return ctx.enter_context(nc.sbuf_tensor(name, shape, dt))

        def sem(name):
            return ctx.enter_context(nc.semaphore(name))

        bank = [ctx.enter_context(nc.psum_tensor(f"bank{i}", [P, 512], F32)) for i in range(8)]
        proj, turn, score = bank[0:2], bank[2:4], bank[4:6]
        pv_bank, bc_bank = bank[6], bank[7]

        ident = sb("ident", [P, P])
        causal = sb("causal", [P, P])
        cos_s = sb("cos_s", [P, HEADS])
        sin_s = sb("sin_s", [P, HEADS])
        norm_w = sb("norm_w", [P, 2])
        f_s = sb("f_s", [P, HEADS])
        f_cur = sb("f_cur", [P, G])
        xhl = sb("xhl", [P, 2, KD, N], F32R)
        wraw = sb("wraw", [P, 3 * KD * GW])
        whl = sb("whl", [P, 2, 3 * KD * GW], F32R)
        wo_raw = sb("wo_raw", [P, G, D])
        wo_hl = sb("wo_hl", [P, 2, G, D], F32R)
        qk = sb("qk", [P, 4, GW])
        squares = sb("squares", [P, GW])
        ss = sb("ss", [P, 4, G])
        nx = sb("nx", [P, 4, G])
        ny = sb("ny", [P, 4, G])
        nt = sb("nt", [P, 4, G])
        rs = sb("rs", [P, 2, 4, G])
        qT = sb("qT", [P, G, T])
        kT = sb("kT", [P, G, T])
        v_s = sb("v_s", [P, 2, NT, G, DH + 1])
        pT = sb("pT", [P, G, 3 * P])
        rz = sb("rz", [P, 2, NT])
        o_s = sb("o_s", [P, NT, GW])
        oT = sb("oT", [P, 2, G, T], F32R)
        y_acc = sb("y_acc", [P, B, NT, D])
        xn = sb("xn", [P, B, NT, D])
        ctx_s = sb("ctx_s", [P, N])
        in_w = sb("in_w", [P, DI])
        xp_w = sb("xp_w", [P, NC, P])
        dt_w = sb("dt_w", [P, DI])
        chan = sb("chan", [P, NC, 3 + DC + DS])
        cb_s, db_s, dsk_s = chan[:, :, 0], chan[:, :, 1], chan[:, :, 2]
        cw_s, al_s = chan[:, :, 3:3 + DC], chan[:, :, 3 + DC:3 + DC + DS]
        a_s = sb("a_s", [P, NC, DS])
        u_s = sb("u_s", [P, NC, N])
        delta = sb("delta", [P, NC, N])
        du = sb("du", [P, NC, N])
        y_m = sb("y_m", [P, NC, N])
        xd_hl = sb("xd_hl", [P, 2, N], F32R)
        sel = sb("sel", [P, 2 * G], F32R)
        a_cur = sb("a_cur", [P, NC, G])
        dA = sb("dA", [P, 2, NC, T])
        hb = sb("hb", [P, 2, NC, T])
        gate_s = sb("gate_s", [P, KD, E])
        bn = sb("bn", [P, B * NT, 6])
        mv = sb("mv", [P, B * NT, 2])
        ln_r = sb("ln_r", [P, B * NT])
        lx = sb("lx", [P, B * NT])
        lt = sb("lt", [P, B * NT])
        gl = sb("gl", [P, B * NT, E])
        rank = sb("rank", [P, E])
        g1 = sb("g1", [P, B * NT, E])
        g2 = sb("g2", [P, B * NT, E])
        oh1 = sb("oh1", [P, B * NT, E])
        cwt = sb("cwt", [P, B * NT, E])
        m1 = sb("m1", [P, B * NT])
        m2 = sb("m2", [P, B * NT])
        mr = sb("mr", [P, B * NT])
        w1 = sb("w1", [P, B * NT])
        w2 = sb("w2", [P, B * NT])
        pool_mark = sb("pool_mark", [P, 1])
        h_odd = sb("h_odd", [P, 2, KM, 512], F32R)

        xT_raw = [o_s[:, :, :].rearrange("p t n -> p (t n)"), qT[:, :, :].rearrange("p h t -> p (h t)")]
        xd_s = pT[:, :, :].rearrange("p a b -> p (a b)")[:, 0:N]
        one_p = xn[:, :, :, :].rearrange("p b t d -> p (b t d)").rearrange("p (c n) -> p c n", c=NC)
        wq_raw = wraw[:, :].rearrange("p (x k n) -> p x k n", x=3, k=KD)
        wq_hl = whl[:, :, :].rearrange("p h (x k n) -> p h x k n", x=3, k=KD)
        wf_raw = wraw[:, :].rearrange("p (s m k n) -> p s m k n", s=2, m=3, k=KD)
        wf_hl = whl[:, :, :].rearrange("p h (s m k n) -> p h s m k n", s=2, m=3, k=KD)
        x2T = u_s
        gate_in = delta
        gated = du
        sg = dA[:, :, :, :].rearrange("p s c t -> p s (c t)")
        h_hl = [xd_hl[:, :, :].rearrange("p h (m n) -> p h m n", m=KM), h_odd[:, :, :, :]]
        h32 = qk[:, :, :].rearrange("p (r m) n -> p r m n", r=2)

        s_zeroed, s_inw, s_chan, s_small, s_x, s_tab, s_wo = (sem(n) for n in (
            "zeroed", "in_proj_loaded", "channels_loaded", "small_loaded", "x_loaded", "tables_loaded", "wo_loaded"))
        s_gatew, s_wohi, s_wosplit, s_olow = sem("gate_loaded"), sem("wo_high"), sem("wo_split"), sem("o_low")
        s_ctx = [sem(f"ctx_loaded{half}") for half in range(2)]
        s_wraw = [sem(f"raw_loaded{x}") for x in range(3)]
        s_gt3, s_x2hl3 = sem("gated_last"), sem("x2_split_last")
        s_xacc = sem("residual_loaded")
        s_eraw = [sem(f"expert_loaded{p}") for p in range(2)]
        s_const, s_ones = sem("constants_made"), sem("ones_made")
        s_inproj, s_conv, s_u, s_xdbl, s_xds, s_xdhi, s_xdhl = (sem(n) for n in (
            "inproj_done", "conv_tap", "u_ready", "xdbl_done", "xdbl_copied", "xdbl_high", "xdbl_split"))
        s_dt, s_z, s_e, s_w, s_ln, s_drop, s_delta = (sem(n) for n in (
            "dt_done", "z_read", "exp_of_z", "one_plus", "ln_done", "dropped", "delta_ready"))
        s_log1p, s_du = ([sem(f"{n}{half}") for half in range(2)] for n in ("log1p_done", "du_ready"))
        s_ready, s_tap0 = sem("a_ready"), sem("conv_first_tap")
        s_xhi, s_xsplit, s_fac = sem("x_high"), sem("x_split"), sem("factors")
        s_whi, s_split = sem("w_high"), [sem(f"w_split{x}") for x in range(3)]
        s_proj, s_copied, s_squared, s_stat, s_scaled = (sem(n) for n in (
            "projected", "proj_copied", "squared", "norm_step", "q_scaled"))
        s_turned, s_evac, s_yadd, s_scores, s_tanh, s_exp, s_masked = (sem(n) for n in (
            "turned", "turn_copied", "y_added", "scored", "tanh_done", "exp_done", "masked"))
        s_pv, s_rz, s_onorm = sem("pv_done"), sem("z_inverted"), sem("o_normed")
        s_fcur, s_ystart = sem("score_factors"), sem("y_started")
        s_cur, s_bc, s_bcfree, s_dA, s_dbu, s_scan, s_ysum = (sem(n) for n in (
            "group_columns", "bc_spread", "bc_used", "dA_ready", "dbu_ready", "scanned", "y_summed"))
        s_mid, s_gate, s_gt, s_tg, s_x2, s_x2T, s_x2c, s_logit = (sem(n) for n in (
            "x1_ready", "gate_ready", "gated", "gated_turned", "x2_ready", "x2_turned", "x2_copied", "logits"))
        s_a, s_b, s_c = ([sem(f"{n}{b}") for b in range(B)] for n in ("norm1_step", "norm2_step", "norm3_step"))
        s_gd, s_ge, s_rank = sem("logit_gap"), sem("gap_exp"), sem("rank_made")
        s_route = [sem(f"router_step{half}") for half in range(2)]
        s_x2hi, s_x2hl, s_ehi, s_esplit = sem("x2_high"), sem("x2_split"), sem("expert_high"), sem("expert_split")
        s_h0, s_h1, s_sg, s_h, s_hhi, s_hlo, s_out, s_outfree = (sem(n) for n in (
            "h0_done", "h1_done", "silu_done", "h_ready", "h_high", "h_low", "out_done", "out_added"))
        s_store, s_fin = sem("stored"), sem("normed")

        block = ctx.enter_context(nc.Block())

        def bcast(ap, shape):
            return ap.broadcast_to(shape)

        @block.sync
        def _(sp):
            sp.dma_start(in_w[:, :], in_projT).then_inc(s_inw, 16)
            for half in range(2):
                at = slice(half * 512, (half + 1) * 512)
                sp.dma_start(ctx_s[:, at], ctxT[:, at]).then_inc(s_ctx[half], 16)
                if half == 0:
                    sp.dma_start(chan[:, :, :], channels.rearrange("(c p) n -> p c n", p=P)).then_inc(s_chan, 16)
            sp.wait_ge(s_zeroed, 1)
            sp.dma_start(xp_w[:, :, 0:DR + 2 * DS], x_projT.rearrange("(c p) n -> p c n", p=P)).then_inc(s_small, 16)
            sp.dma_start(dt_w[0:DR, :], dt_projT).then_inc(s_small, 16)
            for half in range(2):
                sp.dma_start(cos_s[half * 64:half * 64 + 64, :], cosT).then_inc(s_tab, 16)
                sp.dma_start(sin_s[half * 64:half * 64 + 64, :], sinT).then_inc(s_tab, 16)
            sp.dma_start(norm_w[:, 0:1], qw.rearrange("(n o) -> n o", o=1)).then_inc(s_tab, 16)
            sp.dma_start(norm_w[:, 1:2], kw.rearrange("(n o) -> n o", o=1)).then_inc(s_tab, 16)
            sp.dma_start(wo_raw[:, :, :], woT[0].rearrange("(h p) n -> p h n", p=P)).then_inc(s_wo, 16)
            sp.dma_start(gate_s[:, :, :], gate.rearrange("(k p) n -> p k n", p=P)).then_inc(s_gatew, 16)
            sp.dma_start(y_acc[:, :, :, :], x.rearrange("(b t p) d -> p b t d", p=P, t=NT)).then_inc(s_xacc, 16)
            with sp.Fori(0, GROUPS - 1) as i:
                sp.wait_ge(s_wosplit, i + 1)
                sp.dma_start(wo_raw[:, :, :], woT[ds(i + 1, 1)].rearrange("o (h p) n -> p (o h) n", p=P)).then_inc(s_wo, 16)
                for x_ in range(3):
                    sp.wait_ge(s_split[x_], i + 1)
                    src = wkqv[ds(i + 1, 1), x_].rearrange("o (k p) n -> p (o k) n", p=P)
                    sp.dma_start(wq_raw[:, x_], src).then_inc(s_wraw[x_], 16)
            for x_ in range(3):
                sp.wait_ge(s_split[x_], GROUPS)
            for e in range(2):
                sp.dma_start(wf_raw[:, e].rearrange("p m k n -> p (m k) n"),
                             experts[e].rearrange("(a p) n -> p a n", p=P)).then_inc(s_eraw[e], 16)
            with sp.Fori(0, E // 2 - 1) as i:
                for p in range(2):
                    sp.wait_ge(s_esplit, i * 2 + (p + 1))
                    src = experts[ds(i * 2 + (2 + p), 1)].rearrange("o (a p) n -> p (o a) n", p=P)
                    sp.dma_start(wf_raw[:, p].rearrange("p m k n -> p (m k) n"), src).then_inc(s_eraw[p], 16)
            for b in range(B):
                sp.wait_ge(s_fin, b + 1)
                sp.dma_start(out.rearrange("(b t p) d -> p b t d", p=P, t=NT)[:, b], xn[:, b]).then_inc(s_store, 16)
            sp.wait_ge(s_store, 16 * B)

        @block.tensor
        def _(pe):
            def three_pass(dst, pairs):
                for n, (s, m) in enumerate(pairs):
                    pe.matmul(dst, s[HI], m[HI], start=n == 0, stop=False)
                    pe.matmul(dst, s[HI], m[LO], start=False, stop=False)
                    last = pe.matmul(dst, s[LO], m[HI], start=False, stop=n == len(pairs) - 1)
                return last

            def fill(U, b, f, first_of_group=None):
                part, t = FILLS[f]
                if isinstance(U, int) and U == 0:
                    if f >= 2:
                        pe.wait_ge(s_copied, f - 1)
                else:
                    pe.wait_ge(s_copied, U * NF + (f - 1))
                if first_of_group is not None:
                    pe.wait_ge(s_split[part], first_of_group + 1)
                at = b * T + t * P
                pairs = [((xhl[:, HI, k, at:at + P], xhl[:, LO, k, at:at + P]),
                          (wq_hl[:, HI, part, k, :], wq_hl[:, LO, part, k, :])) for k in range(KD)]
                three_pass(proj[f % 2][:, :], pairs).then_inc(s_proj, 1)

            pe.wait_ge(s_inw, 16)
            for half in range(2):
                pe.wait_ge(s_ctx[half], 16)
                for c in range(NC):
                    pe.matmul(bank[2 + 2 * half + c][:, :], in_w[:, c * P:(c + 1) * P],
                              ctx_s[:, half * 512:(half + 1) * 512], start=True, stop=True).then_inc(s_inproj, 1)

            def x_dbl(half):
                pe.wait_ge(s_u, 2 * half + 2)
                pe.wait_ge(s_small, 16 * 2)
                for c in range(NC):
                    last = pe.matmul(bank[6 + half][:, :], xp_w[:, c, :], u_s[:, c, half * 512:(half + 1) * 512],
                                     start=c == 0, stop=c == NC - 1)
                last.then_inc(s_xdbl, 1)

            def dt(half):
                pe.wait_ge(s_xds, half + 1)
                for c in range(NC):
                    pe.matmul(bank[2 + 2 * half + c][:, :], dt_w[:, c * P:(c + 1) * P],
                              xd_s[:, half * 512:(half + 1) * 512], start=True, stop=True).then_inc(s_dt, 1)

            pe.wait_ge(s_xsplit, KD)
            fill(0, 0, 0, 0)
            x_dbl(0)
            x_dbl(1)
            fill(0, 0, 1, 0)
            dt(0)
            fill(0, 0, 2)
            dt(1)
            fill(0, 0, 3)
            fill(0, 0, 4, 0)
            fill(0, 0, 5)

            def turns(n, src):
                for h in range(G):
                    last = pe.transpose(turn[n % 2][:, h * P:(h + 1) * P], src[:, h * DH:(h + 1) * DH], ident[:, :])
                last.then_inc(s_turned, 1)

            def turn_k(V_, t, n):
                pe.wait_ge(s_copied, V_ * NF + (2 * t + 1))
                turns(n, qk[:, 2 * t])

            def turn_q(V_, t, n):
                pe.wait_ge(s_scaled, V_ * 2 + (t + 1))
                turns(n, qk[:, 2 * t + 1])

            def scores(U, h):
                if h == 0:
                    pe.wait_ge(s_evac, U * EVACS + FIRST)
                if h >= 2:
                    pe.wait_ge(s_tanh, U * 4 + (h - 1))
                pe.matmul(score[h % 2][:, 0:T], kT[:, h, 0:P], qT[:, h, :], start=True, stop=True)
                pe.matmul(score[h % 2][:, T:T + P], kT[:, h, P:T], qT[:, h, P:T],
                          start=True, stop=True).then_inc(s_scores, 1)

            def values(U, u, h):
                pe.wait_ge(s_masked, U * 4 + (h + 1))
                if h == 0:
                    pe.wait_ge(s_copied, U * NF + NF)
                else:
                    pe.wait_ge(s_onorm, U * 4 + h)
                W = DH + 1
                pe.matmul(pv_bank[:, 0:W], pT[:, h, 0:P], v_s[:, u % 2, 0, h, :], start=True, stop=True)
                pe.matmul(pv_bank[:, T:T + W], pT[:, h, P:2 * P], v_s[:, u % 2, 0, h, :], start=True, stop=False)
                pe.matmul(pv_bank[:, T:T + W], pT[:, h, 2 * P:3 * P], v_s[:, u % 2, 1, h, :],
                          start=False, stop=True).then_inc(s_pv, 1)

            def spread(U, i, u, j):
                if u == 0 and j == 0:
                    pe.wait_ge(s_cur, i + 1)
                pe.wait_ge(s_bcfree, U * 4 + (j + 1))
                for s in range(2):
                    one_hot = bcast(sel[:, s * G + j:s * G + j + 1], [P, P])
                    for part in (HI, LO):
                        last = pe.matmul(bc_bank[:, s * T:(s + 1) * T], one_hot, xd_hl[:, part, u * T:(u + 1) * T],
                                         start=part == HI, stop=part == LO)
                last.then_inc(s_bc, 1)

            def turn_o(U, t, n):
                if t == 0:
                    pe.wait_ge(s_onorm, U * 4 + G)
                turns(n, o_s[:, t])

            def project_out(U, i, u, n):
                pe.wait_ge(s_olow, U * NT + NT)
                if u == 0:
                    pe.wait_ge(s_wosplit, i + 1)
                for t in range(NT):
                    pairs = [((oT[:, HI, h, t * P:(t + 1) * P], oT[:, LO, h, t * P:(t + 1) * P]),
                              (wo_hl[:, HI, h, :], wo_hl[:, LO, h, :])) for h in range(G)]
                    last = three_pass(turn[n % 2][:, t * D:(t + 1) * D], pairs)
                last.then_inc(s_turned, 1)

            gate_bank, x2_bank = [score[0], score[0], score[0], pv_bank], [score[1], proj[1], bc_bank, bc_bank]
            logit_bank = [score[1], pv_bank]

            def turn_gated(b):
                pe.wait_ge(s_gt3 if b == 3 else s_gt, 1 if b == 3 else b + 1)
                for l in range(NT):
                    for c in range(NC):
                        last = pe.transpose(gate_bank[b][:, l * DI + c * P:l * DI + (c + 1) * P],
                                            gated[:, c, b * T + l * P:b * T + (l + 1) * P], ident[:, :])
                last.then_inc(s_tg, 1)

            def turn_x2(b):
                pe.wait_ge(s_x2, b + 1)
                for k in range(KD):
                    for t in range(NT):
                        last = pe.transpose(x2_bank[b][:, k * T + t * P:k * T + (t + 1) * P],
                                            xn[:, b, t, k * P:(k + 1) * P], ident[:, :])
                last.then_inc(s_x2T, 1)

            def logits(half):
                pe.wait_ge(s_gatew, 16)
                pe.wait_ge(s_x2c, 2 * half + 2)
                for n in range(4 * half, 4 * half + 4):
                    for k in range(KD):
                        last = pe.matmul(logit_bank[half][:, n * E:(n + 1) * E], x2T[:, k, n * P:(n + 1) * P],
                                         gate_s[:, k, :], start=k == 0, stop=k == KD - 1)
                last.then_inc(s_logit, 1)

            def hidden(S, e, slot, half, ms=range(KM), first=0, last=512):
                if half == 0 and 0 in ms:
                    pe.wait_ge(s_esplit, e + 1)
                for m in ms:
                    if first == 0 and not (isinstance(S, int) and S == 0):
                        pe.wait_ge(s_h, S * 2 + (m - 1))
                    for w, s_done in ((0, s_h0), (1, s_h1)):
                        pairs = [((wf_hl[:, HI, slot, w, k, m * P:(m + 1) * P], wf_hl[:, LO, slot, w, k, m * P:(m + 1) * P]),
                                  (xhl[:, HI, k, half * 512 + first:half * 512 + last],
                                   xhl[:, LO, k, half * 512 + first:half * 512 + last])) for k in range(KD)]
                        done = three_pass(bank[2 * m + w][:, first:last], pairs)
                        if last == 512:
                            done.then_inc(s_done, 1)

            def down(S, slot, par):
                pe.wait_ge(s_hlo, S * 2 + 2)
                for r in range(2):
                    pe.wait_ge(s_outfree, S * 2 + (r + 1))
                    for t in range(2):
                        at = (2 * r + t) * P
                        pairs = [((h_hl[par][:, HI, m, at:at + P], h_hl[par][:, LO, m, at:at + P]),
                                  (wf_hl[:, HI, slot, 2, m, :], wf_hl[:, LO, slot, 2, m, :])) for m in range(KM)]
                        last = three_pass(bank[4 + r][:, t * D:(t + 1) * D], pairs)
                    last.then_inc(s_out, 1)

            def unit(i, u, after, after2, ending=False):
                U = i * B + u
                first, second = (i + 1 if u == B - 1 else None), (i + 1 if u == B - 2 else None)
                n0 = TURNS * u
                evacs = U * EVACS + FIRST

                def ahead(f):
                    if f >= 2 and after:
                        fill(U + 1, (u + 1) % B, f, first if f == 4 else None)
                    if f < 2 and after2:
                        if f == 0 and u == 0:
                            pe.wait_ge(s_xsplit, 2 * KD)
                        fill(U + 2, (u + 2) % B, f, second)

                if ending and u >= 2:
                    pe.wait_ge(s_b[u - 2], 1)
                scores(U, 0)
                spread(U, i, u, 0)
                if ending and u == 3:
                    pe.wait_ge(s_x2hi, 1)
                scores(U, 1)
                ahead(2)
                scores(U, 2)
                values(U, u, 0)
                ahead(3)
                spread(U, i, u, 1)
                scores(U, 3)
                values(U, u, 1)
                ahead(4)
                values(U, u, 2)
                if after:
                    pe.wait_ge(s_evac, evacs)
                    turn_k(U + 1, 0, n0 + K_TURN)
                    pe.wait_ge(s_yadd, U + 1)
                    turn_k(U + 1, 1, n0 + K_TURN + 1)
                ahead(5)
                values(U, u, 3)
                spread(U, i, u, 2)
                ahead(0)
                if after:
                    pe.wait_ge(s_evac, evacs + (K_TURN + 1))
                    turn_o(U, 0, n0 + O_TURN)
                    pe.wait_ge(s_evac, evacs + (K_TURN + 2))
                    turn_o(U, 1, n0 + O_TURN + 1)
                else:
                    turn_o(U, 0, n0)
                    pe.wait_ge(s_yadd, U + 1)
                    turn_o(U, 1, n0 + 1)
                ahead(1)
                if after:
                    for t in range(NT):
                        pe.wait_ge(s_olow, U * NT + (t + 1))
                        turn_q(U + 1, t, n0 + Q_TURN + t)
                if not after:
                    project_out(U, i, u, n0 + 2)
                    pe.wait_ge(s_copied, U * NF + NF)
                    turn_x2(1)
                spread(U, i, u, 3)
                if ending and u >= 1:
                    pe.wait_ge(s_tanh, U * 4 + 4)
                    if u == 2:
                        turn_x2(0)
                    turn_gated(u - 1)
                if after:
                    pe.wait_ge(s_evac, evacs + (Q_TURN + 1))
                    project_out(U, i, u, n0 + Y_TURN)

            pe.wait_ge(s_z, 1)
            pe.wait_ge(s_const, 1)
            turn_k(0, 0, 0)
            turn_k(0, 1, 1)
            fill(1, 1, 0)
            for t in range(NT):
                pe.wait_ge(s_evac, t + 1)
                turn_q(0, t, t)
            fill(1, 1, 1)
            pe.wait_ge(s_xdhl, 1)
            with pe.Fori(0, GROUPS - 1) as i:
                for u in range(B):
                    unit(i, u, True, True)
            for u in range(B):
                unit(GROUPS - 1, u, u < B - 1, u < B - 2, True)

            pe.wait_ge(s_x2hl, 2)
            hidden(0, 0, 0, 0, [0])
            pe.wait_ge(s_yadd, GROUPS * B + 1)
            hidden(0, 0, 0, 0, [1])
            logits(0)
            pe.wait_ge(s_bcfree, GROUPS * B * 4 + 1)
            hidden(1, 1, 1, 0, [0])
            turn_x2(2)
            turn_gated(3)
            hidden(1, 1, 1, 0, [1])
            down(0, 0, 0)
            pe.wait_ge(s_x2hi, 3)
            pe.wait_ge(s_x2hl, B - 1)
            hidden(2, 0, 0, 1, last=T)
            turn_x2(3)
            down(1, 1, 1)
            pe.wait_ge(s_x2hl3, 1)
            hidden(2, 0, 0, 1, first=T)
            logits(1)
            down(2, 0, 0)
            hidden(3, 1, 1, 1)
            hidden(4, 2, 0, 0)
            down(3, 1, 1)

            def experts_pair(i, last_pair):
                for q in range(4):
                    S = i * 4 + q
                    if not (last_pair and q == 3):
                        nq = (q + 1) % 4
                        e = i * 2 + ((q + 1) // 2)
                        hidden(S + 1, e, nq // 2, nq % 2)
                    down(S, q // 2, q % 2)

            with pe.Fori(1, E // 2 - 1) as i:
                experts_pair(i, False)
            experts_pair(E // 2 - 1, True)

        @block.scalar
        def _(act):
            def copy_proj(U, par, f):
                part, t = FILLS[f]
                act.wait_ge(s_proj, U * NF + (f + 1))
                if part == V:
                    act.activation(v_s[:, par, t, :, 0:DH], proj[f % 2][:, :].rearrange("p (h d) -> p h d", h=G),
                                   ACT.Copy).then_inc(s_copied, 1)
                else:
                    if not (isinstance(U, int) and U == 0):
                        act.wait_ge(s_squared, U * 4 + (f - 3))
                    act.activation(qk[:, f, :], proj[f % 2][:, :], ACT.Copy).then_inc(s_copied, 1)

            for k in range(KD):
                act.dma_start(xT_raw[k], xT[k * P:(k + 1) * P, :]).then_inc(s_x, 16)
            for x_ in range(3):
                act.dma_start(wq_raw[:, x_], wkqv[0, x_].rearrange("(k p) n -> p k n", p=P)).then_inc(s_wraw[x_], 16)

            def high_x(half):
                for k in range(KD):
                    act.activation(xhl[:, HI, k, half * 512:(half + 1) * 512], xT_raw[k][:, half * 512:(half + 1) * 512],
                                   ACT.Copy).then_inc(s_xhi, 1)

            def high_w(part):
                act.wait_ge(s_wraw[part], 16)
                act.activation(wq_hl[:, HI, part], wq_raw[:, part], ACT.Copy).then_inc(s_whi, 1)

            def silu_u(half):
                for c in range(NC):
                    act.wait_ge(s_conv, half * (DC - 1) * NC + (DC - 2) * NC + c + 1)
                    act.activation(u_s[:, c, half * 512:(half + 1) * 512], y_m[:, c, half * 512:(half + 1) * 512],
                                   ACT.Silu, bias=cb_s[:, c:c + 1]).then_inc(s_u, 1)

            def copy_xdbl(half):
                act.wait_ge(s_xdbl, half + 1)
                act.activation(xd_s[:, half * 512:(half + 1) * 512], bank[6 + half][:, :], ACT.Copy).then_inc(s_xds, 1)

            def read_z(half):
                at = slice(half * 512, (half + 1) * 512)
                for c in range(NC):
                    z = bank[2 + 2 * half + c][:, :]
                    act.wait_ge(s_dt, 2 * half + c + 1)
                    act.activation(du[:, c, at], z, ACT.Abs, bias=db_s[:, c:c + 1])
                    last = act.activation(y_m[:, c, at], z, ACT.Relu, bias=db_s[:, c:c + 1])
                last.then_inc(s_z, 1)

            def exp_z(half):
                at = slice(half * 512, (half + 1) * 512)
                act.wait_ge(s_z, half + 1)
                act.activation(delta[:, :, at], du[:, :, at], ACT.Exp, scale=-1.0).then_inc(s_e, 1)

            def ln_z(half):
                at = slice(half * 512, (half + 1) * 512)
                act.wait_ge(s_w, half + 1)
                act.wait_ge(s_e, half + 1)
                act.activation(du[:, :, at], one_p[:, :, at], ACT.Ln).then_inc(s_ln, 1)

            def first_tap(half, c):
                act.wait_ge(s_inproj, 2 * half + c + 1)
                act.activation(y_m[:, c, half * 512:(half + 1) * 512], bank[2 + 2 * half + c][:, :], ACT.Copy,
                               scale=cw_s[:, c, DC - 1:DC]).then_inc(s_tap0, 1)

            act.wait_ge(s_chan, 16)
            first_tap(0, 0)
            act.wait_ge(s_x, 16 * KD)
            high_x(0)
            first_tap(0, 1)
            high_w(K)
            for c in range(NC):
                first_tap(1, c)
            high_w(Q)
            silu_u(0)
            high_x(1)
            high_w(V)
            copy_proj(0, 0, 0)
            silu_u(1)
            copy_xdbl(0)
            copy_xdbl(1)
            copy_proj(0, 0, 1)
            read_z(0)
            copy_proj(0, 0, 2)
            exp_z(0)
            act.activation(a_s[:, :, :], al_s[:, :, :], ACT.Exp).then_inc(s_ready, 1)
            copy_proj(0, 0, 3)
            read_z(1)
            copy_proj(0, 0, 4)
            exp_z(1)
            copy_proj(0, 0, 5)
            ln_z(0)
            ln_z(1)

            def turned(n, count):
                act.wait_ge(s_turned, count + 1)
                return turn[n % 2][:, :].rearrange("p (h t) -> p h t", h=G)

            def copy_turned(dst, t, n, count):
                act.activation(dst[:, :, t * P:(t + 1) * P], turned(n, count), ACT.Copy).then_inc(s_evac, 1)

            def copy_k(t, n, count):
                src = turned(n, count)
                for h in range(G):
                    last = act.activation(kT[:, h, t * P:(t + 1) * P], src[:, h, :], ACT.Copy, scale=f_cur[:, h:h + 1])
                last.then_inc(s_evac, 1)

            def softcap(U, u, h):
                act.wait_ge(s_scores, U * 4 + (h + 1))
                act.activation(pT[:, h, 0:T], score[h % 2][:, 0:T], ACT.Tanh, scale=rs[:, u % 2, 0, h:h + 1])
                act.activation(pT[:, h, T:T + P], score[h % 2][:, T:T + P], ACT.Tanh,
                               scale=rs[:, u % 2, 2, h:h + 1]).then_inc(s_tanh, 1)

            def exps(U, h):
                act.wait_ge(s_tanh, U * 4 + (h + 1))
                act.activation(pT[:, h, :], pT[:, h, :], ACT.Exp, scale=CAP).then_inc(s_exp, 1)

            def decay(U, u, j):
                if u == 2 and j == 0:
                    act.wait_ge(s_delta, 2)
                act.wait_ge(s_scan, U * 4 + (j + 1))
                for c in range(NC):
                    last = act.activation(dA[:, j % 2, c, :], delta[:, c, u * T:(u + 1) * T], ACT.Exp,
                                          scale=a_cur[:, c, j:j + 1])
                last.then_inc(s_dA, 1)

            x2_bank = [score[1], proj[1], bc_bank, bc_bank]

            def gate(b):
                act.wait_ge(s_mid, b + 1)
                act.activation(gate_in[:, :, b * T:(b + 1) * T], y_acc[:, b], ACT.Silu).then_inc(s_gate, 1)

            def copy_x2(b):
                at = slice(b * T, (b + 1) * T)
                src = x2_bank[b][:, :].rearrange("p (k t) -> p k t", k=KD)
                act.wait_ge(s_x2T, b + 1)
                act.activation(x2T[:, :, at], src, ACT.Copy).then_inc(s_x2c, 1)
                act.activation(xhl[:, HI, :, at], src, ACT.Copy).then_inc(s_x2hi, 1)

            def gap_exp(half):
                n = slice(4 * half, 4 * half + 4)
                act.wait_ge(s_gd, half + 1)
                act.activation(w1[:, n], m2[:, n], ACT.Exp).then_inc(s_ge, 1)

            def unit(i, u, after, after2, ending=False):
                U = i * B + u
                n0, count = TURNS * u, U * TURNS + FIRST

                def ahead(f):
                    if f >= 2 and after:
                        copy_proj(U + 1, (u + 1) % 2, f)
                    if f < 2 and after2:
                        copy_proj(U + 2, u % 2, f)

                softcap(U, u, 0)
                exps(U, 0)
                softcap(U, u, 1)
                exps(U, 1)
                ahead(2)
                softcap(U, u, 2)
                exps(U, 2)
                ahead(3)
                decay(U, u, 1)
                softcap(U, u, 3)
                exps(U, 3)
                ahead(4)
                if after:
                    if u == B - 1:
                        act.wait_ge(s_fcur, i + 2)
                    copy_k(0, n0 + K_TURN, count + K_TURN)
                    copy_k(1, n0 + K_TURN + 1, count + (K_TURN + 1))
                decay(U, u, 2)
                ahead(5)
                decay(U, u, 3)
                if ending and u in (1, 2):
                    gate(u - 1)
                for t in range(NT):
                    k = (O_TURN if after else 0) + t
                    copy_turned(oT[:, HI], t, n0 + k, count + k)
                ahead(0)
                if ending and u == 3:
                    gate(2)
                    copy_x2(1)
                if after:
                    for t in range(NT):
                        copy_turned(qT, t, n0 + Q_TURN + t, count + (Q_TURN + t))
                ahead(1)
                if after:
                    if u == B - 1:
                        act.wait_ge(s_cur, i + 2)
                    decay(U + 1, (u + 1) % B, 0)
                if ending and u == 2:
                    copy_x2(0)

            act.wait_ge(s_fcur, 1)
            for t in range(NT):
                copy_k(t, t, t)
            copy_proj(1, 1, 0)
            act.wait_ge(s_xsplit, 2 * KD)
            for t in range(NT):
                copy_turned(qT, t, t, NT + t)
            copy_proj(1, 1, 1)
            act.wait_ge(s_delta, 1)
            act.wait_ge(s_cur, 1)
            decay(0, 0, 0)
            with act.Fori(0, GROUPS - 1) as i:
                for u in range(B):
                    unit(i, u, True, True)
            for u in range(B):
                unit(GROUPS - 1, u, u < B - 1, u < B - 2, True)

            def silu(S, m):
                act.wait_ge(s_h0, S * 2 + (m + 1))
                act.activation(sg[:, m, :], bank[2 * m][:, :], ACT.Silu).then_inc(s_sg, 1)

            def high(S, par, m):
                act.wait_ge(s_h, S * 2 + (m + 1))
                act.activation(h_hl[par][:, HI, m, :], h32[:, par, m, :], ACT.Copy).then_inc(s_hhi, 1)

            def step(S, par):
                silu(S, 0)
                silu(S, 1)
                high(S, par, 0)
                high(S, par, 1)

            act.wait_ge(s_scan, GROUPS * B * 4 + 2)
            silu(0, 0)
            silu(0, 1)
            high(0, 0, 0)
            high(0, 0, 1)
            gate(3)
            silu(1, 0)
            copy_x2(2)
            silu(1, 1)
            gap_exp(0)
            high(1, 1, 0)
            high(1, 1, 1)
            copy_x2(3)
            step(2, 0)
            gap_exp(1)
            step(3, 1)
            with act.Fori(1, E // 2) as i:
                for q in range(4):
                    step(i * 4 + q, q % 2)

        @block.vector
        def _(dve):
            dve.memset(xp_w[:, :, :], 0.0)
            dve.memset(dt_w[:, :], 0.0).then_inc(s_zeroed, 1)
            for e in range(E):
                last = dve.memset(rank[:, e:e + 1], float(E - e))
            last.then_inc(s_rank, 1)
            dve.memset(rz[:, 0:1, :], 0.0).then_inc(s_scan, 2)
            dve.memset(rz[:, 1:2, :], 0.0).then_inc(s_yadd, 1)

            dve.wait_ge(s_chan, 16)
            for half in range(2):
                for tap in range(1, DC):
                    for c in range(NC):
                        n = 2 * half + c
                        src = bank[2 + n][:, :].rearrange("p (b t) -> p b t", b=2)[:, :, 0:T - tap]
                        acc = y_m[:, c, half * 512:(half + 1) * 512].rearrange("p (b t) -> p b t", b=2)[:, :, tap:T]
                        w = cw_s[:, c, DC - 1 - tap:DC - tap]
                        if tap == 1:
                            dve.wait_ge(s_tap0, n + 1)
                        else:
                            dve.wait_ge(s_conv, half * (DC - 1) * NC + (tap - 2) * NC + c + 1)
                        dve.scalar_tensor_tensor(out=acc, in0=src, scalar=w, in1=acc, op0=ALU.mult,
                                                 op1=ALU.add).then_inc(s_conv, 1)

            def split_high(i, part):
                dve.wait_ge(s_wraw[part], i * 16 + 16)
                dve.tensor_copy(wq_hl[:, HI, part], wq_raw[:, part]).then_inc(s_whi, 1)

            dve.wait_ge(s_tab, 96)
            dve.tensor_tensor(cos_s[:, :], cos_s[:, :], cos_s[:, :], ALU.mult)
            dve.tensor_tensor(sin_s[:, :], sin_s[:, :], sin_s[:, :], ALU.mult).then_inc(s_fac, 1)
            dve.wait_ge(s_fac, 1)
            dve.tensor_tensor(f_s[:, :], cos_s[:, :], sin_s[:, :], ALU.add).then_inc(s_fac, 1)
            dve.wait_ge(s_fac, 2)
            dve.tensor_scalar(f_s[:, :], f_s[:, :], norm_w[:, 0:1], norm_w[:, 1:2], ALU.mult, ALU.mult).then_inc(s_fac, 1)

            def squares_of(U, x_):
                dve.wait_ge(s_copied, U * NF + (x_ + 1))
                if not (isinstance(U, int) and U == 0 and x_ == 0):
                    dve.wait_ge(s_squared, U * 4 + x_)
                for h in range(G):
                    col = qk[:, x_, h * DH:(h + 1) * DH]
                    last = dve.tensor_tensor_reduce(squares[:, h * DH:(h + 1) * DH], col, col, 1.0, 0.0, ALU.mult, ALU.add, ss[:, x_, h:h + 1])
                last.then_inc(s_squared, 1)

            def chain_steps(x, y, t, first, final, s, at):
                steps = [first]
                steps.append(lambda: dve.tensor_scalar(t.bitcast(I32), x.bitcast(I32), 1, None, ALU.logical_shift_right))
                steps.append(lambda: dve.tensor_scalar(y.bitcast(I32), t.bitcast(I32), -1.0, MAGIC, ALU.mult, ALU.add))
                for k in range(NEWTON):
                    dst = final if k == NEWTON - 1 else y
                    steps.append(lambda: dve.tensor_tensor(t, y, y, ALU.mult))
                    steps.append(lambda: dve.scalar_tensor_tensor(out=t, in0=t, scalar=-0.5, in1=x, op0=ALU.mult, op1=ALU.mult))
                    steps.append(lambda dst=dst: dve.scalar_tensor_tensor(out=dst, in0=t, scalar=1.5, in1=y, op0=ALU.add, op1=ALU.mult))
                for n, make in enumerate(steps):
                    if n:
                        dve.wait_ge(s, at + n)
                    make().then_inc(s, 1)
                    yield

            def norm_factors(U, par):
                c2 = CAP_SCALE ** 2

                def first():
                    dve.wait_ge(s_squared, U * 4 + 4)
                    dve.tensor_scalar(nx[:, 1::2, :], ss[:, 1::2, :], 1.0 / DH, RMS_EPS, ALU.mult, ALU.add)
                    return dve.tensor_scalar(nx[:, 0::2, :], ss[:, 0::2, :], 1.0 / (DH * c2), RMS_EPS / c2, ALU.mult, ALU.add)
                return chain_steps(nx[:, :, :], ny[:, :, :], nt[:, :, :], first, rs[:, par], s_stat, U * CHAIN)

            def run(steps, n=CHAIN):
                for _ in range(n):
                    next(steps, None)

            def one_plus(half):
                at = slice(half * 512, (half + 1) * 512)
                dve.wait_ge(s_e, half + 1)
                dve.tensor_scalar(one_p[:, :, at], delta[:, :, at], 1.0, None, ALU.add).then_inc(s_w, 1)

            def make_delta(half):
                at = slice(half * 512, (half + 1) * 512)
                dve.wait_ge(s_ln, half + 1)
                for c in range(NC):
                    last = dve.scalar_tensor_tensor(out=one_p[:, c, at], in0=one_p[:, c, at], scalar=-1.0, in1=delta[:, c, at],
                                                    op0=ALU.add, op1=ALU.subtract)
                last.then_inc(s_drop, 1)
                yield
                if half == 0:
                    dve.wait_ge(s_drop, 1)
                    dve.tensor_tensor(du[:, :, at], du[:, :, at], one_p[:, :, at], ALU.subtract).then_inc(s_log1p[0], 1)
                    yield
                dve.wait_ge(s_log1p[half], 1)
                dve.tensor_tensor(delta[:, :, at], du[:, :, at], y_m[:, :, at], ALU.add).then_inc(s_delta, 1)
                yield
                if half == 1:
                    return
                dve.wait_ge(s_delta, 1)
                dve.tensor_tensor(du[:, :, at], delta[:, :, at], u_s[:, :, at], ALU.mult).then_inc(s_du[0], 1)
                yield

            def start_y(half):
                at = slice(half * 512, (half + 1) * 512)
                dve.wait_ge(s_delta, half + 1)
                for c in range(NC):
                    last = dve.tensor_scalar(y_m[:, c, at], u_s[:, c, at], dsk_s[:, c:c + 1], None, ALU.mult)
                last.then_inc(s_ystart, 1)

            def split_xdbl(half):
                at = slice(half * 512, (half + 1) * 512)
                dve.wait_ge(s_xds, half + 1)
                dve.tensor_copy(xd_hl[:, HI, at], xd_s[:, at]).then_inc(s_xdhi, 1)
                dve.wait_ge(s_xdhi, half + 1)
                dve.tensor_tensor(xd_hl[:, LO, at], xd_s[:, at], xd_hl[:, HI, at].bitcast(F32), ALU.subtract).then_inc(s_xdhl, 1)

            nf0 = norm_factors(0, 0)

            def low_o(U, u, t, k, evac):
                dve.wait_ge(s_evac, U * EVACS + evac)
                src = turn[(TURNS * u + k) % 2][:, :].rearrange("p (h t) -> p h t", h=G)
                at = slice(t * P, (t + 1) * P)
                dve.tensor_tensor(oT[:, LO, :, at], src, oT[:, HI, :, at].bitcast(F32), ALU.subtract).then_inc(s_olow, 1)

            def group_columns(i):
                for s in range(2):
                    dve.tensor_scalar(sel[:, s * G:(s + 1) * G], ident[:, ds(i * G + (DR + s * DS), G)], 1.0, None, ALU.mult)
                dve.tensor_scalar(a_cur[:, :, :], a_s[:, :, ds(i * G, G)], 1.0, None, ALU.mult).then_inc(s_cur, 1)

            def bx(ap):
                return bcast(ap.rearrange("p (o t) -> p o t", o=1), [P, NC, T])

            def scan_in(U, u, j):
                if u == 2 and j == 0:
                    dve.wait_ge(s_du[1], 1)
                dve.wait_ge(s_bc, U * 4 + (j + 1))
                dve.wait_ge(s_ysum, U * 4 + (j + 1))
                dve.tensor_tensor(hb[:, j % 2], du[:, :, u * T:(u + 1) * T], bx(bc_bank[:, 0:T]), ALU.mult).then_inc(s_dbu, 1)

            def scan(U, j):
                dve.wait_ge(s_dbu, U * 4 + (j + 1))
                dve.wait_ge(s_dA, U * 4 + (j + 1))
                for c in range(NC):
                    last = dve.tensor_tensor_scan(hb[:, j % 2, c, :], dA[:, j % 2, c, :], hb[:, j % 2, c, :], 0.0,
                                                  ALU.mult, ALU.add)
                last.then_inc(s_scan, 1)

            def scan_out(U, j):
                dve.wait_ge(s_scan, U * 4 + (j + 3))
                dve.tensor_tensor(hb[:, j % 2], hb[:, j % 2], bx(bc_bank[:, T:2 * T]), ALU.mult).then_inc(s_bcfree, 1)

            def invert_z(U, h):
                dve.wait_ge(s_pv, U * 4 + (h + 1))
                z = pv_bank[:, :].rearrange("p (t c) -> p t c", t=NT)[:, :, DH:DH + 1]
                dve.reciprocal(rz[:, h % 2, :].rearrange("p (t o) -> p t o", o=1), z).then_inc(s_rz, 1)

            def norm_o(U, h):
                dve.wait_ge(s_rz, U * 4 + (h + 1))
                o = pv_bank[:, :].rearrange("p (t c) -> p t c", t=NT)[:, :, 0:DH]
                dve.tensor_tensor(o_s[:, :, h * DH:(h + 1) * DH], o,
                                  bcast(rz[:, h % 2, :].rearrange("p (t o) -> p t o", o=1), [P, NT, DH]), ALU.mult).then_inc(s_onorm, 1)

            def layer_norm(buf, b, s_step, at, s_done):
                n = slice(NT * b, NT * (b + 1))
                if at:
                    dve.wait_ge(s_step, at)
                for t in range(NT):
                    last = dve.bn_stats(bn[:, NT * b + t, :], buf[:, b, t, :])
                last.then_inc(s_step, 1)
                yield
                dve.wait_ge(s_step, at + 1)
                for t in range(NT):
                    last = dve.bn_aggr(mv[:, NT * b + t, :], bn[:, NT * b + t, :])
                last.then_inc(s_step, 1)
                yield

                def first():
                    dve.wait_ge(s_step, at + 2)
                    return dve.tensor_scalar(lx[:, n], mv[:, n, 1], LN_EPS, None, ALU.add)
                yield from chain_steps(lx[:, n], ln_r[:, n], lt[:, n], first, ln_r[:, n], s_step, at + 2)
                dve.wait_ge(s_step, at + 2 + CHAIN)
                for t in range(NT):
                    m = NT * b + t
                    last = dve.tensor_scalar(buf[:, b, t, :], buf[:, b, t, :], mv[:, m, 0:1], ln_r[:, m:m + 1],
                                             ALU.subtract, ALU.mult)
                last.then_inc(s_done, 1)
                yield

            def make_x1(b):
                dve.wait_ge(s_yadd, (GROUPS - 1) * B + b + 2)
                yield from layer_norm(y_acc, b, s_a[b], 0, s_mid)

            def make_x2(b):
                src = (pv_bank if b == 3 else score[0])[:, :].rearrange("p (t d) -> p t d", t=NT)
                dve.wait_ge(s_tg, b + 1)
                dve.tensor_tensor(xn[:, b], y_acc[:, b], src, ALU.add).then_inc(s_b[b], 1)
                yield
                yield from layer_norm(xn, b, s_b[b], 1, s_x2)

            AX = mybir.AxisListType.X

            def router(half):
                n, NTL, done = slice(4 * half, 4 * half + 4), 4, s_route[half]
                a, o1, r1, r2, c = gl[:, n, :], oh1[:, n, :], g1[:, n, :], g2[:, n, :], cwt[:, n, :]
                b1, b2, br, v1, v2 = m1[:, n], m2[:, n], mr[:, n], w1[:, n], w2[:, n]
                src = (pv_bank if half else score[1])[:, 4 * half * E:(4 * half + 4) * E]
                rank_w = bcast(rank[:, :].rearrange("p (o e) -> p o e", o=1), [P, NTL, E])

                def wide(col):
                    return bcast(col.rearrange("p (n o) -> p n o", o=1), [P, NTL, E])

                dve.wait_ge(s_rank, 1)
                dve.wait_ge(s_logit, half + 1)
                steps = [
                    lambda: dve.tensor_copy(a, src.rearrange("p (n e) -> p n e", e=E)),
                    lambda: dve.tensor_reduce(b1, a, AX, ALU.max),
                    lambda: dve.tensor_tensor(r1, a, wide(b1), ALU.is_equal),
                    lambda: dve.tensor_tensor(r1, r1, rank_w, ALU.mult),
                    lambda: dve.tensor_reduce(br, r1, AX, ALU.max),
                    lambda: dve.tensor_tensor(o1, r1, wide(br), ALU.is_equal),
                    lambda: dve.scalar_tensor_tensor(out=a, in0=o1, scalar=-3.0e38, in1=a, op0=ALU.mult, op1=ALU.add),
                    lambda: dve.tensor_reduce(b2, a, AX, ALU.max),
                    lambda: dve.tensor_tensor(r2, a, wide(b2), ALU.is_equal),
                ]
                for k, make in enumerate(steps):
                    if k:
                        dve.wait_ge(done, k)
                    make().then_inc(done, 1)
                    yield
                at = len(steps)
                dve.wait_ge(done, at)
                dve.tensor_tensor(b2, b2, b1, ALU.subtract).then_inc(s_gd, 1)
                dve.tensor_tensor(r2, r2, rank_w, ALU.mult).then_inc(done, 1)
                yield
                dve.wait_ge(done, at + 1)
                dve.tensor_reduce(br, r2, AX, ALU.max).then_inc(done, 1)
                yield
                dve.wait_ge(done, at + 2)
                dve.tensor_tensor(r2, r2, wide(br), ALU.is_equal).then_inc(done, 1)
                yield
                dve.wait_ge(s_ge, half + 1)
                dve.tensor_scalar(v2, v1, 1.0, None, ALU.add).then_inc(done, 1)
                yield
                dve.wait_ge(done, at + 4)
                dve.reciprocal(v2, v2).then_inc(done, 1)
                yield
                dve.wait_ge(done, at + 5)
                dve.tensor_tensor(v1, v1, v2, ALU.mult).then_inc(done, 1)
                dve.tensor_tensor(o1, o1, wide(v2), ALU.mult).then_inc(done, 1)
                yield
                dve.wait_ge(done, at + 6)
                dve.tensor_tensor(r2, r2, wide(v1), ALU.mult).then_inc(done, 1)
                yield
                dve.wait_ge(done, at + 8)
                dve.tensor_tensor(c, o1, r2, ALU.add).then_inc(done, 1)
                yield

            ROUTED = 18

            def expert_high(p, times):
                dve.wait_ge(s_eraw[p], times * 16)
                dve.tensor_copy(wf_hl[:, HI, p], wf_raw[:, p]).then_inc(s_ehi, 1)

            def later(n, stream):
                for _ in range(n):
                    yield
                yield from stream

            def mix(*streams):
                streams = list(streams)
                while streams:
                    streams = [g for g in streams if next(g, g) is not g]

            def unit(i, u, after, after2, splits, early=(), late=(), ending=False,
                     last_x1=iter(())):
                U = i * B + u
                nf = norm_factors(U + 1, (u + 1) % 2) if after else iter(())

                def ahead(f):
                    if f >= 2 and after:
                        squares_of(U + 1, f)
                    if f < 2 and after2:
                        squares_of(U + 2, f)

                def weights(part, at):
                    if splits and u == B - 2:
                        dve.wait_ge(s_copied, (U + 1) * NF + at)
                        split_high(i + 1, part)

                def add_y():
                    n_y = Y_TURN if after else 2
                    y = y_acc[:, u].rearrange("p t d -> p (t d)")
                    dve.wait_ge(s_turned, U * TURNS + (FIRST + n_y + 1))
                    dve.tensor_tensor(y, y, turn[(TURNS * u + n_y) % 2][:, :], ALU.add).then_inc(s_yadd, 1)

                def low_os():
                    for t in range(NT):
                        k = (O_TURN if after else 0) + t
                        low_o(U, u, t, k, FIRST + k + 1)

                def beside(streams, n=1):
                    for g in streams:
                        run(g, n)

                scan_in(U, u, 0)
                beside(early)
                scan(U, 0)
                beside(early)
                if splits and u == B - 1:
                    dve.wait_ge(s_evac, U * EVACS + FIRST)
                    dve.tensor_scalar(f_cur[:, :], f_s[:, ds(i * G + G, G)], 1.0, None, ALU.mult).then_inc(s_fcur, 1)
                scan_out(U, 0)
                if u == 0:
                    dve.wait_ge(s_wo, i * 16 + 16)
                    dve.tensor_copy(wo_hl[:, HI], wo_raw[:, :, :]).then_inc(s_wohi, 1)
                beside(early)
                invert_z(U, 0)
                ahead(2)
                beside(early)
                norm_o(U, 0)
                if not after:
                    dve.wait_ge(s_copied, U * NF + NF)
                    expert_high(0, 1)
                beside(early)
                weights(K, 3)
                ahead(3)
                invert_z(U, 1)
                run(nf, 1)
                beside(early)
                norm_o(U, 1)
                weights(Q, 4)
                run(nf, 1)
                beside(early)
                scan_in(U, u, 1)
                run(nf, 1)
                beside(early)
                scan(U, 1)
                run(nf, 1)
                beside(early)
                invert_z(U, 2)
                run(nf, 1)
                beside(early)
                norm_o(U, 2)
                beside(early)
                scan_out(U, 1)
                for n in range(5):
                    run(nf, 1)
                    if n < 2:
                        beside(early)
                invert_z(U, 3)
                run(nf, 1)
                beside(early)
                norm_o(U, 3)
                if not after:
                    beside(early)
                    beside(early)
                    low_os()
                    expert_high(1, 1)
                if ending:
                    mix(nf, *early)
                run(nf, 1)
                scan_in(U, u, 2)
                run(nf)
                scan(U, 2)
                if after:
                    low_os()
                scan_out(U, 2)
                ahead(0)
                if not after:
                    add_y()
                    beside([last_x1], 1)
                scan_in(U, u, 3)
                beside([last_x1], 2)
                scan(U, 3)
                beside([last_x1], 1)
                if splits and u == B - 1:
                    group_columns(i + 1)
                scan_out(U, 3)
                beside([last_x1], 1)
                weights(V, 6)
                ahead(1)
                beside(late, 3)
                if after:
                    add_y()

            dve.wait_ge(s_fac, 3)
            dve.tensor_scalar(f_cur[:, :], f_s[:, 0:G], 1.0, None, ALU.mult).then_inc(s_fcur, 1)
            d0, d1 = make_delta(0), make_delta(1)
            squares_of(0, 0)
            split_xdbl(0)
            split_xdbl(1)
            dve.memset(rz[:, :, :], 0.0).then_inc(s_bcfree, 1)
            squares_of(0, 1)
            squares_of(0, 2)
            one_plus(0)
            dve.wait_ge(s_ready, 1)
            dve.tensor_scalar(a_s[:, :, :], a_s[:, :, :], -1.0, None, ALU.mult).then_inc(s_ready, 1)
            squares_of(0, 3)
            run(nf0, 7)
            one_plus(1)
            run(nf0, 1)
            dve.wait_ge(s_ready, 2)
            dve.wait_ge(s_const, 1)
            group_columns(0)
            run(nf0, 2)
            run(d0, 1)
            run(nf0)
            run(d1, 1)
            run(d0, 1)
            squares_of(1, 0)
            run(d0, 1)
            start_y(0)
            run(d0, 1)
            run(d1, 1)
            start_y(1)
            squares_of(1, 1)
            dve.wait_ge(s_du[0], 1)
            dve.wait_ge(s_xacc, 16)
            with dve.Fori(0, GROUPS - 1) as i:
                for u in range(B):
                    unit(i, u, True, True, True)
            x1, x2 = [make_x1(b) for b in range(B)], [make_x2(b) for b in range(B)]
            for u in range(B):
                unit(GROUPS - 1, u, u < B - 1, u < B - 2, False,
                     early=([x2[u - 2]] if u >= 2 else []) + ([x1[u - 1]] if u >= 1 else []),
                     late=[x2[u - 1]] if u >= 1 else [], ending=True,
                     last_x1=x1[3] if u == 3 else iter(()))

            def make_h(S, par, m):
                dve.wait_ge(s_sg, S * 2 + (m + 1))
                dve.wait_ge(s_h1, S * 2 + (m + 1))
                dve.tensor_tensor(h32[:, par, m, :], sg[:, m, :], bank[2 * m + 1][:, :], ALU.mult).then_inc(s_h, 1)

            def low(S, par, m):
                dve.wait_ge(s_hhi, S * 2 + (m + 1))
                dve.tensor_tensor(h_hl[par][:, LO, m, :], h32[:, par, m, :], h_hl[par][:, HI, m, :].bitcast(F32),
                                  ALU.subtract).then_inc(s_hlo, 1)

            def add_row(S, half, e, r):
                dve.wait_ge(s_out, S * 2 + (r + 1))
                for t in range(2):
                    n = half * 4 + 2 * r + t
                    acc = xn[:, n // NT, n % NT, :]
                    w = cwt[:, n, ds(e, 1)]
                    last = dve.scalar_tensor_tensor(out=acc, in0=bank[4 + r][:, t * D:(t + 1) * D], scalar=w, in1=acc,
                                                    op0=ALU.mult, op1=ALU.add)
                last.then_inc(s_outfree, 1)

            def add_out(S, half, e):
                for r in range(2):
                    add_row(S, half, e, r)

            def make(S, par):
                make_h(S, par, 0)
                make_h(S, par, 1)
                low(S, par, 0)
                low(S, par, 1)

            def make_steps(S, par):
                for m in range(KM):
                    make_h(S, par, m)
                    yield
                for m in range(KM):
                    low(S, par, m)
                    yield

            r0, r1 = router(0), router(1)
            mix(x1[3], x2[2], later(5, make_steps(0, 0)))
            at = slice(3 * T, N)
            dve.wait_ge(s_gate, B)
            dve.wait_ge(s_ysum, GROUPS * B * 4 + 2)
            dve.tensor_tensor(gated[:, :, at], y_m[:, :, at], gate_in[:, :, at], ALU.mult).then_inc(s_gt3, 1)
            run(r0, 1)
            dve.wait_ge(s_route[0], 1)
            dve.memset(rz[:, :, :], 0.0).then_inc(s_outfree, 2)
            run(r0, 6)
            mix(x2[3], r0, later(2, make_steps(1, 1)))
            dve.wait_ge(s_route[0], ROUTED)
            add_out(0, 0, 0)
            dve.wait_ge(s_x2hi, B)
            dve.tensor_tensor(xhl[:, LO, :, at], x2T[:, :, at], xhl[:, HI, :, at].bitcast(F32), ALU.subtract).then_inc(s_x2hl3, 1)
            add_out(1, 0, 1)
            make(2, 0)
            mix(r1)
            dve.wait_ge(s_route[1], ROUTED)
            dve.wait_ge(s_out, 6)
            expert_high(0, 2)
            add_out(2, 1, 0)
            make(3, 1)
            make(4, 0)
            add_out(3, 1, 1)
            expert_high(1, 2)

            def experts_pair(i, last_pair):
                for q in range(4):
                    S = i * 4 + q
                    if not (last_pair and q == 3):
                        make(S + 1, (q + 1) % 2)
                        add_out(S, q % 2, i * 2 + q // 2)
                    if q % 2 == 1 and not last_pair:
                        expert_high(q // 2, i + 2)

            with dve.Fori(1, E // 2 - 1) as i:
                experts_pair(i, False)
            experts_pair(E // 2 - 1, True)

            def last_out(r):
                add_row(2 * E - 1, 1, E - 1, r)
                yield
                dve.wait_ge(s_outfree, 2 * (2 * E - 1) + 2 + (r + 1))
                yield from layer_norm(xn, 2 + r, s_c[2 + r], 0, s_fin)

            dve.wait_ge(s_outfree, 2 * (2 * E - 1) + 2)
            x3 = [layer_norm(xn, b, s_c[b], 0, s_fin) for b in range(2)]
            for _ in range(3):
                run(x3[0], 1)
                run(x3[1], 1)
            mix(*x3, last_out(0), last_out(1))

        @block.gpsimd
        def _(pool):
            pool.memset(ident[:, :], 0.0)
            pool.memset(causal[:, :], 1.0)
            pool.memset(v_s[:, :, :, :, DH:DH + 1], 1.0).then_inc(s_ones, 1)
            pool.wait_ge(s_ones, 1)
            pool.affine_select(out=causal[:, :], in_=causal[:, :], compare_op=ALU.is_ge, fill=0.0, base=0,
                               pattern=[[1, P]], channel_multiplier=-1)
            pool.affine_select(out=ident[:, :], in_=ident[:, :], compare_op=ALU.not_equal, fill=1.0, base=0,
                               pattern=[[-1, P]], channel_multiplier=1).then_inc(s_const, 1)
            pool.wait_ge(s_const, 1)

            def scale_q(U, par, t):
                pool.wait_ge(s_stat, U * CHAIN + CHAIN)
                q = qk[:, 2 * t + 1, :].rearrange("p (h d) -> p h d", h=G)
                f = rs[:, par, 2 * t + 1, :].rearrange("p (h o) -> p h o", o=1)
                pool.tensor_tensor(q, q, bcast(f, [P, G, DH]), ALU.mult).then_inc(s_scaled, 1)

            def mask(U, h):
                pool.wait_ge(s_exp, U * 4 + (h + 1))
                d = pT[:, h, :].rearrange("p (k t) -> p k t", k=3)[:, 0:3:2, :]
                pool.tensor_tensor(d, d, bcast(causal[:, :].rearrange("p (o t) -> p o t", o=1), [P, 2, P]),
                                   ALU.mult).then_inc(s_masked, 1)

            def sum_y(U, u, j):
                pool.wait_ge(s_bcfree, U * 4 + (j + 2))
                pool.wait_ge(s_ysum, U * 4 + (j + 2))
                if u % 2 == 0 and j == 0:
                    pool.wait_ge(s_ystart, u // 2 + 1)
                y = y_m[:, :, u * T:(u + 1) * T]
                pool.tensor_tensor(y, y, hb[:, j % 2], ALU.add).then_inc(s_ysum, 1)

            def split_low(i, part):
                pool.wait_ge(s_whi, i * 3 + (part + 1))
                pool.tensor_tensor(wq_hl[:, LO, part], wq_raw[:, part], wq_hl[:, HI, part].bitcast(F32),
                                   ALU.subtract).then_inc(s_split[part], 1)

            def low_x(half):
                for k in range(KD):
                    at = slice(half * 512, (half + 1) * 512)
                    pool.wait_ge(s_xhi, KD * half + k + 1)
                    pool.tensor_tensor(xhl[:, LO, k, at], xT_raw[k][:, at], xhl[:, HI, k, at].bitcast(F32),
                                       ALU.subtract).then_inc(s_xsplit, 1)

            low_x(0)
            split_low(0, K)
            split_low(0, Q)
            split_low(0, V)
            low_x(1)
            scale_q(0, 0, 0)
            scale_q(0, 0, 1)
            at = slice(512, N)
            pool.wait_ge(s_drop, 2)
            pool.tensor_tensor(du[:, :, at], du[:, :, at], one_p[:, :, at], ALU.subtract).then_inc(s_log1p[1], 1)
            pool.memset(pool_mark[:, :], 0.0).then_inc(s_ysum, 2)
            pool.wait_ge(s_delta, 2)
            pool.tensor_tensor(du[:, :, at], delta[:, :, at], u_s[:, :, at], ALU.mult).then_inc(s_du[1], 1)

            def gate_y(b):
                at = slice(b * T, (b + 1) * T)
                pool.wait_ge(s_gate, b + 1)
                pool.wait_ge(s_ysum, ((GROUPS - 1) * B + b) * 4 + 6)
                pool.tensor_tensor(gated[:, :, at], y_m[:, :, at], gate_in[:, :, at], ALU.mult).then_inc(s_gt, 1)

            def low_x2(b):
                at = slice(b * T, (b + 1) * T)
                pool.wait_ge(s_x2hi, b + 1)
                pool.wait_ge(s_x2c, b + 1)
                pool.tensor_tensor(xhl[:, LO, :, at], x2T[:, :, at], xhl[:, HI, :, at].bitcast(F32), ALU.subtract).then_inc(s_x2hl, 1)

            def low_expert(e, p):
                pool.wait_ge(s_ehi, e + 1)
                pool.tensor_tensor(wf_hl[:, LO, p], wf_raw[:, p], wf_hl[:, HI, p].bitcast(F32), ALU.subtract).then_inc(s_esplit, 1)

            def unit(i, u, more, splits, ending=False):
                U = i * B + u
                mask(U, 0)
                mask(U, 1)
                if splits and u == B - 1:
                    split_low(i + 1, V)
                sum_y(U, u, 0)
                mask(U, 2)
                if splits and u == B - 2:
                    split_low(i + 1, K)
                mask(U, 3)
                if u == 0:
                    pool.wait_ge(s_wohi, i + 1)
                    pool.tensor_tensor(wo_hl[:, LO], wo_raw[:, :, :], wo_hl[:, HI].bitcast(F32),
                                       ALU.subtract).then_inc(s_wosplit, 1)
                if splits and u == B - 2:
                    split_low(i + 1, Q)
                sum_y(U, u, 1)
                if ending and u == 3:
                    low_x2(0)
                    low_expert(0, 0)
                if more:
                    scale_q(U + 1, (u + 1) % 2, 0)
                    scale_q(U + 1, (u + 1) % 2, 1)
                if ending and u == 3:
                    gate_y(2)
                sum_y(U, u, 2)
                if ending and u in (1, 2):
                    gate_y(u - 1)
                if ending and u == 3:
                    low_x2(1)
                sum_y(U, u, 3)

            with pool.Fori(0, GROUPS - 1) as i:
                for u in range(B):
                    unit(i, u, True, True)
            for u in range(B):
                unit(GROUPS - 1, u, u < B - 1, False, True)
            low_expert(1, 1)
            low_x2(2)
            with pool.Fori(1, E // 2) as i:
                for p in range(2):
                    low_expert(i * 2 + p, p)


def kernel(**inputs):
    import concourse.bacc as _bacc
    from concourse.bass_utils import run_bass_kernel_spmd as _run

    a = {k.replace("L0_", ""): np.asarray(v) for k, v in inputs.items()}
    halves = np.concatenate([np.arange(0, DH, 2), np.arange(1, DH, 2)])

    def grouped(w, permute):
        w = w.reshape(GROUPS, G, DH, D)
        if permute:
            w = w[:, :, halves, :]
        return w.transpose(0, 3, 1, 2).reshape(GROUPS, D, GW)

    x2d = a["x"].reshape(N, D)
    arrays = {
        "xT": x2d.T,
        "x": x2d,
        "wkqv": np.stack([grouped(a["attn_wk"], True), grouped(a["attn_wq"], True), grouped(a["attn_wv"], False)], axis=1),
        "woT": a["attn_wo"].T.reshape(GROUPS, GW, D),
        "qw": a["attn_q_norm_w"][halves],
        "kw": a["attn_k_norm_w"][halves],
        "cosT": a["attn_rope_cos"][:HEADS].T,
        "sinT": a["attn_rope_sin"][:HEADS].T,
        "ctxT": a["ctx_1024"].reshape(N, DM).T,
        "in_projT": a["xattn_in_proj_w"].T,
        "channels": np.concatenate([a["xattn_conv_b"][:, None], a["xattn_dt_proj_b"][:, None], a["xattn_D"][:, None],
                                    a["xattn_conv_w"], a["xattn_A_log"]], axis=1),
        "x_projT": a["xattn_x_proj_w"].T,
        "dt_projT": a["xattn_dt_proj_w"].T,
        "gate": a["ffn_gate_kernel"],
        "experts": np.stack([a["ffn_wi_0"], a["ffn_wi_1"], a["ffn_wo"]], axis=1).reshape(E, 3 * D, M),
    }
    nc = _bacc.Bacc("TRN2", target_bir_lowering=False, num_devices=1)
    feeds, args = {}, []
    for name, v in arrays.items():
        v = np.ascontiguousarray(v)
        feeds[f"in_{name}"] = v
        args.append(nc.dram_tensor(f"in_{name}", v.shape, mybir.dt.from_np(v.dtype), kind="ExternalInput").ap())
    out = nc.dram_tensor("out", (N, D), F32, kind="ExternalOutput").ap()
    build(nc, *args, out)
    r = _run(nc, [feeds], core_ids=[0])
    return np.asarray(r.results[0]["out"]).reshape(B, T, D)
```
